# Optimizing a Trainium2 kernel written in Bass

```python
import numpy as np
import jax
import jax.numpy as jnp

def _softmax(x, axis=-1):
    return jax.nn.softmax(x, axis=axis)

def _gelu(x):
    return jax.nn.gelu(x, approximate=True)

def _silu(x):
    return jax.nn.silu(x)

def _sigmoid(x):
    return jax.nn.sigmoid(x)

def _layernorm(x, axis=-1, eps=1e-05):
    m = jnp.mean(x, axis=axis, keepdims=True)
    v = jnp.var(x, axis=axis, keepdims=True)
    return (x - m) / jnp.sqrt(v + eps)

def _scatter_add(tgt, idx, src, axis=0):
    return tgt.at[idx].add(src)

def _segment_sum(src, seg, n):
    return jax.ops.segment_sum(src, seg, n)
kernel_name = 'mk_recurrent_d1_jaxref_r4_f7f2bd'

def setup_inputs(seed: int=0):
    np.random.seed(seed)
    _w = jnp.asarray

    def _L0_attn_setup():
        import jax, jax.numpy as jnp
        import numpy as np
        B, S, HMODEL = (2, 1024, 512)
        NH, HD, K = (16, 128, 4)
        RMS_EPS = 1e-05
        L2_EPS = 1e-06

        def causal_conv_silu(x, w):
            Kw = w.shape[1]
            xp = jnp.pad(x, ((0, 0), (Kw - 1, 0), (0, 0)))
            out = sum((w[:, i] * xp[:, i:i + x.shape[1], :] for i in range(Kw)))
            return jax.nn.silu(out)

        def l2norm(x):
            return x * jax.lax.rsqrt(jnp.sum(x * x, axis=-1, keepdims=True) + L2_EPS)
        key = jax.random.key(seed)
        ks = jax.random.split(key, 10)

        def p(k, shape, std=0.02):
            return jax.random.normal(k, shape, jnp.float32) * std
        return {'x': jax.random.normal(ks[0], (B, S, HMODEL), jnp.float32), 'Wq': p(ks[1], (NH * HD, HMODEL)), 'Wk': p(ks[2], (NH * HD, HMODEL)), 'Wv': p(ks[3], (NH * HD, HMODEL)), 'Wb': p(ks[4], (NH, HMODEL)), 'Wo': p(ks[5], (HMODEL, NH * HD)), 'conv_q': p(ks[6], (NH * HD, K), 0.3), 'conv_k': p(ks[7], (NH * HD, K), 0.3), 'conv_v': p(ks[8], (NH * HD, K), 0.3), 'rms_w': jnp.ones((HD,), jnp.float32)}
    _L0_attn_in = _L0_attn_setup()

    def _L0_ffn_setup():
        import jax, jax.numpy as jnp
        import numpy as np
        DIM_IN = 512
        DIM_HIDDEN = 2048
        key = jax.random.key(seed)
        k_x, k_g, k_u, k_d = jax.random.split(key, 4)
        s_in = 1.0 / np.sqrt(DIM_IN)
        s_hid = 1.0 / np.sqrt(DIM_HIDDEN)
        x = jax.random.normal(k_x, (4, 512, DIM_IN), dtype=jnp.float32)
        w_gate = jax.random.uniform(k_g, (DIM_HIDDEN, DIM_IN), jnp.float32, -s_in, s_in)
        w_up = jax.random.uniform(k_u, (DIM_HIDDEN, DIM_IN), jnp.float32, -s_in, s_in)
        w_down = jax.random.uniform(k_d, (DIM_IN, DIM_HIDDEN), jnp.float32, -s_hid, s_hid)
        return {'x': x, 'w_gate': w_gate, 'w_up': w_up, 'w_down': w_down}
    _L0_ffn_in = _L0_ffn_setup()
    _d = {'L0_attn_x': _L0_attn_in['x'], 'L0_attn_Wq': _L0_attn_in['Wq'], 'L0_attn_Wk': _L0_attn_in['Wk'], 'L0_attn_Wv': _L0_attn_in['Wv'], 'L0_attn_Wb': _L0_attn_in['Wb'], 'L0_attn_Wo': _L0_attn_in['Wo'], 'L0_attn_conv_q': _L0_attn_in['conv_q'], 'L0_attn_conv_k': _L0_attn_in['conv_k'], 'L0_attn_conv_v': _L0_attn_in['conv_v'], 'L0_attn_rms_w': _L0_attn_in['rms_w'], 'L0_ffn_w_gate': _L0_ffn_in['w_gate'], 'L0_ffn_w_up': _L0_ffn_in['w_up'], 'L0_ffn_w_down': _L0_ffn_in['w_down']}
    _x0 = _d['L0_attn_x']
    _d['L0_attn_x'] = jax.random.normal(jax.random.fold_in(jax.random.key(seed), 1), (2, 1024, 512), dtype=_x0.dtype)
    del _x0
    return _d

def reference(L0_attn_x, L0_attn_Wq, L0_attn_Wk, L0_attn_Wv, L0_attn_Wb, L0_attn_Wo, L0_attn_conv_q, L0_attn_conv_k, L0_attn_conv_v, L0_attn_rms_w, L0_ffn_w_gate, L0_ffn_w_up, L0_ffn_w_down):

    def _L0_attn_ref(x, Wq, Wk, Wv, Wb, Wo, conv_q, conv_k, conv_v, rms_w):
        import jax, jax.numpy as jnp
        import numpy as np
        B, S, HMODEL = (2, 1024, 512)
        NH, HD, K = (16, 128, 4)
        RMS_EPS = 1e-05
        L2_EPS = 1e-06

        def causal_conv_silu(x, w):
            Kw = w.shape[1]
            xp = jnp.pad(x, ((0, 0), (Kw - 1, 0), (0, 0)))
            out = sum((w[:, i] * xp[:, i:i + x.shape[1], :] for i in range(Kw)))
            return jax.nn.silu(out)

        def l2norm(x):
            return x * jax.lax.rsqrt(jnp.sum(x * x, axis=-1, keepdims=True) + L2_EPS)
        b, s, _ = x.shape
        nh = Wb.shape[0]
        hd = Wq.shape[0] // nh
        q = causal_conv_silu(x @ Wq.T, conv_q)
        k = causal_conv_silu(x @ Wk.T, conv_k)
        v = causal_conv_silu(x @ Wv.T, conv_v)
        q = q.reshape(b, s, nh, hd)
        k = k.reshape(b, s, nh, hd)
        v = v.reshape(b, s, nh, hd)
        beta = jax.nn.sigmoid(x @ Wb.T)
        q = l2norm(q) * hd ** (-0.5)
        k = l2norm(k)
        qT = jnp.moveaxis(q, 1, 0)
        kT = jnp.moveaxis(k, 1, 0)
        vT = jnp.moveaxis(v, 1, 0)
        bT = jnp.moveaxis(beta, 1, 0)

        def step(state, inp):
            qt, kt, vt, bt = inp
            pred = jnp.einsum('bhd,bhdv->bhv', kt, state)
            delta = bt[..., None] * (vt - pred)
            state = state + jnp.einsum('bhd,bhv->bhdv', kt, delta)
            ot = jnp.einsum('bhd,bhdv->bhv', qt, state)
            return (state, ot)
        s0 = jnp.zeros((b, nh, hd, hd), x.dtype)
        _, o = jax.lax.scan(step, s0, (qT, kT, vT, bT))
        o = jnp.moveaxis(o, 0, 1)
        o = o * jax.lax.rsqrt(jnp.mean(o * o, axis=-1, keepdims=True) + RMS_EPS) * rms_w
        o = o.reshape(b, s, nh * hd) @ Wo.T
        return o

    def _L0_ffn_ref(x, w_gate, w_up, w_down):
        import jax, jax.numpy as jnp
        import numpy as np
        DIM_IN = 512
        DIM_HIDDEN = 2048
        gate = jnp.einsum('bsd,hd->bsh', x, w_gate)
        up = jnp.einsum('bsd,hd->bsh', x, w_up)
        gated = jax.nn.silu(gate) * up
        return jnp.einsum('bsh,dh->bsd', gated, w_down)
    x = L0_attn_x
    xn = _layernorm(x, axis=-1)
    s = _L0_attn_ref(xn, L0_attn_Wq, L0_attn_Wk, L0_attn_Wv, L0_attn_Wb, L0_attn_Wo, L0_attn_conv_q, L0_attn_conv_k, L0_attn_conv_v, L0_attn_rms_w)
    g = _silu(_L0_ffn_ref(xn, L0_ffn_w_gate, L0_ffn_w_up, L0_ffn_w_down))
    x = x + s * g
    return x

_drawn_inputs = setup_inputs


def setup_inputs(seed=0):
    import zlib

    import numpy as np

    out = dict(_drawn_inputs(seed))
    spreads = {'L0_attn_rms_w': (1.0, 0.6)}
    factors = {'L0_attn_Wb': 4.337}
    for name, (base, spread) in spreads.items():
        noise = np.random.default_rng([zlib.crc32(name.encode()), seed]).standard_normal(out[name].shape)
        drawn = base * np.exp(spread * noise) if base else spread * noise
        out[name] = jnp.asarray(drawn.astype(out[name].dtype))
    for name, factor in factors.items():
        out[name] = (out[name] * factor).astype(out[name].dtype)
    return out
```

```python
from contextlib import ExitStack

import concourse.bass as bass
from concourse import mybir

F32 = mybir.dt.float32
F32R = mybir.dt.float32r
ALU = mybir.AluOpType
ACT = mybir.ActivationFunctionType
AX_X = mybir.AxisListType.X

P = 128
B, S, DM = 2, 1024, 512
NH, HD, KW = 16, 128, 4
DH = 2048
KT = DM // P
HG = 4
NG = NH // HG
BLK = 2 * P
NBLK = B * S // BLK
SPG = S // BLK
STEPS = NG * B * SPG
GROUPS = STEPS // SPG
PAIRS = 3 * HG // 2
WPAIR = 2 * (KT * P + KW)
HOPS = 15
LEVELS = [2, 4, 8, 16, 32]
AHEAD, DMA_AHEAD = 1, 16
LN_EPS, RMS_EPS, L2_EPS = 1e-5, 1e-5, 1e-6


def causal_masks(nc, eng, done, ident, upper, upper_diag, below1, above1, level_masks):
    n = 0

    def keep(t, op, base, pattern, mult, fill=0.0):
        nonlocal n
        eng.wait_ge(done, n)
        eng.affine_select(out=t, in_=t, compare_op=op, fill=fill, base=base, pattern=pattern,
                          channel_multiplier=mult).then_inc(done, 1)
        n += 1

    ones = [upper, upper_diag, *level_masks.values()]
    for t in ones:
        eng.memset(t[:], 1.0).then_inc(done, 1)
        n += 1
    for t in (ident, below1, above1):
        eng.memset(t[:], 0.0).then_inc(done, 1)
        n += 1
    keep(ident[:], ALU.not_equal, 0, [[-1, P]], 1, 1.0)
    keep(upper[:], ALU.is_gt, 0, [[1, P]], -1)
    keep(upper_diag[:], ALU.is_ge, 0, [[1, P]], -1)
    keep(below1[:], ALU.not_equal, -1, [[-2, P // 2]], 1, 1.0)
    keep(above1[:], ALU.not_equal, 0, [[-2, P // 2]], 1, 1.0)
    for m, t in level_masks.items():
        v = t[:].rearrange("p (b j) -> p b j", j=m)
        keep(v, ALU.is_ge, -m, [[-2 * m, P // (2 * m)], [0, m]], 1)
        keep(v, ALU.is_ge, 2 * m - 1, [[2 * m, P // (2 * m)], [0, m]], -1)
    return n


def phase_normalise(nc, ctx, x, wb, xT, const, sqrt_beta):
    with ExitStack() as own:
        sb = lambda name, shape, dt=F32: own.enter_context(nc.sbuf_tensor(name, shape, dt))
        sem = lambda name: ctx.enter_context(nc.semaphore(name))
        xt = [sb(f"n_x{u}", [P, DM]) for u in range(2)]
        xn = [sb(f"n_xn{u}", [P, DM]) for u in range(2)]
        stats = [sb(f"n_stats{u}", [P, 6]) for u in range(2)]
        mv = [sb(f"n_mv{u}", [P, 2]) for u in range(2)]
        veps = [sb(f"n_veps{u}", [P, 1]) for u in range(2)]
        rstd = [sb(f"n_rstd{u}", [P, 1]) for u in range(2)]
        hi = [sb(f"n_hi{u}", [P, KT, P], F32R) for u in range(2)]
        lo = [sb(f"n_lo{u}", [P, KT, P], F32R) for u in range(2)]
        beta = [sb(f"n_beta{u}", [P, NH]) for u in range(2)]
        wb_in = sb("n_wb", [P, KT * NH])
        wb_hi = sb("n_wbhi", [P, KT, NH], F32R)
        wb_lo = sb("n_wblo", [P, KT, NH], F32R)
        power = sb("n_power", [P, NH + 1])
        ps_t = [own.enter_context(nc.psum_tensor(f"n_pst{u}", [P, KT, P], F32)) for u in range(2)]
        ps_b = [own.enter_context(nc.psum_tensor(f"n_psb{u}", [P, 512], F32)) for u in range(2)]
        masks_done, powers = sem("n_masks"), sem("n_powers")
        wb_loaded, wb_split = sem("n_wb_loaded"), sem("n_wb_split")
        loaded = [sem(f"n_loaded{u}") for u in range(2)]
        stat_steps, rstd_ready, xn_ready = sem("n_stat_steps"), sem("n_rstd_ready"), sem("n_xn_ready")
        transposed, hi_ready, lo_ready = sem("n_transposed"), sem("n_hi_ready"), sem("n_lo_ready")
        logits, beta_ready, root_ready = sem("n_logits"), sem("n_beta_ready"), sem("n_root_ready")
        stored = [sem(f"n_stored{u}") for u in range(2)]
        block = own.enter_context(nc.Block())

        @block.sync
        def _(sp):
            for u in range(2):
                sp.sem_inc(stored[u], DMA_AHEAD)
            sp.dma_start(wb_in[:], wb).then_inc(wb_loaded, 16)
            for u in range(2):
                sp.dma_start(xt[u][:], x[u]).then_inc(loaded[u], 16)
            with sp.Fori(0, NBLK) as i:
                for u in range(2):
                    sp.wait_ge(lo_ready, AHEAD + 2 * i + u + 1)
                    sp.dma_start(xT[i][:, 0, :, u * P:(u + 1) * P], hi[u][:].bitcast(F32)).then_inc(stored[u], 16)
                    sp.dma_start(xT[i][:, 1, :, u * P:(u + 1) * P], lo[u][:].bitcast(F32)).then_inc(stored[u], 16)
                    sp.dma_start(xt[u][:], x[(2 * i + u + 2) % (2 * NBLK)]).then_inc(loaded[u], 16)
            for u in range(2):
                sp.wait_ge(stored[u], DMA_AHEAD + 32 * NBLK)
                sp.wait_ge(loaded[u], 16 * (NBLK + 1))

        @block.gpsimd
        def _(pool):
            pool.sem_inc(root_ready, AHEAD)
            nc.gpsimd.memset(power[:, 0:1], -0.5).then_inc(powers, 1)
            nc.gpsimd.memset(power[:, 1:], 0.5).then_inc(powers, 1)
            n = causal_masks(nc, pool, masks_done, *const["masks"])
            pool.wait_ge(masks_done, n)
            pool.wait_ge(powers, 2)
            with pool.Fori(0, NBLK) as i:
                for u in range(2):
                    pool.wait_ge(stat_steps, 6 * i + 3 * u + 3)
                    nc.gpsimd.tensor_tensor(rstd[u][:], veps[u][:], power[:, 0:1], ALU.pow)\
                        .then_inc(rstd_ready, 1)
                for u in range(2):
                    pool.wait_ge(beta_ready, AHEAD + 2 * i + u + 1)
                    nc.gpsimd.tensor_tensor(
                        sqrt_beta[:, :, bass.ds(8 * i + 4 * u, 4)],
                        beta[u][:].rearrange("p (g h) -> p g h", h=HG),
                        power[:, 1:].rearrange("p (g h) -> p g h", h=HG), ALU.pow).then_inc(root_ready, 1)

        @block.vector
        def _(dve):
            dve.sem_inc(lo_ready, AHEAD)
            dve.wait_ge(wb_loaded, 16)
            nc.vector.tensor_copy(wb_hi[:].rearrange("p k h -> p (k h)"), wb_in[:]).then_inc(wb_split, 1)
            dve.wait_ge(wb_split, 1)
            nc.vector.tensor_tensor(wb_lo[:].rearrange("p k h -> p (k h)"), wb_in[:],
                                    wb_hi[:].bitcast(F32).rearrange("p k h -> p (k h)"), ALU.subtract)\
                .then_inc(wb_split, 1)
            with dve.Fori(0, NBLK) as i:
                for u in range(2):
                    dve.wait_ge(loaded[u], 16 * i + 16)
                    nc.vector.bn_stats(stats[u][:], xt[u][:]).then_inc(stat_steps, 1)
                    dve.drain()
                    nc.vector.bn_aggr(mv[u][:], stats[u][:]).then_inc(stat_steps, 1)
                    dve.wait_ge(stat_steps, 6 * i + 3 * u + 2)
                    nc.vector.tensor_scalar(veps[u][:], mv[u][:, 1:2], LN_EPS, None, ALU.add)\
                        .then_inc(stat_steps, 1)
                for u in range(2):
                    dve.wait_ge(rstd_ready, 2 * i + u + 1)
                    dve.wait_ge(transposed, AHEAD + 2 * i)
                    nc.vector.tensor_scalar(xn[u][:], xt[u][:], mv[u][:, 0:1], rstd[u][:],
                                            ALU.subtract, ALU.mult).then_inc(xn_ready, 1)
                for u in range(2):
                    dve.wait_ge(hi_ready, 2 * i + u + 1)
                    nc.vector.tensor_tensor(lo[u][:], ps_t[u][:], hi[u][:].bitcast(F32), ALU.subtract)\
                        .then_inc(lo_ready, 1)

        @block.scalar
        def _(act):
            act.sem_inc(beta_ready, AHEAD)
            with act.Fori(0, NBLK) as i:
                for u in range(2):
                    act.wait_ge(transposed, AHEAD + 2 * i + u + 1)
                    act.wait_ge(stored[u], DMA_AHEAD + 32 * i)
                    act.wait_ge(logits, AHEAD + 2 * i)
                    nc.scalar.activation(hi[u][:], ps_t[u][:], ACT.Copy).then_inc(hi_ready, 1)
                for u in range(2):
                    act.wait_ge(logits, AHEAD + 2 * i + u + 1)
                    act.wait_ge(root_ready, AHEAD + 2 * i)
                    nc.scalar.activation(beta[u][:], ps_b[u][:, 0:NH], ACT.Sigmoid).then_inc(beta_ready, 1)

        @block.tensor
        def _(pe):
            pe.sem_inc(transposed, AHEAD)
            pe.sem_inc(logits, AHEAD)
            ident = const["ident"]
            pe.wait_ge(masks_done, const["masks_n"])
            pe.wait_ge(wb_split, 2)
            with pe.Fori(0, NBLK) as i:
                for u in range(2):
                    pe.wait_ge(xn_ready, 2 * i + u + 1)
                    pe.wait_ge(lo_ready, AHEAD + 2 * i)
                    for k in range(KT):
                        last = nc.tensor.transpose(ps_t[u][:, k, :], xn[u][:, k * P:(k + 1) * P], ident[:])
                    last.then_inc(transposed, 1)
                for u in range(2):
                    pe.wait_ge(lo_ready, AHEAD + 2 * i + u + 1)
                    pe.wait_ge(beta_ready, AHEAD + 2 * i)
                    for k in range(KT):
                        for n, (a, w) in enumerate(((hi, wb_hi), (lo, wb_hi), (hi, wb_lo))):
                            last = nc.tensor.matmul(ps_b[u][:, 0:NH], a[u][:, k, :], w[:, k, :],
                                                    start=(k == 0 and n == 0),
                                                    stop=(k == KT - 1 and n == 2))
                    last.then_inc(logits, 1)


def phase_attention(nc, ctx, w, wo, rms, xT, part, const, sqrt_beta):
    with ExitStack() as own:
        sb = lambda name, shape, dt=F32: own.enter_context(nc.sbuf_tensor(name, shape, dt))
        sem = lambda name: ctx.enter_context(nc.semaphore(name))
        bank = lambda name, shape: own.enter_context(nc.psum_tensor(name, shape, F32))

        xb = [sb(f"xb{u}", [P, 2, KT, BLK], F32R) for u in range(2)]
        w_in = sb("w_in", [P, 2, KT * P + KW])
        w_hi = sb("w_hi", [P, PAIRS, 2, KT, P], F32R)
        w_lo = sb("w_lo", [P, PAIRS, 2, KT, P], F32R)
        taps = sb("taps", [P, PAIRS, 2, KW])
        wo_sb = sb("wo_sb", [P, HG, DM])
        rms_sb = sb("rms_sb", [P, 1])
        raw = [sb(f"raw{u}", [P, 2, BLK + KW - 1]) for u in range(2)]
        halo = sb("halo", [P, PAIRS, 2, KW - 1])
        conv = [sb(f"conv{u}", [P, 2, BLK]) for u in range(2)]
        squares = [sb(f"squares{u}", [P, 2, BLK]) for u in range(2)]
        kT = sb("kT", [P, HG, BLK])
        vT = sb("vT", [P, HG, BLK])
        qT = [sb(f"qT{u}", [P, HG, BLK]) for u in range(2)]
        k_sum = sb("k_sum", [P, 2, HG])
        k_rsqrt = sb("k_rsqrt", [P, 2, HG])
        k_scale = sb("k_scale", [P, 2, HG])
        v_scale = sb("v_scale", [P, 2, HG])
        q_term = [sb(f"q_term{u}", [P, 2, HG]) for u in range(4)]
        two = range(2)
        k_nat = [[sb(f"k_nat{u}{x}", [P, HG, P]) for x in two] for u in two]
        k_chn = [[sb(f"k_chn{u}{x}", [P, HG, P]) for x in two] for u in two]
        v_nat = [[sb(f"v_nat{u}{x}", [P, HG, P]) for x in two] for u in two]
        pT = [[sb(f"pT{u}{x}", [P, HG, P]) for x in two] for u in two]
        TU = [sb(f"TU{x}", [P, 3, HG, P]) for x in two]
        M = [sb(f"M{x}", [P, HG, P]) for x in two]
        Y = [{m: sb(f"Y{x}_{m}", [P, HG, P]) for m in LEVELS} for x in two]
        y_half = [sb(f"y_half{x}", [P, HG + 1, P // 2]) for x in two]
        above = [sb(f"m_above{x}", [P, HG, P // 2]) for x in two]
        state = [sb(f"state{u}", [P, HG, P]) for u in two]
        resid = sb("resid", [P, HG, P])
        upd = sb("upd", [P, HG, P])
        o_raw = [sb(f"o_raw{x}", [P, HG, P]) for x in two]
        o_sum = [sb(f"o_sum{x}", [P, HG]) for x in two]
        o_var = [sb(f"o_var{x}", [P, HG]) for x in two]
        o_fac = [sb(f"o_fac{x}", [P, HG]) for x in two]
        o_work = sb("o_work", [P, HG, P])
        o_chn = sb("o_chn", [P, HG, P])
        staged = [sb(f"staged{x}", [P, DM]) for x in two]
        power = sb("a_power", [P, 2 * HG])
        ones = sb("a_ones", [P, 1])

        ps_a = [bank(f"ps_a{u}", [P, 2, BLK]) for u in two]
        ps_sum = bank("ps_sum", [P, 2, 2, HG])
        ps_inv = [bank(f"ps_inv{x}", [P, 512]) for x in two]
        ps_vp = bank("ps_vp", [P, HG, P])
        ps_s = [bank(f"ps_s{u}", [P, HG, P]) for u in two]

        x_loaded = [sem(f"x_loaded{u}") for u in two]
        w_loaded, w_hi_done, w_lo_done = sem("w_loaded"), sem("w_hi_done"), sem("w_lo_done")
        wo_loaded, rms_loaded = sem("wo_loaded"), sem("rms_loaded")
        stored = [sem(f"a_stored{x}") for x in two]
        consts, zeros = sem("a_consts"), sem("a_zeros")
        proj_mm, raw_done, conv_steps, silu_done = (sem(n) for n in (
            "proj_mm", "raw_done", "conv_steps", "silu_done"))
        sq_done, ksum_mm, qsum_mm, ksum_read, qsum_read, kpow_done, kscale_ready = (sem(n) for n in (
            "sq_done", "ksum_mm", "qsum_mm", "ksum_read", "qsum_read", "kpow_done", "kscale_ready"))
        inv_mm = [sem(f"inv_mm{x}") for x in two]
        inv_done = [sem(f"inv_done{x}") for x in two]
        base_steps = [sem(f"base_steps{x}") for x in two]
        v_mm, v_done, p_mm, p_done = sem("v_mm"), sem("v_done"), sem("p_mm"), sem("p_done")
        ks_mm, resid_done, upd_mm, upd_done, state_mm, state_done, o_mm, o_done = (sem(n) for n in (
            "ks_mm", "resid_done", "upd_mm", "upd_done", "state_mm", "state_done", "o_mm", "o_done"))
        osq_done, osum_steps, ofac_done, onorm_done = (sem(n) for n in (
            "osq_done", "osum_steps", "ofac_done", "onorm_done"))
        turn_mm, turn_done, out_mm, out_done = (sem(n) for n in (
            "turn_mm", "turn_done", "out_mm", "out_done"))
        block = own.enter_context(nc.Block())

        ident, upper, upper_diag, below1, above1, level_masks = const["masks"]
        FINISH = [2, 4, 6, 8, 10, 12]
        CONV = [h + 1 for h in FINISH]
        SILU = [h + 2 for h in FINISH]
        KINDS = "kkvvqq"

        def dest(j, u):
            t = {"k": kT, "v": vT, "q": qT[u]}[KINDS[j]]
            return t[:, 2 * (j % 2):2 * (j % 2) + 2, :]

        def per_head(t, x):
            return t[:, x, :].unsqueeze(2).broadcast_to([P, HG, P])

        def all_heads(t, n):
            return t[:].unsqueeze(1).broadcast_to([P, HG, n])

        def first_half(t, m):
            return t.rearrange("p h (b k j) -> p h b k j", k=2, j=m)[:, :, :, 0, :]

        def second_half(t, m):
            return t.rearrange("p h (b k j) -> p h b k j", k=2, j=m)[:, :, :, 1, :]

        def packed(t, m):
            return t.rearrange("p (h b j) -> p h b j", h=HG, j=m)

        def run_slots(emit, eng):
            emit(-1, 3, True, False, False, False)
            emit(0, 0, True, True, False, False)
            emit(1, 1, True, True, True, False)
            with eng.Fori(0, GROUPS - 1) as g:
                for c in (2, 3, 4, 5):
                    emit(4 * g + c, c % 4, True, True, True, True)
            emit(STEPS - 2, 2, True, True, True, True)
            emit(STEPS - 1, 3, False, True, True, True)
            emit(STEPS, 0, False, False, True, True)
            emit(STEPS + 1, 1, False, False, False, True)

        def group_of(s, c):
            return (s - c) // SPG

        @block.sync
        def _(sp):
            def load_x(s, c):
                sp.dma_start(xb[c % 2][:].bitcast(F32), xT[(s // 4) % 2 * 4 + c])\
                    .then_inc(x_loaded[c % 2], 16)

            def load_w(grp, j):
                sp.dma_start(w_in[:], w[grp // 2, j]).then_inc(w_loaded, 16)

            sp.dma_start(rms_sb[:], rms).then_inc(rms_loaded, 16)
            load_w(0, 0)
            load_x(0, 0)
            load_x(1, 1)
            sp.dma_start(wo_sb[:], wo[0]).then_inc(wo_loaded, 16)
            for j in range(1, PAIRS):
                sp.wait_ge(w_lo_done, j)
                load_w(0, j)

            def slot(s, c, A, INV, SCAN, POST):
                more = not isinstance(s, int) or s + 3 <= STEPS
                if more and c == 2 and isinstance(s, int) and s + 2 >= STEPS:
                    more = False
                if c == 2 and more and A:
                    for j in range(PAIRS):
                        sp.wait_ge(w_lo_done, PAIRS * ((s + 2) // SPG) + j)
                        load_w((s + 2) // SPG, j)
                if POST:
                    sp.wait_ge(out_done, 2 * (s - 2) + 2)
                    sp.dma_start(part[2 * (s - 2) + 1], staged[1][:]).then_inc(stored[1], 16)
                    if c == 1 and not (isinstance(s, int) and s > STEPS - 1):
                        sp.dma_start(wo_sb[:], wo[(s // SPG) // 2]).then_inc(wo_loaded, 16)
                if A and not (isinstance(s, int) and s + 2 >= STEPS):
                    if not (isinstance(s, int) and s < 0):
                        sp.wait_ge(proj_mm, PAIRS * (s + 1))
                        load_x(s + 2, (c + 2) % 4)
                if SCAN:
                    sp.wait_ge(out_done, 2 * (s - 1) + 1)
                    sp.dma_start(part[2 * (s - 1)], staged[0][:]).then_inc(stored[0], 16)

            run_slots(slot, sp)
            for x in two:
                sp.wait_ge(stored[x], 16 * STEPS)

        @block.tensor
        def _(pe):
            mm = nc.tensor.matmul
            pe.wait_ge(consts, 2)
            pe.wait_ge(zeros, 2 * len(LEVELS) + 4)

            def project(s, c, lo, hi):
                for n in range(lo, hi):
                    j, r = divmod(n, 24)
                    t, r = divmod(r, 12)
                    k, r = divmod(r, 3)
                    u = j % 2
                    if n % 24 == 0:
                        if j == 0:
                            pe.wait_ge(x_loaded[c % 2], 16 * ((s - c % 2) // 2 + 1))
                        pe.wait_ge(w_lo_done, PAIRS * (s // SPG) + j + 1)
                        if not (isinstance(s, int) and s == 0 and j < 2):
                            pe.wait_ge(raw_done, PAIRS * s + j - 1)
                    weights = (w_hi, w_hi, w_lo)[r]
                    last = mm(ps_a[u][:, t, :], weights[:, j, t, k, :], xb[c % 2][:, (0, 1, 0)[r], k, :],
                              start=(k == 0 and r == 0), stop=(k == KT - 1 and r == 2))
                    if n % 24 == 23:
                        last.then_inc(proj_mm, 1)

            def sum_squares(q, s, i, first):
                n = 4 * s + 2 * q + i
                pe.wait_ge(sq_done, n + 1)
                if i == 0 and not first:
                    pe.wait_ge(ksum_read if q else qsum_read, s + 1 if q else s)
                for t in range(2):
                    for x in two:
                        last = mm(ps_sum[:, q, x, 2 * i + t:2 * i + t + 1],
                                  squares[i][:, t, x * P:(x + 1) * P], ones[:], start=True, stop=True)
                last.then_inc(qsum_mm if q else ksum_mm, 1)

            def inverse(s, c, x, hop):
                u = c % 2
                out = ps_inv[x]
                if not (isinstance(s, int) and s == 0 and hop == 0):
                    pe.wait_ge(inv_done[x], HOPS * s + hop)
                if hop == 0:
                    pe.wait_ge(silu_done, PAIRS * s + 2)
                    for h in range(HG):
                        last = nc.tensor.transpose(out[:, h * P:(h + 1) * P],
                                                   kT[:, h, x * P:(x + 1) * P], ident[:])
                elif hop == 1:
                    for h in range(HG):
                        last = nc.tensor.transpose(out[:, h * P:(h + 1) * P], k_nat[u][x][:, h, :], ident[:])
                elif hop == 2:
                    for h in range(HG):
                        last = mm(out[:, h * P:(h + 1) * P], k_chn[u][x][:, h, :], k_chn[u][x][:, h, :],
                                  start=True, stop=True)
                elif hop < 13 and hop % 2 == 1:
                    m = LEVELS[(hop - 3) // 2]
                    if hop == 3:
                        pe.wait_ge(base_steps[x], 6 * s + 6)
                    for h in range(HG):
                        last = mm(out[:, 64 * h:64 * h + 64], M[x][:, h, :],
                                  first_half(TU[x][:, 0], m)[:, h], start=True, stop=True)
                elif hop < 13:
                    m = LEVELS[(hop - 3) // 2]
                    for h in range(HG):
                        mm(out[:, 64 * h:64 * h + 64], TU[x][:, 1 + u, h, :],
                           first_half(Y[x][m][:], m)[:, h], start=True, stop=True)
                    for h in range(HG):
                        last = mm(out[:, 256 + 64 * h:320 + 64 * h], Y[x][m][:, h, :],
                                  second_half(TU[x][:, 1 + u], m)[:, h], start=True, stop=True)
                elif hop == 13:
                    for h in range(HG):
                        last = mm(out[:, 64 * h:64 * h + 64], M[x][:, h, :], TU[x][:, 0, h, 0:64],
                                  start=True, stop=True)
                else:
                    for h in range(HG):
                        last = mm(out[:, 64 * h:64 * h + 64],
                                  y_half[x][64:P, h:h + 2, :].rearrange("p h j -> p (h j)"),
                                  TU[x][64:P, 1 + u, h, 64:P], start=True, stop=True)
                last.then_inc(inv_mm[x], 1)

            def values(s, c, x):
                if x == 0:
                    pe.wait_ge(silu_done, PAIRS * s + 4)
                if x == 1 or not (isinstance(s, int) and s == 0):
                    if x:
                        pe.wait_ge(v_done, 2 * s + 1)
                    else:
                        pe.wait_ge(p_done, 2 * s)
                for h in range(HG):
                    last = nc.tensor.transpose(ps_vp[:, h, :], vT[:, h, x * P:(x + 1) * P], ident[:])
                last.then_inc(v_mm, 1)

            def scores(s, c, x):
                u = c % 2
                if x == 0:
                    pe.wait_ge(silu_done, PAIRS * s + 6)
                    pe.wait_ge(v_done, 2 * s + 2)
                else:
                    pe.wait_ge(p_done, 2 * s + 1)
                pe.wait_ge(inv_done[x], HOPS * s + 2)
                for h in range(HG):
                    last = mm(ps_vp[:, h, :], k_chn[u][x][:, h, :], qT[u][:, h, x * P:(x + 1) * P],
                              start=True, stop=True)
                last.then_inc(p_mm, 1)

            def scan_ks(r, c, x):
                u, n = c % 2, 2 * r + x
                if x == 0:
                    for y in two:
                        pe.wait_ge(inv_done[y], HOPS * (r + 1))
                pe.wait_ge(state_done, n + 1)
                if not (isinstance(r, int) and r == 0 and x == 0):
                    if x == 0:
                        pe.wait_ge(turn_done, 2 * r - 1)
                for h in range(HG):
                    last = mm(ps_s[0][:, h, :], k_chn[u][x][:, h, :], state[x][:, h, :], start=True, stop=True)
                last.then_inc(ks_mm, 1)

            def scan_upd(r, c, x):
                u, n = c % 2, 2 * r + x
                pe.wait_ge(resid_done, n + 1)
                if x == 0:
                    if not (isinstance(r, int) and r == 0):
                        pe.wait_ge(out_done, 2 * r - 1)
                else:
                    if isinstance(r, int) and r == 0:
                        pe.wait_ge(o_done, n)
                    else:
                        pe.wait_ge(out_done, 2 * r)
                for h in range(HG):
                    last = mm(ps_s[1][:, h, :], TU[x][:, 1 + u, h, :], resid[:, h, :], start=True, stop=True)
                last.then_inc(upd_mm, 1)

            def scan_state_out(r, c, x):
                u, n = c % 2, 2 * r + x
                pe.wait_ge(upd_done, n + 1)
                if x == 0 and not (isinstance(r, int) and r == 0):
                    pe.wait_ge(turn_done, 2 * r)
                for h in range(HG):
                    last = mm(ps_s[0][:, h, :], k_nat[u][x][:, h, :], upd[:, h, :], start=True, stop=True)
                last.then_inc(state_mm, 1)
                if x == 0:
                    pe.wait_ge(p_done, 2 * r + 2)
                for h in range(HG):
                    mm(ps_s[1][:, h, :], qT[u][:, h, x * P:(x + 1) * P], state[x][:, h, :],
                       start=True, stop=False)
                    last = mm(ps_s[1][:, h, :], pT[u][x][:, h, :], upd[:, h, :], start=False, stop=True)
                last.then_inc(o_mm, 1)

            def turn(r, c, x, next_scan):
                n = 2 * r + x
                pe.wait_ge(onorm_done, n + 1)
                if x == 0:
                    pe.wait_ge(state_done, n + 3)
                elif next_scan:
                    pe.wait_ge(resid_done, n + 2)
                else:
                    pe.wait_ge(turn_done, n)
                for h in range(HG):
                    last = nc.tensor.transpose(ps_s[0][:, h, :], o_work[:, h, :], ident[:])
                last.then_inc(turn_mm, 1)

            def project_out(r, c, x, next_scan):
                n = 2 * r + x
                pe.wait_ge(turn_done, n + 1)
                pe.wait_ge(wo_loaded, 16 * (r // SPG + 1))
                if x == 0:
                    pe.wait_ge(o_done, n + 2)
                elif next_scan:
                    pe.wait_ge(o_done, n + 2)
                else:
                    pe.wait_ge(out_done, n)
                for h in range(HG):
                    last = mm(ps_s[1][:].rearrange("p h d -> p (h d)"), o_chn[:, h, :], wo_sb[:, h, :],
                              start=(h == 0), stop=(h == HG - 1))
                last.then_inc(out_mm, 1)

            def slot(s, c, A, INV, SCAN, POST):
                for hop in range(HOPS):
                    if INV:
                        for x in two:
                            inverse(s, c, x, hop)
                    r, rc = s - 1, (c - 1) % 4
                    if SCAN and hop == 1:
                        scan_ks(r, rc, 0)
                    if INV and hop in (1, 2):
                        values(s, c, hop - 1)
                    if INV and hop == 1:
                        for i in range(2):
                            sum_squares(1, s, i, isinstance(s, int) and s == 0 and False)
                    if POST and hop == 2:
                        turn(s - 2, (c - 2) % 4, 1, SCAN)
                    if SCAN and hop == 3:
                        scan_upd(r, rc, 0)
                    if INV and hop in (3, 4):
                        scores(s, c, hop - 3)
                    if SCAN and hop == 4:
                        scan_state_out(r, rc, 0)
                    if POST and hop == 5:
                        project_out(s - 2, (c - 2) % 4, 1, SCAN)
                    if SCAN and hop == 6:
                        scan_ks(r, rc, 1)
                    if SCAN and hop == 8:
                        scan_upd(r, rc, 1)
                    if SCAN and hop == 9:
                        scan_state_out(r, rc, 1)
                    if SCAN and hop == 11:
                        turn(r, rc, 0, True)
                    if SCAN and hop == 13:
                        project_out(r, rc, 0, True)
                    if A and hop < 13:
                        project(s + 1, (c + 1) % 4, 0 if hop == 0 else 12 + 11 * (hop - 1),
                                12 + 11 * hop)
                    if A and hop in (7, 9):
                        sum_squares(0, s + 1, (hop - 7) // 2, isinstance(s, int) and s == -1)

            run_slots(slot, pe)

        @block.scalar
        def _(act):
            act.wait_ge(rms_loaded, 16)

            def split_w(grp, j):
                act.wait_ge(w_loaded, 16 * (PAIRS * grp + j + 1))
                if not (isinstance(grp, int) and grp == 0):
                    act.wait_ge(proj_mm, PAIRS * (SPG * grp - 1) + j + 1)
                nc.scalar.activation(w_hi[:, j].rearrange("p t k c -> p t (k c)"), w_in[:, :, 0:KT * P],
                                     ACT.Copy).then_inc(w_hi_done, 1)

            def copy_raw(s, c, j):
                act.wait_ge(proj_mm, PAIRS * s + j + 1)
                if not (isinstance(s, int) and s == 0 and j < 2):
                    act.wait_ge(conv_steps, 10 * (PAIRS * s + j - 1))
                nc.scalar.activation(raw[j % 2][:, :, KW - 1:], ps_a[j % 2][:], ACT.Copy)\
                    .then_inc(raw_done, 1)

            def silu(s, c, j):
                act.wait_ge(conv_steps, 10 * (PAIRS * s + j) + 9)
                if not (isinstance(s, int) and s == 0):
                    if KINDS[j] == "k":
                        for x in two:
                            act.wait_ge(inv_mm[x], HOPS * (s - 1) + 1)
                        act.wait_ge(sq_done, 4 * (s - 1) + 2)
                    elif KINDS[j] == "v":
                        act.wait_ge(v_mm, 2 * (s - 1) + 2)
                    elif not (isinstance(s, int) and s < 2):
                        act.wait_ge(o_mm, 2 * (s - 2) + 2)
                nc.scalar.activation(dest(j, c % 2), conv[j % 2][:], ACT.Silu).then_inc(silu_done, 1)

            def inverse(s, c, x, hop):
                u = c % 2
                out = ps_inv[x]
                act.wait_ge(inv_mm[x], HOPS * s + hop + 1)
                if hop == 1:
                    if not (isinstance(s, int) and s < 2):
                        act.wait_ge(ks_mm, 2 * (s - 2) + x + 1)
                    last = nc.scalar.activation(k_chn[u][x][:].rearrange("p h t -> p (h t)"), out[:], ACT.Copy)
                elif hop in (11, 12):
                    blocks = [(32, 0), (96, 64)]
                    ps = out[:, 0:256].rearrange("p (h b j) -> p h b j", h=HG, j=32)
                    if hop == 11:
                        for b, (row, col) in enumerate(blocks):
                            last = nc.scalar.activation(Y[x][32][row:row + 32, :, col:col + 32],
                                                        ps[row:row + 32, :, b, :], ACT.Copy)
                    else:
                        psu = out[:, 256:512].rearrange("p (h b j) -> p h b j", h=HG, j=32)
                        for b, (row, col) in enumerate(blocks):
                            nc.scalar.activation(TU[x][row:row + 32, 0, :, col:col + 32],
                                                 ps[row:row + 32, :, b, :], ACT.Copy, scale=-1.0)
                            last = nc.scalar.activation(TU[x][col:col + 32, 1 + u, :, row:row + 32],
                                                        psu[col:col + 32, :, b, :], ACT.Copy, scale=-1.0)
                elif hop == 13:
                    last = nc.scalar.activation(y_half[x][64:P, 0:HG, :],
                                                out[64:P, 0:256].rearrange("p (h j) -> p h j", h=HG), ACT.Copy)
                elif hop == 14:
                    last = nc.scalar.activation(TU[x][0:64, 1 + u, :, 64:P],
                                                out[0:64, 0:256].rearrange("p (h j) -> p h j", h=HG),
                                                ACT.Copy, scale=-1.0)
                last.then_inc(inv_done[x], 1)

            def copy_upd(r, x):
                n = 2 * r + x
                act.wait_ge(upd_mm, n + 1)
                if not (isinstance(r, int) and n == 0):
                    act.wait_ge(o_mm, n)
                nc.scalar.activation(upd[:], ps_s[1][:], ACT.Copy).then_inc(upd_done, 1)

            def copy_o(r, x):
                n = 2 * r + x
                act.wait_ge(o_mm, n + 1)
                if not (isinstance(r, int) and r == 0):
                    act.wait_ge(onorm_done, n - 1)
                nc.scalar.activation(o_raw[x][:], ps_s[1][:], ACT.Copy).then_inc(o_done, 1)

            def copy_turned(r, x):
                n = 2 * r + x
                act.wait_ge(turn_mm, n + 1)
                if not (isinstance(r, int) and n == 0):
                    act.wait_ge(out_mm, n)
                nc.scalar.activation(o_chn[:], ps_s[0][:], ACT.Copy, scale=rms_sb[:]).then_inc(turn_done, 1)

            def copy_out(r, x):
                n = 2 * r + x
                act.wait_ge(out_mm, n + 1)
                if not (isinstance(r, int) and r == 0):
                    act.wait_ge(stored[x], 16 * r)
                nc.scalar.activation(staged[x][:], ps_s[1][:].rearrange("p h d -> p (h d)"), ACT.Copy)\
                    .then_inc(out_done, 1)

            for j in range(PAIRS):
                split_w(0, j)

            def slot(s, c, A, INV, SCAN, POST):
                for hop in range(HOPS):
                    if INV and hop in (1, 11, 12, 13, 14):
                        for x in two:
                            inverse(s, c, x, hop)
                    r = s - 1
                    if POST and hop == 2:
                        copy_turned(s - 2, 1)
                    if SCAN and hop == 3:
                        copy_upd(r, 0)
                    if SCAN and hop == 4:
                        copy_o(r, 0)
                    if POST and hop == 5:
                        copy_out(s - 2, 1)
                    if SCAN and hop == 8:
                        copy_upd(r, 1)
                    if SCAN and hop == 9:
                        copy_o(r, 1)
                    if SCAN and hop == 11:
                        copy_turned(r, 0)
                    if SCAN and hop == 13:
                        copy_out(r, 0)
                    if A and hop in CONV:
                        copy_raw(s + 1, (c + 1) % 4, CONV.index(hop))
                    if A and hop in SILU:
                        silu(s + 1, (c + 1) % 4, SILU.index(hop))
                    ahead = not (isinstance(s, int) and s + 2 > STEPS)
                    if c == 2 and A and hop in SILU[:5] and not (isinstance(s, int) and s + 2 >= STEPS):
                        split_w((s + 2) // SPG, SILU.index(hop))
                    if c == 3 and hop == 0 and A and not (isinstance(s, int) and s < 0):
                        split_w((s + 1) // SPG, 5)

            run_slots(slot, act)

        @block.gpsimd
        def _(pool):
            nc.gpsimd.memset(power[:], -0.5).then_inc(consts, 1)
            nc.gpsimd.memset(ones[:], 1.0).then_inc(consts, 1)
            for x in two:
                for m in LEVELS:
                    nc.gpsimd.memset(Y[x][m][:], 0.0).then_inc(zeros, 1)
                nc.gpsimd.memset(y_half[x][:, HG], 0.0).then_inc(zeros, 1)
            nc.gpsimd.memset(state[0][:], 0.0).then_inc(zeros, 1)
            nc.gpsimd.memset(halo[:], 0.0).then_inc(zeros, 1)
            pool.wait_ge(consts, 2)

            def square(s, c, i):
                j = (0, 1, 4, 5)[i]
                n = 4 * s + i
                pool.wait_ge(silu_done, PAIRS * s + j + 1)
                if i < 2:
                    if not (isinstance(s, int) and s == 0):
                        pool.wait_ge(qsum_mm, 2 * (s - 1) + i + 1)
                else:
                    pool.wait_ge(ksum_mm, 2 * s + i - 1)
                src = dest(j, c % 2)
                nc.gpsimd.tensor_tensor(squares[i % 2][:], src, src, ALU.mult).then_inc(sq_done, 1)

            def norm_o(r, c, x):
                n = 2 * r + x
                pool.wait_ge(osum_steps, 2 * n + 2)
                nc.gpsimd.tensor_tensor(o_fac[x][:], o_var[x][:], power[:, 0:HG], ALU.pow)\
                    .then_inc(ofac_done, 1)
                pool.wait_ge(ofac_done, n + 1)
                if not (isinstance(r, int) and n == 0):
                    pool.wait_ge(turn_mm, n)
                nc.gpsimd.tensor_tensor(o_work[:], o_raw[x][:],
                                        o_fac[x][:].unsqueeze(2).broadcast_to([P, HG, P]), ALU.mult)\
                    .then_inc(onorm_done, 1)

            def square_o(r, x):
                n = 2 * r + x
                pool.wait_ge(o_done, n + 1)
                if not (isinstance(r, int) and n == 0):
                    pool.wait_ge(turn_mm, n)
                nc.gpsimd.tensor_tensor(o_work[:], o_raw[x][:], o_raw[x][:], ALU.mult).then_inc(osq_done, 1)

            def slot(s, c, A, INV, SCAN, POST):
                for hop in range(HOPS):
                    r = s - 1
                    if POST and hop == 1:
                        norm_o(s - 2, (c - 2) % 4, 1)
                    if SCAN and hop == 5:
                        square_o(r, 0)
                    if SCAN and hop == 7:
                        norm_o(r, (c - 1) % 4, 0)
                    if A and hop in (5, 7):
                        square(s + 1, (c + 1) % 4, (hop - 5) // 2)
                    if A and hop == 11:
                        pool.wait_ge(ksum_read, s + 2)
                        if not (isinstance(s, int) and s < 0):
                            pool.wait_ge(kscale_ready, 2 * (s + 1))
                        nc.gpsimd.tensor_tensor(k_rsqrt[:].rearrange("p x h -> p (x h)"),
                                                k_sum[:].rearrange("p x h -> p (x h)"), power[:],
                                                ALU.pow).then_inc(kpow_done, 1)
                    if SCAN and hop == 13:
                        square_o(r, 1)
                    if A and hop in (13, 14):
                        square(s + 1, (c + 1) % 4, hop - 11)

            run_slots(slot, pool)

        @block.vector
        def _(dve):
            tt = nc.vector.tensor_tensor
            dve.wait_ge(zeros, 2 * len(LEVELS) + 4)

            nc.vector.tensor_copy(state[0][:], state[0][:]).then_inc(state_done, 1)

            def split_w(grp, j):
                dve.wait_ge(w_hi_done, PAIRS * grp + j + 1)
                if not (isinstance(grp, int) and grp == 0):
                    dve.wait_ge(proj_mm, PAIRS * (SPG * grp - 1) + j + 1)
                    dve.wait_ge(conv_steps, 10 * (PAIRS * (SPG * grp - 1) + j + 1))
                nc.vector.tensor_copy(taps[:, j], w_in[:, :, KT * P:])
                tt(w_lo[:, j].rearrange("p t k c -> p t (k c)"), w_in[:, :, 0:KT * P],
                   w_hi[:, j].bitcast(F32).rearrange("p t k c -> p t (k c)"), ALU.subtract).then_inc(w_lo_done, 1)

            def convolve(s, c, j):
                u = j % 2
                n = 10 * (PAIRS * s + j)
                dve.wait_ge(raw_done, PAIRS * s + j + 1)
                if c == 0:
                    nc.vector.memset(raw[u][:, :, 0:KW - 1], 0.0).then_inc(conv_steps, 1)
                else:
                    nc.vector.tensor_copy(raw[u][:, :, 0:KW - 1], halo[:, j]).then_inc(conv_steps, 1)
                if not (isinstance(s, int) and s == 0 and j < 2):
                    dve.wait_ge(silu_done, PAIRS * s + j - 1)
                dve.wait_ge(w_lo_done, PAIRS * (s // SPG) + j + 1)
                dve.wait_ge(conv_steps, n + 1)
                for i in range(KW):
                    for t in range(2):
                        if i == 0:
                            nc.vector.tensor_scalar(conv[u][:, t, :], raw[u][:, t, 0:BLK],
                                                    taps[:, j, t, 0:1], None, ALU.mult)\
                                .then_inc(conv_steps, 1)
                        else:
                            dve.wait_ge(conv_steps, n + 1 + 2 * i + t)
                            nc.vector.scalar_tensor_tensor(
                                conv[u][:, t, :], raw[u][:, t, i:i + BLK], taps[:, j, t, i:i + 1],
                                conv[u][:, t, :], ALU.mult, ALU.add).then_inc(conv_steps, 1)
                nc.vector.tensor_copy(halo[:, j], raw[u][:, :, BLK:]).then_inc(conv_steps, 1)

            def inverse(s, c, x, hop):
                u = c % 2
                out = ps_inv[x]
                dve.wait_ge(inv_mm[x], HOPS * s + hop + 1)
                if hop == 0:
                    dve.wait_ge(kscale_ready, 2 * (s + 1))
                    if not (isinstance(s, int) and s < 2):
                        dve.wait_ge(state_mm, 2 * (s - 2) + x + 1)
                    tt(k_nat[u][x][:], out[:].rearrange("p (h d) -> p h d", h=HG), per_head(k_scale, x),
                       ALU.mult).then_inc(inv_done[x], 1)
                elif hop == 2:
                    n = 6 * s
                    ps = out[:].rearrange("p (h t) -> p h t", h=HG)
                    tt(M[x][:], ps, all_heads(upper, P), ALU.mult).then_inc(base_steps[x], 1)
                    tt(y_half[x][:, 0:HG], ps.rearrange("p h (c k) -> p h c k", k=2)[:, :, :, 0],
                       all_heads(below1, P // 2), ALU.mult).then_inc(inv_done[x], 1)
                    if not (isinstance(s, int) and s < 2):
                        dve.wait_ge(upd_mm, 2 * (s - 2) + x + 1)
                    idn = ident[:].rearrange("p (c k) -> p c k", k=2)
                    even = idn[:, :, 0].unsqueeze(1).broadcast_to([P, HG, P // 2])
                    odd = idn[:, :, 1].unsqueeze(1).broadcast_to([P, HG, P // 2])
                    T = TU[x][:, 0].rearrange("p h (c k) -> p h c k", k=2)
                    U = TU[x][:, 1 + u].rearrange("p h (c k) -> p h c k", k=2)
                    nc.vector.tensor_copy(T[:, :, :, 1], odd).then_inc(base_steps[x], 1)
                    nc.vector.tensor_copy(U[:, :, :, 0], even).then_inc(base_steps[x], 1)
                    dve.wait_ge(base_steps[x], n + 1)
                    tt(above[x][:], M[x][:].rearrange("p h (c k) -> p h c k", k=2)[:, :, :, 1],
                       all_heads(above1, P // 2), ALU.mult).then_inc(base_steps[x], 1)
                    dve.wait_ge(inv_done[x], HOPS * s + 3)
                    tt(T[:, :, :, 0], even, y_half[x][:, 0:HG], ALU.subtract).then_inc(base_steps[x], 1)
                    dve.wait_ge(base_steps[x], n + 4)
                    tt(U[:, :, :, 1], odd, above[x][:], ALU.subtract).then_inc(base_steps[x], 1)
                elif hop % 2 == 1:
                    m = LEVELS[(hop - 3) // 2]
                    mask = level_masks[m][:].rearrange("p (b j) -> p b j", j=m)\
                        .unsqueeze(1).broadcast_to([P, HG, P // (2 * m), m])
                    tt(first_half(Y[x][m][:], m), packed(out[:, 0:256], m), mask, ALU.mult)\
                        .then_inc(inv_done[x], 1)
                else:
                    m = LEVELS[(hop - 3) // 2]
                    T, U = first_half(TU[x][:, 0], m), second_half(TU[x][:, 1 + u], m)
                    tt(T, T, packed(out[:, 0:256], m), ALU.subtract)
                    tt(U, U, packed(out[:, 256:512], m), ALU.subtract).then_inc(inv_done[x], 1)

            def values(s, c, x):
                u = c % 2
                dve.wait_ge(v_mm, 2 * s + x + 1)
                tt(v_nat[u][x][:], ps_vp[:], per_head(v_scale, x), ALU.mult).then_inc(v_done, 1)

            def scores(s, c, x):
                u = c % 2
                dve.wait_ge(p_mm, 2 * s + x + 1)
                if not (isinstance(s, int) and s < 2):
                    dve.wait_ge(o_mm, 2 * (s - 2) + x + 1)
                tt(pT[u][x][:], ps_vp[:], all_heads(upper_diag, P), ALU.mult).then_inc(p_done, 1)

            def residual(r, c, x):
                n = 2 * r + x
                dve.wait_ge(ks_mm, n + 1)
                if not (isinstance(r, int) and n == 0):
                    dve.wait_ge(upd_mm, n)
                dve.wait_ge(v_done, n + 1)
                tt(resid[:], v_nat[c % 2][x][:], ps_s[0][:], ALU.subtract).then_inc(resid_done, 1)

            def new_state(r, c, x):
                n = 2 * r + x
                dve.wait_ge(state_mm, n + 1)
                if c == SPG - 1 and x == 1:
                    dve.wait_ge(o_mm, n)
                    nc.vector.memset(state[0][:], 0.0).then_inc(state_done, 1)
                    return
                if not (isinstance(r, int) and n == 0):
                    dve.wait_ge(o_mm, n)
                dve.wait_ge(state_done, n + 1)
                tt(state[1 - x][:], state[x][:], ps_s[0][:], ALU.add).then_inc(state_done, 1)

            def sum_o(r, c, x):
                n = 2 * r + x
                dve.wait_ge(osq_done, n + 1)
                nc.vector.reduce_sum(o_sum[x][:], o_work[:], AX_X).then_inc(osum_steps, 1)
                dve.wait_ge(osum_steps, 2 * n + 1)
                dve.wait_ge(qsum_read, r + 1)
                if not (isinstance(r, int) and r == 0):
                    dve.wait_ge(ofac_done, n - 1)
                nc.vector.scalar_tensor_tensor(o_var[x][:], o_sum[x][:], 1.0 / HD, q_term[c][:, x, :],
                                               ALU.mult, ALU.add).then_inc(osum_steps, 1)

            for j in range(PAIRS):
                split_w(0, j)

            def slot(s, c, A, INV, SCAN, POST):
                for hop in range(HOPS):
                    r, rc = s - 1, (c - 1) % 4
                    if INV and (hop in (0, 2) or 3 <= hop <= 10):
                        for x in two:
                            inverse(s, c, x, hop)
                    if SCAN and hop == 1:
                        residual(r, rc, 0)
                    if INV and hop in (1, 2):
                        values(s, c, hop - 1)
                    if INV and hop == 3:
                        dve.wait_ge(qsum_mm, 2 * s + 2)
                        nc.vector.tensor_scalar(q_term[c][:], ps_sum[:, 1], L2_EPS, HD * RMS_EPS,
                                                ALU.add, ALU.mult).then_inc(qsum_read, 1)
                    if INV and hop in (3, 4):
                        scores(s, c, hop - 3)
                    if SCAN and hop == 4:
                        new_state(r, rc, 0)
                    if SCAN and hop == 6:
                        residual(r, rc, 1)
                        sum_o(r, rc, 0)
                    if SCAN and hop == 9:
                        new_state(r, rc, 1)
                    if SCAN and hop == 14:
                        sum_o(r, rc, 1)
                    if A and hop in CONV:
                        convolve(s + 1, (c + 1) % 4, CONV.index(hop))
                    if A and hop == 10:
                        dve.wait_ge(ksum_mm, 2 * (s + 1) + 2)
                        if not (isinstance(s, int) and s < 0):
                            dve.wait_ge(kpow_done, s + 1)
                        nc.vector.tensor_scalar(k_sum[:], ps_sum[:, 0], L2_EPS, None, ALU.add)\
                            .then_inc(ksum_read, 1)
                    if A and hop == 12:
                        dve.wait_ge(kpow_done, s + 2)
                        root = sqrt_beta[:].rearrange("p g t -> p (g t)")[:, bass.ds(8 * (s + 1), 8)]
                        tt(k_scale[:].rearrange("p x h -> p (x h)"),
                           k_rsqrt[:].rearrange("p x h -> p (x h)"), root, ALU.mult)\
                            .then_inc(kscale_ready, 1)
                        nc.vector.tensor_copy(v_scale[:].rearrange("p x h -> p (x h)"), root)\
                            .then_inc(kscale_ready, 1)
                    if c == 2 and A and hop in SILU[:5] and not (isinstance(s, int) and s + 2 >= STEPS):
                        split_w((s + 2) // SPG, SILU.index(hop))
                    if c == 3 and hop == 1 and A and not (isinstance(s, int) and s < 0):
                        split_w((s + 1) // SPG, 5)

            run_slots(slot, dve)


def phase_feed_forward(nc, ctx, x, wf, xT, part, out):
    TB = 512
    NJ = DH // P
    NT = TB // P
    with ExitStack() as own:
        sb = lambda name, shape, dt=F32: own.enter_context(nc.sbuf_tensor(name, shape, dt))
        sem = lambda name: ctx.enter_context(nc.semaphore(name))
        bank = lambda name, shape: own.enter_context(nc.psum_tensor(name, shape, F32))
        two = range(2)
        wf_sb = sb("wf_sb", [P, NJ, 3 * DM])
        w_hi = [sb(f"f_whi{u}", [P, 3, DM], F32R) for u in two]
        w_lo = [sb(f"f_wlo{u}", [P, 3, DM], F32R) for u in two]
        xb = sb("f_x", [P, 2, 2, KT, BLK], F32R)
        act_g = [sb(f"f_g{u}", [P, TB]) for u in two]
        hid = [sb(f"f_hid{u}", [P, TB]) for u in two]
        h_hi = [sb(f"f_hhi{u}", [P, TB], F32R) for u in two]
        h_lo = [sb(f"f_hlo{u}", [P, TB], F32R) for u in two]
        parts = [sb(f"f_part{u}", [P, NG, DM]) for u in two]
        x_res = [sb(f"f_xres{u}", [P, DM]) for u in two]
        gate = [sb(f"f_gate{u}", [P, DM]) for u in two]
        total = [sb(f"f_total{u}", [P, DM]) for u in two]
        ps_g = [bank(f"f_psg{u}", [P, TB]) for u in two]
        ps_u = [bank(f"f_psu{u}", [P, TB]) for u in two]
        ps_o = [bank(f"f_pso{t}", [P, DM]) for t in range(NT)]
        wf_loaded = [sem(f"f_wf_loaded{j}") for j in range(4)]
        x_loaded = sem("f_x_loaded")
        part_loaded = [sem(f"f_part_loaded{u}") for u in two]
        hi_done, lo_done = sem("f_hi_done"), sem("f_lo_done")
        g_mm, u_mm, g_done, hid_done, hhi_done, hlo_done, down_mm = (sem(n) for n in (
            "f_g_mm", "f_u_mm", "f_g_done", "f_hid_done", "f_hhi_done", "f_hlo_done", "f_down_mm"))
        gate_done, sums, res_done = sem("f_gate_done"), sem("f_sums"), sem("f_res_done")
        out_stored = [sem(f"f_out_stored{u}") for u in two]
        block = own.enter_context(nc.Block())
        NB = B * S // TB

        @block.sync
        def _(sp):
            for u in two:
                sp.sem_inc(out_stored[u], DMA_AHEAD)
            def load_x(b):
                for i in range(2):
                    sp.dma_start(xb[:, i].bitcast(F32), xT[2 * b + i]).then_inc(x_loaded, 16)

            def load_parts(b, t):
                u = t % 2
                sp.dma_start(parts[u][:], part.rearrange("(g q) p d -> q p g d", g=NG)[NT * b + t])\
                    .then_inc(part_loaded[u], 16)
                sp.dma_start(x_res[u][:], x[NT * b + t]).then_inc(part_loaded[u], 16)

            sp.dma_start(wf_sb[:, 0:4], wf[:, 0:4]).then_inc(wf_loaded[0], 16)
            load_x(0)
            for j in range(1, 4):
                sp.dma_start(wf_sb[:, 4 * j:4 * j + 4], wf[:, 4 * j:4 * j + 4]).then_inc(wf_loaded[j], 16)
            with sp.Fori(0, NB) as b:
                for t in range(2):
                    load_parts(b, t)
                sp.wait_ge(u_mm, NJ * (b + 1))
                for i in range(2):
                    sp.dma_start(xb[:, i].bitcast(F32), xT[(2 * b + 2) % NBLK + i]).then_inc(x_loaded, 16)
                for t in range(NT):
                    sp.wait_ge(res_done, AHEAD + 2 * (NT * b + t) + 2)
                    sp.dma_start(out[NT * b + t], total[t % 2][:]).then_inc(out_stored[t % 2], 16)
                    if t < 2:
                        load_parts(b, t + 2)
            for u in two:
                sp.wait_ge(out_stored[u], DMA_AHEAD + 16 * NB * NT // 2)
            sp.wait_ge(x_loaded, 32 * (NB + 1))

        @block.tensor
        def _(pe):
            pe.sem_inc(down_mm, AHEAD)
            def gate_up(b, j):
                u = j % 2
                n = NJ * b + j
                if j == 0:
                    pe.wait_ge(x_loaded, 32 * (b + 1))
                pe.wait_ge(lo_done, n + 1)
                if not (j < 2):
                    pe.wait_ge(hid_done, AHEAD + n - 1)
                else:
                    pe.wait_ge(hid_done, AHEAD + NJ * b)
                for i, ps in enumerate((ps_g[u], ps_u[u])):
                    for k in range(KT):
                        for r in range(3):
                            w = (w_hi, w_hi, w_lo)[r][u]
                            last = nc.tensor.matmul(
                                ps[:].rearrange("p (b t) -> p b t", b=2), w[:, i, k * P:(k + 1) * P],
                                xb[:, :, (0, 1, 0)[r], k, :],
                                start=(k == 0 and r == 0), stop=(k == KT - 1 and r == 2))
                    last.then_inc(u_mm if i else g_mm, 1)

            def down(b, j):
                u = j % 2
                n = NJ * b + j
                pe.wait_ge(hlo_done, n + 1)
                if j == 0:
                    pe.wait_ge(gate_done, AHEAD + NT * b)
                for t in range(NT):
                    for r in range(3):
                        h = (h_hi, h_hi, h_lo)[r][u]
                        w = (w_hi, w_lo, w_hi)[r][u]
                        last = nc.tensor.matmul(ps_o[t][:], h[:, t * P:(t + 1) * P], w[:, 2, :],
                                                start=(j == 0 and r == 0), stop=(j == NJ - 1 and r == 2))
                last.then_inc(down_mm, 1)

            with pe.Fori(0, NB) as b:
                gate_up(b, 0)
                for j in range(1, NJ):
                    gate_up(b, j)
                    down(b, j - 1)
                down(b, NJ - 1)

        @block.scalar
        def _(act):
            act.sem_inc(gate_done, AHEAD)
            act.sem_inc(hhi_done, AHEAD)
            def split_hi(b, j):
                n = NJ * b + j
                if j >= 2:
                    act.wait_ge(down_mm, AHEAD + n - 1)
                else:
                    act.wait_ge(down_mm, AHEAD + NJ * b)
                nc.scalar.activation(w_hi[j % 2][:].rearrange("p i d -> p (i d)"), wf_sb[:, j, :], ACT.Copy)\
                    .then_inc(hi_done, 1)

            def silu_gate(b, j):
                n = NJ * b + j
                act.wait_ge(g_mm, n + 1)
                act.wait_ge(hid_done, AHEAD + (n - 1 if j >= 2 else NJ * b))
                nc.scalar.activation(act_g[j % 2][:], ps_g[j % 2][:], ACT.Silu).then_inc(g_done, 1)

            def split_hidden(b, j):
                n = NJ * b + j
                act.wait_ge(hid_done, AHEAD + n + 1)
                act.wait_ge(down_mm, AHEAD + (n - 1 if j >= 2 else NJ * b))
                nc.scalar.activation(h_hi[j % 2][:], hid[j % 2][:], ACT.Copy).then_inc(hhi_done, 1)

            for j in range(4):
                act.wait_ge(wf_loaded[j], 16)
            with act.Fori(0, NB) as b:
                split_hi(b, 0)
                split_hi(b, 1)
                for j in range(NJ):
                    silu_gate(b, j)
                    split_hidden(b, j)
                    if j + 2 < NJ:
                        split_hi(b, j + 2)
                act.wait_ge(down_mm, AHEAD + NJ * (b + 1))
                for t in range(NT):
                    act.wait_ge(res_done, AHEAD + 2 * NT * b + (0 if t < 2 else 2 * t - 3))
                    nc.scalar.activation(gate[t % 2][:], ps_o[t][:], ACT.Silu).then_inc(gate_done, 1)

        @block.vector
        def _(dve):
            dve.sem_inc(hid_done, AHEAD)
            dve.sem_inc(res_done, AHEAD)
            tt = nc.vector.tensor_tensor

            def split_lo(b, j):
                dve.wait_ge(hi_done, NJ * b + j + 1)
                tt(w_lo[j % 2][:].rearrange("p i d -> p (i d)"), wf_sb[:, j, :],
                   w_hi[j % 2][:].bitcast(F32).rearrange("p i d -> p (i d)"), ALU.subtract).then_inc(lo_done, 1)

            with dve.Fori(0, NB) as b:
                split_lo(b, 0)
                split_lo(b, 1)
                for j in range(NJ):
                    n = NJ * b + j
                    u = j % 2
                    dve.wait_ge(g_done, n + 1)
                    dve.wait_ge(u_mm, n + 1)
                    dve.wait_ge(hhi_done, AHEAD + (n - 1 if j >= 2 else NJ * b))
                    tt(hid[u][:], act_g[u][:], ps_u[u][:], ALU.mult).then_inc(hid_done, 1)
                    dve.wait_ge(hhi_done, AHEAD + n + 1)
                    tt(h_lo[u][:], hid[u][:], h_hi[u][:].bitcast(F32), ALU.subtract).then_inc(hlo_done, 1)
                    if j + 2 < NJ:
                        split_lo(b, j + 2)
                for t in range(NT):
                    u = t % 2
                    m = NT * b + t
                    dve.wait_ge(gate_done, AHEAD + m + 1)
                    dve.wait_ge(sums, 3 * m + 3)
                    tt(total[u][:], total[u][:], gate[u][:], ALU.mult).then_inc(res_done, 1)
                    dve.wait_ge(res_done, AHEAD + 2 * m + 1)
                    tt(total[u][:], total[u][:], x_res[u][:], ALU.add).then_inc(res_done, 1)

        @block.gpsimd
        def _(pool):
            tt = nc.gpsimd.tensor_tensor
            with pool.Fori(0, NB) as b:
                for t in range(NT):
                    u = t % 2
                    m = NT * b + t
                    pool.wait_ge(part_loaded[u], 32 * (2 * b + t // 2 + 1))
                    pool.wait_ge(out_stored[u], DMA_AHEAD + 16 * (2 * b + t // 2))
                    tt(total[u][:], parts[u][:, 0], parts[u][:, 1], ALU.add).then_inc(sums, 1)
                    for g in (2, 3):
                        pool.wait_ge(sums, 3 * m + g - 1)
                        tt(total[u][:], total[u][:], parts[u][:, g], ALU.add).then_inc(sums, 1)


def build(nc, x, wqkv, wb, wo, rms, wf, out):
    with ExitStack() as ctx:
        sb = lambda name, shape: ctx.enter_context(nc.sbuf_tensor(name, shape, F32))
        xT = nc.dram_tensor("xT", (NBLK, P, 2, KT, BLK), F32, kind="Internal").ap()
        part = nc.dram_tensor("part", (2 * STEPS, P, DM), F32, kind="Internal").ap()
        ident = sb("ident", [P, P])
        upper = sb("upper", [P, P])
        upper_diag = sb("upper_diag", [P, P])
        below1 = sb("below1", [P, P // 2])
        above1 = sb("above1", [P, P // 2])
        level_masks = {m: sb(f"mask{m}", [P, P // 2]) for m in LEVELS if m < 32}
        sqrt_beta = sb("sqrt_beta", [P, NG, 2 * NBLK * HG])
        const = {"masks": (ident, upper, upper_diag, below1, above1, level_masks), "ident": ident,
                 "masks_n": 2 + len(level_masks) + 3 + 5 + 2 * len(level_masks)}
        phase_normalise(nc, ctx, x, wb, xT, const, sqrt_beta)
        phase_attention(nc, ctx, wqkv, wo, rms, xT, part, const, sqrt_beta)
        phase_feed_forward(nc, ctx, x, wf, xT, part, out)


def kernel(L0_attn_x, L0_attn_Wq, L0_attn_Wk, L0_attn_Wv, L0_attn_Wb, L0_attn_Wo, L0_attn_conv_q,
           L0_attn_conv_k, L0_attn_conv_v, L0_attn_rms_w, L0_ffn_w_gate, L0_ffn_w_up, L0_ffn_w_down):
    import numpy as np
    import concourse.bacc as bacc
    from concourse.bass_utils import run_bass_kernel_spmd as run

    def a(v):
        return np.asarray(v)

    xs = a(L0_attn_x).reshape(B * S // P, P, DM)
    tiles = []
    for w, cw in ((L0_attn_Wk, L0_attn_conv_k), (L0_attn_Wv, L0_attn_conv_v), (L0_attn_Wq, L0_attn_conv_q)):
        wt = a(w).reshape(NG, 2, 2, P, KT, P).transpose(0, 1, 5, 2, 4, 3).reshape(NG, 2, P, 2, KT * P)
        ct = a(cw).reshape(NG, 2, 2, P, KW).transpose(0, 1, 3, 2, 4)
        tiles.append(np.concatenate([wt, ct], axis=-1))
    wqkv = np.ascontiguousarray(np.stack(tiles, axis=1).reshape(NG, PAIRS, P, 2, KT * P + KW))
    wb = np.ascontiguousarray(a(L0_attn_Wb).reshape(NH, KT, P).transpose(2, 1, 0).reshape(P, KT * NH))
    wo = np.ascontiguousarray(a(L0_attn_Wo).reshape(DM, NG, HG, P).transpose(1, 3, 2, 0))
    rms = np.ascontiguousarray(a(L0_attn_rms_w).reshape(P, 1))
    nj = DH // P
    gu = [a(w).reshape(nj, P, KT, P).transpose(3, 0, 2, 1).reshape(P, nj, DM)
          for w in (L0_ffn_w_gate, L0_ffn_w_up)]
    down = a(L0_ffn_w_down).reshape(DM, nj, P).transpose(2, 1, 0)
    wf = np.ascontiguousarray(np.concatenate([*gu, down], axis=-1))

    nc = bacc.Bacc("TRN2", target_bir_lowering=False, num_devices=1)
    arrays, aps = {}, []
    for name, v in (("x", xs), ("wqkv", wqkv), ("wb", wb), ("wo", wo), ("rms", rms), ("wf", wf)):
        arrays[name] = v
        aps.append(nc.dram_tensor(name, v.shape, mybir.dt.from_np(v.dtype), kind="ExternalInput").ap())
    out = nc.dram_tensor("out", (B * S // P, P, DM), F32, kind="ExternalOutput").ap()
    build(nc, *aps, out)
    r = run(nc, [arrays], core_ids=[0])
    return r.results[0]["out"].reshape(B, S, DM)
```

```python
from contextlib import ExitStack

import concourse.bass as bass
from concourse import mybir

F32 = mybir.dt.float32
F32R = mybir.dt.float32r
ALU = mybir.AluOpType
ACT = mybir.ActivationFunctionType
AX_X = mybir.AxisListType.X

P = 128
B, S, DM = 2, 1024, 512
NH, HD, KW = 16, 128, 4
DH = 2048
KT = DM // P
HG = 4
NG = NH // HG
BLK = 2 * P
NBLK = B * S // BLK
SPG = S // BLK
STEPS = NG * B * SPG
GROUPS = STEPS // SPG
PAIRS = 3 * HG // 2
WPAIR = 2 * (KT * P + KW)
LEVELS = [2, 4, 8, 16, 32, 64]
RESIDUAL = 3 + 2 * len(LEVELS)
HOPS = RESIDUAL + 3
AHEAD, DMA_AHEAD = 1, 16
LN_EPS, RMS_EPS, L2_EPS = 1e-5, 1e-5, 1e-6


def causal_masks(nc, eng, done, ident, upper, upper_diag, below1, above1, level_masks):
    n = 0

    def keep(t, op, base, pattern, mult, fill=0.0):
        nonlocal n
        eng.wait_ge(done, n)
        eng.affine_select(out=t, in_=t, compare_op=op, fill=fill, base=base, pattern=pattern,
                          channel_multiplier=mult).then_inc(done, 1)
        n += 1

    ones = [upper, upper_diag, *level_masks.values()]
    for t in ones:
        eng.memset(t[:], 1.0).then_inc(done, 1)
        n += 1
    for t in (ident, below1, above1):
        eng.memset(t[:], 0.0).then_inc(done, 1)
        n += 1
    keep(ident[:], ALU.not_equal, 0, [[-1, P]], 1, 1.0)
    keep(upper[:], ALU.is_gt, 0, [[1, P]], -1)
    keep(upper_diag[:], ALU.is_ge, 0, [[1, P]], -1)
    keep(below1[:], ALU.not_equal, -1, [[-2, P // 2]], 1, 1.0)
    keep(above1[:], ALU.not_equal, 0, [[-2, P // 2]], 1, 1.0)
    for m, t in level_masks.items():
        v = t[:].rearrange("p (b j) -> p b j", j=m)
        keep(v, ALU.is_ge, -m, [[-2 * m, P // (2 * m)], [0, m]], 1)
        keep(v, ALU.is_ge, 2 * m - 1, [[2 * m, P // (2 * m)], [0, m]], -1)
    return n


def phase_normalise(nc, ctx, x, wb, xT, const, sqrt_beta):
    with ExitStack() as own:
        sb = lambda name, shape, dt=F32: own.enter_context(nc.sbuf_tensor(name, shape, dt))
        sem = lambda name: ctx.enter_context(nc.semaphore(name))
        xt = [sb(f"n_x{u}", [P, DM]) for u in range(2)]
        xn = [sb(f"n_xn{u}", [P, DM]) for u in range(2)]
        stats = [sb(f"n_stats{u}", [P, 6]) for u in range(2)]
        mv = [sb(f"n_mv{u}", [P, 2]) for u in range(2)]
        veps = [sb(f"n_veps{u}", [P, 1]) for u in range(2)]
        rstd = [sb(f"n_rstd{u}", [P, 1]) for u in range(2)]
        hi = [sb(f"n_hi{u}", [P, KT, P], F32R) for u in range(2)]
        lo = [sb(f"n_lo{u}", [P, KT, P], F32R) for u in range(2)]
        beta = [sb(f"n_beta{u}", [P, NH]) for u in range(2)]
        wb_in = sb("n_wb", [P, KT * NH])
        wb_hi = sb("n_wbhi", [P, KT, NH], F32R)
        wb_lo = sb("n_wblo", [P, KT, NH], F32R)
        power = sb("n_power", [P, NH + 1])
        ps_t = [own.enter_context(nc.psum_tensor(f"n_pst{u}", [P, KT, P], F32)) for u in range(2)]
        ps_b = [own.enter_context(nc.psum_tensor(f"n_psb{u}", [P, 512], F32)) for u in range(2)]
        masks_done, powers = sem("n_masks"), sem("n_powers")
        wb_loaded, wb_split = sem("n_wb_loaded"), sem("n_wb_split")
        loaded = [sem(f"n_loaded{u}") for u in range(2)]
        stat_steps, rstd_ready, xn_ready = sem("n_stat_steps"), sem("n_rstd_ready"), sem("n_xn_ready")
        transposed, hi_ready, lo_ready = sem("n_transposed"), sem("n_hi_ready"), sem("n_lo_ready")
        logits, beta_ready, root_ready = sem("n_logits"), sem("n_beta_ready"), sem("n_root_ready")
        stored = [sem(f"n_stored{u}") for u in range(2)]
        block = own.enter_context(nc.Block())

        @block.sync
        def _(sp):
            for u in range(2):
                sp.sem_inc(stored[u], DMA_AHEAD)
            sp.dma_start(wb_in[:], wb).then_inc(wb_loaded, 16)
            for u in range(2):
                sp.dma_start(xt[u][:], x[u]).then_inc(loaded[u], 16)
            with sp.Fori(0, NBLK) as i:
                for u in range(2):
                    sp.wait_ge(lo_ready, AHEAD + 2 * i + u + 1)
                    sp.dma_start(xT[i][:, 0, :, u * P:(u + 1) * P], hi[u][:].bitcast(F32)).then_inc(stored[u], 16)
                    sp.dma_start(xT[i][:, 1, :, u * P:(u + 1) * P], lo[u][:].bitcast(F32)).then_inc(stored[u], 16)
                    sp.dma_start(xt[u][:], x[(2 * i + u + 2) % (2 * NBLK)]).then_inc(loaded[u], 16)
            for u in range(2):
                sp.wait_ge(stored[u], DMA_AHEAD + 32 * NBLK)
                sp.wait_ge(loaded[u], 16 * (NBLK + 1))

        @block.gpsimd
        def _(pool):
            pool.sem_inc(root_ready, AHEAD)
            nc.gpsimd.memset(power[:, 0:1], -0.5).then_inc(powers, 1)
            nc.gpsimd.memset(power[:, 1:], 0.5).then_inc(powers, 1)
            n = causal_masks(nc, pool, masks_done, *const["masks"])
            pool.wait_ge(masks_done, n)
            pool.wait_ge(powers, 2)
            with pool.Fori(0, NBLK) as i:
                for u in range(2):
                    pool.wait_ge(stat_steps, 6 * i + 3 * u + 3)
                    nc.gpsimd.tensor_tensor(rstd[u][:], veps[u][:], power[:, 0:1], ALU.pow)\
                        .then_inc(rstd_ready, 1)
                for u in range(2):
                    pool.wait_ge(beta_ready, AHEAD + 2 * i + u + 1)
                    nc.gpsimd.tensor_tensor(
                        sqrt_beta[:, :, bass.ds(8 * i + 4 * u, 4)],
                        beta[u][:].rearrange("p (g h) -> p g h", h=HG),
                        power[:, 1:].rearrange("p (g h) -> p g h", h=HG), ALU.pow).then_inc(root_ready, 1)

        @block.vector
        def _(dve):
            dve.sem_inc(lo_ready, AHEAD)
            dve.wait_ge(wb_loaded, 16)
            nc.vector.tensor_copy(wb_hi[:].rearrange("p k h -> p (k h)"), wb_in[:]).then_inc(wb_split, 1)
            dve.wait_ge(wb_split, 1)
            nc.vector.tensor_tensor(wb_lo[:].rearrange("p k h -> p (k h)"), wb_in[:],
                                    wb_hi[:].bitcast(F32).rearrange("p k h -> p (k h)"), ALU.subtract)\
                .then_inc(wb_split, 1)
            with dve.Fori(0, NBLK) as i:
                for u in range(2):
                    dve.wait_ge(loaded[u], 16 * i + 16)
                    nc.vector.bn_stats(stats[u][:], xt[u][:]).then_inc(stat_steps, 1)
                    dve.drain()
                    nc.vector.bn_aggr(mv[u][:], stats[u][:]).then_inc(stat_steps, 1)
                    dve.wait_ge(stat_steps, 6 * i + 3 * u + 2)
                    nc.vector.tensor_scalar(veps[u][:], mv[u][:, 1:2], LN_EPS, None, ALU.add)\
                        .then_inc(stat_steps, 1)
                for u in range(2):
                    dve.wait_ge(rstd_ready, 2 * i + u + 1)
                    dve.wait_ge(transposed, AHEAD + 2 * i)
                    nc.vector.tensor_scalar(xn[u][:], xt[u][:], mv[u][:, 0:1], rstd[u][:],
                                            ALU.subtract, ALU.mult).then_inc(xn_ready, 1)
                for u in range(2):
                    dve.wait_ge(hi_ready, 2 * i + u + 1)
                    nc.vector.tensor_tensor(lo[u][:], ps_t[u][:], hi[u][:].bitcast(F32), ALU.subtract)\
                        .then_inc(lo_ready, 1)

        @block.scalar
        def _(act):
            act.sem_inc(beta_ready, AHEAD)
            with act.Fori(0, NBLK) as i:
                for u in range(2):
                    act.wait_ge(transposed, AHEAD + 2 * i + u + 1)
                    act.wait_ge(stored[u], DMA_AHEAD + 32 * i)
                    act.wait_ge(logits, AHEAD + 2 * i)
                    nc.scalar.activation(hi[u][:], ps_t[u][:], ACT.Copy).then_inc(hi_ready, 1)
                for u in range(2):
                    act.wait_ge(logits, AHEAD + 2 * i + u + 1)
                    act.wait_ge(root_ready, AHEAD + 2 * i)
                    nc.scalar.activation(beta[u][:], ps_b[u][:, 0:NH], ACT.Sigmoid).then_inc(beta_ready, 1)

        @block.tensor
        def _(pe):
            pe.sem_inc(transposed, AHEAD)
            pe.sem_inc(logits, AHEAD)
            ident = const["ident"]
            pe.wait_ge(masks_done, const["masks_n"])
            pe.wait_ge(wb_split, 2)
            with pe.Fori(0, NBLK) as i:
                for u in range(2):
                    pe.wait_ge(xn_ready, 2 * i + u + 1)
                    pe.wait_ge(lo_ready, AHEAD + 2 * i)
                    for k in range(KT):
                        last = nc.tensor.transpose(ps_t[u][:, k, :], xn[u][:, k * P:(k + 1) * P], ident[:])
                    last.then_inc(transposed, 1)
                for u in range(2):
                    pe.wait_ge(lo_ready, AHEAD + 2 * i + u + 1)
                    pe.wait_ge(beta_ready, AHEAD + 2 * i)
                    for k in range(KT):
                        for n, (a, w) in enumerate(((hi, wb_hi), (lo, wb_hi), (hi, wb_lo))):
                            last = nc.tensor.matmul(ps_b[u][:, 0:NH], a[u][:, k, :], w[:, k, :],
                                                    start=(k == 0 and n == 0),
                                                    stop=(k == KT - 1 and n == 2))
                    last.then_inc(logits, 1)


def phase_attention(nc, ctx, w, wo, rms, xT, part, const, sqrt_beta):
    with ExitStack() as own:
        sb = lambda name, shape, dt=F32: own.enter_context(nc.sbuf_tensor(name, shape, dt))
        sem = lambda name: ctx.enter_context(nc.semaphore(name))
        bank = lambda name, shape: own.enter_context(nc.psum_tensor(name, shape, F32))

        xb = [sb(f"xb{u}", [P, 2, KT, BLK], F32R) for u in range(2)]
        w_in = sb("w_in", [P, 2, KT * P + KW])
        w_hi = sb("w_hi", [P, PAIRS, 2, KT, P], F32R)
        w_lo = sb("w_lo", [P, PAIRS, 2, KT, P], F32R)
        taps = sb("taps", [P, PAIRS, 2, KW])
        wo_sb = sb("wo_sb", [P, HG, DM])
        rms_sb = sb("rms_sb", [P, 1])
        raw = [sb(f"raw{u}", [P, 2, BLK + KW - 1]) for u in range(2)]
        halo = sb("halo", [P, PAIRS, 2, KW - 1])
        conv = [sb(f"conv{u}", [P, 2, BLK]) for u in range(2)]
        squares = [sb(f"squares{u}", [P, 2, BLK]) for u in range(2)]
        kT = sb("kT", [P, HG, BLK])
        vT = sb("vT", [P, HG, BLK])
        qT = [sb(f"qT{u}", [P, HG, BLK]) for u in range(2)]
        k_sum = sb("k_sum", [P, 2, HG])
        k_rsqrt = sb("k_rsqrt", [P, 2, HG])
        k_scale = sb("k_scale", [P, 2, HG])
        v_scale = sb("v_scale", [P, 2, HG])
        q_term = [sb(f"q_term{u}", [P, 2, HG]) for u in range(4)]
        two = range(2)
        k_nat = [[sb(f"k_nat{u}{x}", [P, HG, P]) for x in two] for u in two]
        k_chn = [[sb(f"k_chn{u}{x}", [P, HG, P]) for x in two] for u in two]
        v_nat = [[sb(f"v_nat{u}{x}", [P, HG, P]) for x in two] for u in two]
        pT = [[sb(f"pT{u}{x}", [P, HG, P]) for x in two] for u in two]
        M = [sb(f"M{x}", [P, HG, P]) for x in two]
        G_hi = [sb(f"G_hi{x}", [P, HG, P], F32R) for x in two]
        T_hi = [sb(f"T_hi{x}", [P, HG, P], F32R) for x in two]
        U_hi = [sb(f"U_hi{x}", [P, HG, P], F32R) for x in two]
        Y = [[sb(f"Y{x}{u}", [P, HG, P], F32R) for u in two] for x in two]
        R = [sb(f"R{x}", [P, HG, P], F32R) for x in two]
        U = [[sb(f"U{u}{x}", [P, HG, P]) for x in two] for u in two]
        ident_hi = sb("ident_hi", [P, P], F32R)
        state = [sb(f"state{u}", [P, HG, P]) for u in two]
        resid = sb("resid", [P, HG, P])
        upd = sb("upd", [P, HG, P])
        o_raw = [sb(f"o_raw{x}", [P, HG, P]) for x in two]
        o_sum = [sb(f"o_sum{x}", [P, HG]) for x in two]
        o_var = [sb(f"o_var{x}", [P, HG]) for x in two]
        o_fac = [sb(f"o_fac{x}", [P, HG]) for x in two]
        o_work = sb("o_work", [P, HG, P])
        o_chn = sb("o_chn", [P, HG, P])
        staged = [sb(f"staged{x}", [P, DM]) for x in two]
        power = sb("a_power", [P, 2 * HG])
        ones = sb("a_ones", [P, 1])
        zero = sb("a_zero", [P, HG])

        ps_a = [bank(f"ps_a{u}", [P, 2, BLK]) for u in two]
        ps_sum = bank("ps_sum", [P, 2, 2, HG])
        ps_inv = [bank(f"ps_inv{x}", [P, 512]) for x in two]
        ps_vp = bank("ps_vp", [P, HG, P])
        ps_s = [bank(f"ps_s{u}", [P, HG, P]) for u in two]

        x_loaded = [sem(f"x_loaded{u}") for u in two]
        w_loaded, w_hi_done, w_lo_done = sem("w_loaded"), sem("w_hi_done"), sem("w_lo_done")
        wo_loaded, rms_loaded = sem("wo_loaded"), sem("rms_loaded")
        stored = [sem(f"a_stored{x}") for x in two]
        consts, zeros, ident_done = sem("a_consts"), sem("a_zeros"), sem("a_ident_done")
        proj_mm, raw_done, conv_steps, silu_done = (sem(n) for n in (
            "proj_mm", "raw_done", "conv_steps", "silu_done"))
        sq_done, ksum_mm, qsum_mm, ksum_read, qsum_read, kpow_done, kscale_ready = (sem(n) for n in (
            "sq_done", "ksum_mm", "qsum_mm", "ksum_read", "qsum_read", "kpow_done", "kscale_ready"))
        inv_mm = [sem(f"inv_mm{x}") for x in two]
        inv_done = [sem(f"inv_done{x}") for x in two]
        base_steps = [sem(f"base_steps{x}") for x in two]
        g_hi_done = [sem(f"g_hi_done{x}") for x in two]
        diag_done = [sem(f"diag_done{x}") for x in two]
        y_clear = [sem(f"y_clear{x}") for x in two]
        i_less_t = [sem(f"i_less_t{x}") for x in two]
        v_mm, v_done, p_mm, p_done = sem("v_mm"), sem("v_done"), sem("p_mm"), sem("p_done")
        ks_mm, resid_done, upd_mm, upd_done, state_mm, state_done, o_mm, o_done = (sem(n) for n in (
            "ks_mm", "resid_done", "upd_mm", "upd_done", "state_mm", "state_done", "o_mm", "o_done"))
        osq_done, osum_steps, ofac_done, onorm_done = (sem(n) for n in (
            "osq_done", "osum_steps", "ofac_done", "onorm_done"))
        turn_mm, turn_done, out_mm, out_done = (sem(n) for n in (
            "turn_mm", "turn_done", "out_mm", "out_done"))
        block = own.enter_context(nc.Block())

        ident, upper, upper_diag, below1, above1, level_masks = const["masks"]
        PROJECT = [22, 0, 6, 7, 0, 0, 7, 20, 7, 0, 14, 15, 14, 0, 14, 18, 0, 0]
        RAW = [3, 8, 11, 12, 15, 16]
        CONV_A, CONV_B = RAW, [4, 9, 12, 13, 16, 17]
        SILU = [5, 10, 13, 14, 17, 17]
        SPLIT_HI, SPLIT_LO = [5, 10, 12, 14, 16], [6, 11, 13, 15, 17]
        CONV_STEPS = 2 * KW
        KINDS = "kkvvqq"

        def dest(j, u):
            t = {"k": kT, "v": vT, "q": qT[u]}[KINDS[j]]
            return t[:, 2 * (j % 2):2 * (j % 2) + 2, :]

        def per_head(t, x):
            return t[:, x, :].unsqueeze(2).broadcast_to([P, HG, P])

        def all_heads(t, n):
            return t[:].unsqueeze(1).broadcast_to([P, HG, n])

        def first_half(t, m):
            return t.rearrange("p h (b k j) -> p h b k j", k=2, j=m)[:, :, :, 0, :]

        def second_half(t, m):
            return t.rearrange("p h (b k j) -> p h b k j", k=2, j=m)[:, :, :, 1, :]

        def packed(t, m):
            return t.rearrange("p (h b j) -> p h b j", h=HG, j=m)

        def run_slots(emit, eng):
            emit(-1, 3, True, False, False, False)
            emit(0, 0, True, True, False, False)
            emit(1, 1, True, True, True, False)
            with eng.Fori(0, GROUPS - 1) as g:
                for c in (2, 3, 4, 5):
                    emit(4 * g + c, c % 4, True, True, True, True)
            emit(STEPS - 2, 2, True, True, True, True)
            emit(STEPS - 1, 3, False, True, True, True)
            emit(STEPS, 0, False, False, True, True)
            emit(STEPS + 1, 1, False, False, False, True)

        def group_of(s, c):
            return (s - c) // SPG

        @block.sync
        def _(sp):
            def load_x(s, c):
                sp.dma_start(xb[c % 2][:].bitcast(F32), xT[(s // 4) % 2 * 4 + c])\
                    .then_inc(x_loaded[c % 2], 16)

            def load_w(grp, j):
                sp.dma_start(w_in[:], w[grp // 2, j]).then_inc(w_loaded, 16)

            sp.dma_start(rms_sb[:], rms).then_inc(rms_loaded, 16)
            load_w(0, 0)
            load_x(0, 0)
            load_x(1, 1)
            sp.dma_start(wo_sb[:], wo[0]).then_inc(wo_loaded, 16)
            for j in range(1, PAIRS):
                sp.wait_ge(w_lo_done, j)
                load_w(0, j)

            def slot(s, c, A, INV, SCAN, POST):
                more = not isinstance(s, int) or s + 3 <= STEPS
                if more and c == 2 and isinstance(s, int) and s + 2 >= STEPS:
                    more = False
                if c == 2 and more and A:
                    for j in range(PAIRS):
                        sp.wait_ge(w_lo_done, PAIRS * ((s + 2) // SPG) + j)
                        load_w((s + 2) // SPG, j)
                if POST:
                    sp.wait_ge(out_done, 2 * (s - 2) + 2)
                    sp.dma_start(part[2 * (s - 2) + 1], staged[1][:]).then_inc(stored[1], 16)
                    if c == 1 and not (isinstance(s, int) and s > STEPS - 1):
                        sp.dma_start(wo_sb[:], wo[(s // SPG) // 2]).then_inc(wo_loaded, 16)
                if A and not (isinstance(s, int) and s + 2 >= STEPS):
                    if not (isinstance(s, int) and s < 0):
                        sp.wait_ge(proj_mm, PAIRS * (s + 1))
                        load_x(s + 2, (c + 2) % 4)
                if SCAN:
                    sp.wait_ge(out_done, 2 * (s - 1) + 1)
                    sp.dma_start(part[2 * (s - 1)], staged[0][:]).then_inc(stored[0], 16)

            run_slots(slot, sp)
            for x in two:
                sp.wait_ge(stored[x], 16 * STEPS)

        @block.tensor
        def _(pe):
            mm = nc.tensor.matmul
            pe.wait_ge(consts, 3)
            pe.wait_ge(ident_done, 1)

            def project(s, c, lo, hi):
                for n in range(lo, hi):
                    j, r = divmod(n, 24)
                    t, r = divmod(r, 12)
                    k, r = divmod(r, 3)
                    u = j % 2
                    if n % 24 == 0:
                        if j == 0:
                            pe.wait_ge(x_loaded[c % 2], 16 * ((s - c % 2) // 2 + 1))
                        pe.wait_ge(w_lo_done, PAIRS * (s // SPG) + j + 1)
                        if not (isinstance(s, int) and s == 0 and j < 2):
                            pe.wait_ge(raw_done, PAIRS * s + j - 1)
                    weights = (w_hi, w_hi, w_lo)[r]
                    last = mm(ps_a[u][:, t, :], weights[:, j, t, k, :], xb[c % 2][:, (0, 1, 0)[r], k, :],
                              start=(k == 0 and r == 0), stop=(k == KT - 1 and r == 2))
                    if n % 24 == 23:
                        last.then_inc(proj_mm, 1)

            def sum_squares(q, s, i, first):
                n = 4 * s + 2 * q + i
                pe.wait_ge(sq_done, n + 1)
                if i == 0 and not first:
                    pe.wait_ge(ksum_read if q else qsum_read, s + 1 if q else s)
                for t in range(2):
                    for x in two:
                        last = mm(ps_sum[:, q, x, 2 * i + t:2 * i + t + 1],
                                  squares[i][:, t, x * P:(x + 1) * P], ones[:], start=True, stop=True)
                last.then_inc(qsum_mm if q else ksum_mm, 1)

            def inverse(s, c, x, hop):
                u = c % 2
                out = ps_inv[x]
                if not (isinstance(s, int) and s == 0 and hop == 0):
                    pe.wait_ge(inv_done[x], HOPS * s + hop)
                if hop == 0:
                    pe.wait_ge(silu_done, PAIRS * s + 2)
                    for h in range(HG):
                        last = nc.tensor.transpose(out[:, h * P:(h + 1) * P],
                                                   kT[:, h, x * P:(x + 1) * P], ident[:])
                elif hop == 1:
                    for h in range(HG):
                        last = nc.tensor.transpose(out[:, h * P:(h + 1) * P], k_nat[u][x][:, h, :], ident[:])
                elif hop == 2:
                    for h in range(HG):
                        last = mm(out[:, h * P:(h + 1) * P], k_chn[u][x][:, h, :], k_chn[u][x][:, h, :],
                                  start=True, stop=True)
                elif hop < RESIDUAL and hop % 2 == 1:
                    i = (hop - 3) // 2
                    if hop == 3:
                        pe.wait_ge(g_hi_done[x], s + 1)
                        pe.wait_ge(diag_done[x], s + 1)
                    for h in range(HG):
                        last = mm(out[:, 64 * h:64 * h + 64], G_hi[x][:, h, :],
                                  first_half(T_hi[x][:], LEVELS[i])[:, h], start=True, stop=True)
                elif hop < RESIDUAL:
                    i = (hop - 3) // 2
                    y = Y[x][i % 2]
                    for h in range(HG):
                        mm(out[:, 64 * h:64 * h + 64], U_hi[x][:, h, :],
                           first_half(y[:], LEVELS[i])[:, h], start=True, stop=True)
                    for h in range(HG):
                        last = mm(out[:, 256 + 64 * h:320 + 64 * h], y[:, h, :],
                                  second_half(U_hi[x][:], LEVELS[i])[:, h], start=True, stop=True)
                elif hop == RESIDUAL:
                    for h in range(HG):
                        last = mm(out[:, h * P:(h + 1) * P], M[x][:, h, :], T_hi[x][:, h, :].bitcast(F32),
                                  start=True, stop=True)
                elif hop == RESIDUAL + 1:
                    for h in range(HG):
                        last = mm(out[:, h * P:(h + 1) * P], R[x][:, h, :], U_hi[x][:, h, :],
                                  start=True, stop=True)
                else:
                    for h in range(HG):
                        mm(out[:, h * P:(h + 1) * P], T_hi[x][:, h, :], ident_hi[:], start=True, stop=False)
                        last = mm(out[:, h * P:(h + 1) * P], R[x][:, h, :], G_hi[x][:, h, :],
                                  start=False, stop=True)
                last.then_inc(inv_mm[x], 1)

            def values(s, c, x):
                if x == 0:
                    pe.wait_ge(silu_done, PAIRS * s + 4)
                if x == 1 or not (isinstance(s, int) and s == 0):
                    if x:
                        pe.wait_ge(v_done, 2 * s + 1)
                    else:
                        pe.wait_ge(p_done, 2 * s)
                for h in range(HG):
                    last = nc.tensor.transpose(ps_vp[:, h, :], vT[:, h, x * P:(x + 1) * P], ident[:])
                last.then_inc(v_mm, 1)

            def scores(s, c, x):
                u = c % 2
                if x == 0:
                    pe.wait_ge(silu_done, PAIRS * s + 6)
                    pe.wait_ge(v_done, 2 * s + 2)
                else:
                    pe.wait_ge(p_done, 2 * s + 1)
                pe.wait_ge(inv_done[x], HOPS * s + 2)
                for h in range(HG):
                    last = mm(ps_vp[:, h, :], k_chn[u][x][:, h, :], qT[u][:, h, x * P:(x + 1) * P],
                              start=True, stop=True)
                last.then_inc(p_mm, 1)

            def scan_ks(r, c, x):
                u, n = c % 2, 2 * r + x
                if x == 0:
                    for y in two:
                        pe.wait_ge(inv_done[y], HOPS * (r + 1))
                pe.wait_ge(state_done, n + 1)
                if not (isinstance(r, int) and r == 0 and x == 0):
                    if x == 0:
                        pe.wait_ge(turn_done, 2 * r - 1)
                for h in range(HG):
                    last = mm(ps_s[0][:, h, :], k_chn[u][x][:, h, :], state[x][:, h, :], start=True, stop=True)
                last.then_inc(ks_mm, 1)

            def scan_upd(r, c, x):
                u, n = c % 2, 2 * r + x
                pe.wait_ge(resid_done, n + 1)
                if x == 0:
                    if not (isinstance(r, int) and r == 0):
                        pe.wait_ge(out_done, 2 * r - 1)
                else:
                    if isinstance(r, int) and r == 0:
                        pe.wait_ge(o_done, n)
                    else:
                        pe.wait_ge(out_done, 2 * r)
                for h in range(HG):
                    last = mm(ps_s[1][:, h, :], U[u][x][:, h, :], resid[:, h, :], start=True, stop=True)
                last.then_inc(upd_mm, 1)

            def scan_state_out(r, c, x):
                u, n = c % 2, 2 * r + x
                pe.wait_ge(upd_done, n + 1)
                if x == 0 and not (isinstance(r, int) and r == 0):
                    pe.wait_ge(turn_done, 2 * r)
                for h in range(HG):
                    last = mm(ps_s[0][:, h, :], k_nat[u][x][:, h, :], upd[:, h, :], start=True, stop=True)
                last.then_inc(state_mm, 1)
                if x == 0:
                    pe.wait_ge(p_done, 2 * r + 2)
                for h in range(HG):
                    mm(ps_s[1][:, h, :], qT[u][:, h, x * P:(x + 1) * P], state[x][:, h, :],
                       start=True, stop=False)
                    last = mm(ps_s[1][:, h, :], pT[u][x][:, h, :], upd[:, h, :], start=False, stop=True)
                last.then_inc(o_mm, 1)

            def turn(r, c, x, next_scan):
                n = 2 * r + x
                pe.wait_ge(onorm_done, n + 1)
                if x == 0:
                    pe.wait_ge(state_done, n + 3)
                elif next_scan:
                    pe.wait_ge(resid_done, n + 2)
                else:
                    pe.wait_ge(turn_done, n)
                for h in range(HG):
                    last = nc.tensor.transpose(ps_s[0][:, h, :], o_work[:, h, :], ident[:])
                last.then_inc(turn_mm, 1)

            def project_out(r, c, x, next_scan):
                n = 2 * r + x
                pe.wait_ge(turn_done, n + 1)
                pe.wait_ge(wo_loaded, 16 * (r // SPG + 1))
                if x == 0:
                    pe.wait_ge(o_done, n + 2)
                elif next_scan:
                    pe.wait_ge(o_done, n + 2)
                else:
                    pe.wait_ge(out_done, n)
                for h in range(HG):
                    last = mm(ps_s[1][:].rearrange("p h d -> p (h d)"), o_chn[:, h, :], wo_sb[:, h, :],
                              start=(h == 0), stop=(h == HG - 1))
                last.then_inc(out_mm, 1)

            def slot(s, c, A, INV, SCAN, POST):
                for hop in range(HOPS):
                    if INV:
                        for x in two:
                            inverse(s, c, x, hop)
                    r, rc = s - 1, (c - 1) % 4
                    if SCAN and hop == 1:
                        scan_ks(r, rc, 0)
                    if INV and hop in (1, 2):
                        values(s, c, hop - 1)
                    if INV and hop == 2:
                        for i in range(2):
                            sum_squares(1, s, i, False)
                    if POST and hop == 2:
                        turn(s - 2, (c - 2) % 4, 1, SCAN)
                    if SCAN and hop == 3:
                        scan_upd(r, rc, 0)
                    if INV and hop in (3, 4):
                        scores(s, c, hop - 3)
                    if SCAN and hop == 4:
                        scan_state_out(r, rc, 0)
                    if POST and hop == 5:
                        project_out(s - 2, (c - 2) % 4, 1, SCAN)
                    if SCAN and hop == 6:
                        scan_ks(r, rc, 1)
                    if SCAN and hop == 8:
                        scan_upd(r, rc, 1)
                    if SCAN and hop == 9:
                        scan_state_out(r, rc, 1)
                    if SCAN and hop == 11:
                        turn(r, rc, 0, True)
                    if SCAN and hop == 13:
                        project_out(r, rc, 0, True)
                    if A:
                        project(s + 1, (c + 1) % 4, sum(PROJECT[:hop]), sum(PROJECT[:hop + 1]))
                    if A and hop in (7, 12):
                        sum_squares(0, s + 1, (hop - 7) // 5, isinstance(s, int) and s == -1)

            run_slots(slot, pe)

        @block.scalar
        def _(act):
            act.wait_ge(rms_loaded, 16)

            def split_w(grp, j):
                act.wait_ge(w_loaded, 16 * (PAIRS * grp + j + 1))
                if not (isinstance(grp, int) and grp == 0):
                    act.wait_ge(proj_mm, PAIRS * (SPG * grp - 1) + j + 1)
                nc.scalar.activation(w_hi[:, j].rearrange("p t k c -> p t (k c)"), w_in[:, :, 0:KT * P],
                                     ACT.Copy).then_inc(w_hi_done, 1)

            def copy_raw(s, c, j):
                act.wait_ge(proj_mm, PAIRS * s + j + 1)
                if not (isinstance(s, int) and s == 0 and j < 2):
                    act.wait_ge(conv_steps, CONV_STEPS * (PAIRS * s + j - 1))
                    act.wait_ge(silu_done, PAIRS * s + j - 1)
                act.wait_ge(w_lo_done, PAIRS * (s // SPG) + j + 1)
                for t in range(2):
                    nc.scalar.activation(conv[j % 2][:, t, :], ps_a[j % 2][:, t, :], ACT.Copy,
                                         scale=taps[:, j, t, KW - 1:])
                nc.scalar.activation(raw[j % 2][:, :, KW - 1:], ps_a[j % 2][:], ACT.Copy)\
                    .then_inc(raw_done, 1)

            def silu(s, c, j):
                act.wait_ge(conv_steps, CONV_STEPS * (PAIRS * s + j + 1) - 1)
                if not (isinstance(s, int) and s == 0):
                    if KINDS[j] == "k":
                        for x in two:
                            act.wait_ge(inv_mm[x], HOPS * (s - 1) + 1)
                        act.wait_ge(sq_done, 4 * (s - 1) + 2)
                    elif KINDS[j] == "v":
                        act.wait_ge(v_mm, 2 * (s - 1) + 2)
                    elif not (isinstance(s, int) and s < 2):
                        act.wait_ge(o_mm, 2 * (s - 2) + 2)
                nc.scalar.activation(dest(j, c % 2), conv[j % 2][:], ACT.Silu).then_inc(silu_done, 1)

            def inverse(s, c, x, hop):
                u = c % 2
                out = ps_inv[x]
                act.wait_ge(inv_mm[x], HOPS * s + hop + 1)
                if hop == 1:
                    if not (isinstance(s, int) and s < 2):
                        act.wait_ge(ks_mm, 2 * (s - 2) + x + 1)
                    last = nc.scalar.activation(k_chn[u][x][:].rearrange("p h t -> p (h t)"), out[:], ACT.Copy)
                elif hop == 2:
                    act.wait_ge(base_steps[x], 3 * s + 3)
                    nc.scalar.activation(G_hi[x][:].rearrange("p h t -> p (h t)"), out[:], ACT.Copy)\
                        .then_inc(g_hi_done[x], 1)
                    return
                elif hop == HOPS - 1:
                    last = nc.scalar.activation(U[u][x][:].rearrange("p h t -> p (h t)"), out[:], ACT.Copy)
                else:
                    i = (hop - 3) // 2
                    m, y = LEVELS[i], Y[x][i % 2]
                    ps = [out[:, k:k + 256].rearrange("p (h b j) -> p h b j", h=HG, j=m) for k in (0, 256)]
                    if hop % 2 == 1:
                        act.wait_ge(y_clear[x], len(LEVELS) * s + i + 1)
                    for b in range(P // (2 * m)):
                        first = slice(2 * m * b, 2 * m * b + m)
                        second = slice(2 * m * b + m, 2 * m * (b + 1))
                        if hop % 2 == 1:
                            last = nc.scalar.activation(y[second, :, first], ps[0][second, :, b, :], ACT.Copy)
                        else:
                            nc.scalar.activation(T_hi[x][second, :, first], ps[0][second, :, b, :],
                                                 ACT.Copy, scale=-1.0)
                            last = nc.scalar.activation(U_hi[x][first, :, second], ps[1][first, :, b, :],
                                                        ACT.Copy, scale=-1.0)
                last.then_inc(inv_done[x], 1)

            def copy_upd(r, x):
                n = 2 * r + x
                act.wait_ge(upd_mm, n + 1)
                if not (isinstance(r, int) and n == 0):
                    act.wait_ge(o_mm, n)
                nc.scalar.activation(upd[:], ps_s[1][:], ACT.Copy).then_inc(upd_done, 1)

            def copy_o(r, x):
                n = 2 * r + x
                act.wait_ge(o_mm, n + 1)
                if not (isinstance(r, int) and r == 0):
                    act.wait_ge(onorm_done, n - 1)
                nc.scalar.activation(o_raw[x][:], ps_s[1][:], ACT.Copy).then_inc(o_done, 1)

            def copy_turned(r, x):
                n = 2 * r + x
                act.wait_ge(turn_mm, n + 1)
                if not (isinstance(r, int) and n == 0):
                    act.wait_ge(out_mm, n)
                nc.scalar.activation(o_chn[:], ps_s[0][:], ACT.Copy, scale=rms_sb[:]).then_inc(turn_done, 1)

            def copy_out(r, x):
                n = 2 * r + x
                act.wait_ge(out_mm, n + 1)
                if not (isinstance(r, int) and r == 0):
                    act.wait_ge(stored[x], 16 * r)
                nc.scalar.activation(staged[x][:], ps_s[1][:].rearrange("p h d -> p (h d)"), ACT.Copy)\
                    .then_inc(out_done, 1)

            for j in range(PAIRS):
                split_w(0, j)

            def slot(s, c, A, INV, SCAN, POST):
                for hop in range(HOPS):
                    if INV and hop in (1, 2, 11, 12, 13, 14, HOPS - 1):
                        for x in two:
                            inverse(s, c, x, hop)
                    r = s - 1
                    if POST and hop == 2:
                        copy_turned(s - 2, 1)
                    if SCAN and hop == 3:
                        copy_upd(r, 0)
                    if SCAN and hop == 4:
                        copy_o(r, 0)
                    if POST and hop == 5:
                        copy_out(s - 2, 1)
                    if SCAN and hop == 8:
                        copy_upd(r, 1)
                    if SCAN and hop == 9:
                        copy_o(r, 1)
                    if SCAN and hop == 11:
                        copy_turned(r, 0)
                    if SCAN and hop == 13:
                        copy_out(r, 0)
                    for j in range(PAIRS):
                        if A and hop == RAW[j]:
                            copy_raw(s + 1, (c + 1) % 4, j)
                        if A and hop == SILU[j]:
                            silu(s + 1, (c + 1) % 4, j)
                    if c == 2 and A and hop in SPLIT_HI and not (isinstance(s, int) and s + 2 >= STEPS):
                        split_w((s + 2) // SPG, SPLIT_HI.index(hop))
                    if c == 3 and hop == 1 and A and not (isinstance(s, int) and s < 0):
                        split_w((s + 1) // SPG, 5)

            run_slots(slot, act)

        @block.gpsimd
        def _(pool):
            nc.gpsimd.memset(power[:], -0.5).then_inc(consts, 1)
            nc.gpsimd.memset(ones[:], 1.0).then_inc(consts, 1)
            nc.gpsimd.memset(zero[:], 0.0).then_inc(consts, 1)
            for x in two:
                for u in two:
                    nc.gpsimd.memset(Y[x][u][:].bitcast(F32), 0.0).then_inc(y_clear[x], 1)
            nc.gpsimd.memset(state[0][:], 0.0).then_inc(zeros, 1)
            nc.gpsimd.memset(halo[:], 0.0).then_inc(zeros, 1)
            pool.wait_ge(consts, 3)

            def clear_y(s, x, i):
                m = LEVELS[(i + 2) % len(LEVELS)]
                none = zero[:].unsqueeze(2).unsqueeze(3).broadcast_to([P, HG, P // (2 * m), m])
                pool.wait_ge(inv_mm[x], HOPS * s + 5 + 2 * i)
                nc.gpsimd.tensor_tensor(second_half(Y[x][i % 2][:], m), none, none, ALU.add)\
                    .then_inc(y_clear[x], 1)

            def ident_less_t(s, c, x):
                pool.wait_ge(inv_done[x], HOPS * s + RESIDUAL)
                if not (isinstance(s, int) and s < 2):
                    pool.wait_ge(upd_mm, 2 * (s - 2) + x + 1)
                nc.gpsimd.tensor_tensor(U[c % 2][x][:], all_heads(ident, P), T_hi[x][:].bitcast(F32),
                                        ALU.subtract).then_inc(i_less_t[x], 1)

            def diagonals(s, x):
                if not (isinstance(s, int) and s == 0):
                    pool.wait_ge(inv_mm[x], HOPS * s)
                for k, t in ((1, T_hi[x]), (0, U_hi[x])):
                    column = ident[:].rearrange("p (c k) -> p c k", k=2)[:, :, k]
                    last = nc.gpsimd.tensor_tensor(t[:].rearrange("p h (c k) -> p h c k", k=2)[:, :, :, k],
                                                   column.unsqueeze(1).broadcast_to([P, HG, P // 2]),
                                                   zero[:].unsqueeze(2).broadcast_to([P, HG, P // 2]), ALU.add)
                last.then_inc(diag_done[x], 1)

            def square(s, c, i):
                j = (0, 1, 4, 5)[i]
                n = 4 * s + i
                pool.wait_ge(silu_done, PAIRS * s + j + 1)
                if i < 2:
                    if not (isinstance(s, int) and s == 0):
                        pool.wait_ge(qsum_mm, 2 * (s - 1) + i + 1)
                else:
                    pool.wait_ge(ksum_mm, 2 * s + i - 1)
                src = dest(j, c % 2)
                nc.gpsimd.tensor_tensor(squares[i % 2][:], src, src, ALU.mult).then_inc(sq_done, 1)

            def norm_o(r, c, x):
                n = 2 * r + x
                pool.wait_ge(osum_steps, 2 * n + 2)
                nc.gpsimd.tensor_tensor(o_fac[x][:], o_var[x][:], power[:, 0:HG], ALU.pow)\
                    .then_inc(ofac_done, 1)
                pool.wait_ge(ofac_done, n + 1)
                if not (isinstance(r, int) and n == 0):
                    pool.wait_ge(turn_mm, n)
                nc.gpsimd.tensor_tensor(o_work[:], o_raw[x][:],
                                        o_fac[x][:].unsqueeze(2).broadcast_to([P, HG, P]), ALU.mult)\
                    .then_inc(onorm_done, 1)

            def square_o(r, x):
                n = 2 * r + x
                pool.wait_ge(o_done, n + 1)
                if not (isinstance(r, int) and n == 0):
                    pool.wait_ge(turn_mm, n)
                nc.gpsimd.tensor_tensor(o_work[:], o_raw[x][:], o_raw[x][:], ALU.mult).then_inc(osq_done, 1)

            def slot(s, c, A, INV, SCAN, POST):
                for hop in range(HOPS):
                    r = s - 1
                    if INV and hop == 0:
                        for x in two:
                            diagonals(s, x)
                    if INV and hop >= 4 and hop % 2 == 0 and hop < RESIDUAL:
                        for x in two:
                            clear_y(s, x, (hop - 4) // 2)
                    if INV and hop == RESIDUAL:
                        for x in two:
                            ident_less_t(s, c, x)
                    if POST and hop == 1:
                        norm_o(s - 2, (c - 2) % 4, 1)
                    if SCAN and hop == 5:
                        square_o(r, 0)
                    if SCAN and hop == 7:
                        norm_o(r, (c - 1) % 4, 0)
                    if A and hop in (6, 11):
                        square(s + 1, (c + 1) % 4, (hop - 6) // 5)
                    if A and hop == 14:
                        pool.wait_ge(ksum_read, s + 2)
                        if not (isinstance(s, int) and s < 0):
                            pool.wait_ge(kscale_ready, 2 * (s + 1))
                        nc.gpsimd.tensor_tensor(k_rsqrt[:].rearrange("p x h -> p (x h)"),
                                                k_sum[:].rearrange("p x h -> p (x h)"), power[:],
                                                ALU.pow).then_inc(kpow_done, 1)
                    if SCAN and hop == 13:
                        square_o(r, 1)
                    if A and hop == 17:
                        for i in (2, 3):
                            square(s + 1, (c + 1) % 4, i)

            run_slots(slot, pool)

        @block.vector
        def _(dve):
            tt = nc.vector.tensor_tensor
            dve.wait_ge(zeros, 2)
            nc.vector.tensor_copy(ident_hi[:], ident[:]).then_inc(ident_done, 1)

            nc.vector.tensor_copy(state[0][:], state[0][:]).then_inc(state_done, 1)

            def split_w(grp, j):
                dve.wait_ge(w_hi_done, PAIRS * grp + j + 1)
                if not (isinstance(grp, int) and grp == 0):
                    dve.wait_ge(proj_mm, PAIRS * (SPG * grp - 1) + j + 1)
                    dve.wait_ge(conv_steps, CONV_STEPS * (PAIRS * (SPG * grp - 1) + j + 1))
                nc.vector.tensor_copy(taps[:, j], w_in[:, :, KT * P:])
                tt(w_lo[:, j].rearrange("p t k c -> p t (k c)"), w_in[:, :, 0:KT * P],
                   w_hi[:, j].bitcast(F32).rearrange("p t k c -> p t (k c)"), ALU.subtract).then_inc(w_lo_done, 1)

            def convolve(s, c, j, half):
                u = j % 2
                n = CONV_STEPS * (PAIRS * s + j)
                if half == 0:
                    dve.wait_ge(raw_done, PAIRS * s + j + 1)
                    if c == 0:
                        nc.vector.memset(raw[u][:, :, 0:KW - 1], 0.0).then_inc(conv_steps, 1)
                    else:
                        nc.vector.tensor_copy(raw[u][:, :, 0:KW - 1], halo[:, j]).then_inc(conv_steps, 1)
                    dve.wait_ge(w_lo_done, PAIRS * (s // SPG) + j + 1)
                    dve.wait_ge(conv_steps, n + 1)
                for k in range(3 * half, 3 * half + 3):
                    i, t = divmod(k, 2)
                    if i:
                        dve.wait_ge(conv_steps, n + k)
                    nc.vector.scalar_tensor_tensor(
                        conv[u][:, t, :], raw[u][:, t, i:i + BLK], taps[:, j, t, i:i + 1],
                        conv[u][:, t, :], ALU.mult, ALU.add).then_inc(conv_steps, 1)
                if half == 1:
                    nc.vector.tensor_copy(halo[:, j], raw[u][:, :, BLK:]).then_inc(conv_steps, 1)

            def inverse(s, c, x, hop):
                u = c % 2
                out = ps_inv[x]
                dve.wait_ge(inv_mm[x], HOPS * s + hop + 1)
                if hop == 0:
                    dve.wait_ge(kscale_ready, 2 * (s + 1))
                    if not (isinstance(s, int) and s < 2):
                        dve.wait_ge(state_mm, 2 * (s - 2) + x + 1)
                    tt(k_nat[u][x][:], out[:].rearrange("p (h d) -> p h d", h=HG), per_head(k_scale, x),
                       ALU.mult).then_inc(inv_done[x], 1)
                elif hop == 2:
                    n = 3 * s
                    ps = out[:].rearrange("p (h t) -> p h t", h=HG)
                    below, above = (R[x][:].rearrange("p h (k c) -> p h k c", k=2)[:, :, k]
                                    for k in two)
                    for k, (part_k, mask) in enumerate(((below, below1), (above, above1))):
                        tt(part_k, ps.rearrange("p h (c k) -> p h c k", k=2)[:, :, :, k],
                           all_heads(mask, P // 2), ALU.mult).then_inc(base_steps[x], 1)
                    tt(M[x][:], ps, all_heads(upper, P), ALU.mult).then_inc(base_steps[x], 1)
                    idn = ident[:].rearrange("p (c k) -> p c k", k=2)
                    for k, (part_k, t) in enumerate(((below, T_hi[x]), (above, U_hi[x]))):
                        dve.wait_ge(base_steps[x], n + 1 + k)
                        last = tt(t[:].rearrange("p h (c k) -> p h c k", k=2)[:, :, :, k],
                                  idn[:, :, k].unsqueeze(1).broadcast_to([P, HG, P // 2]),
                                  part_k.bitcast(F32), ALU.subtract)
                    last.then_inc(inv_done[x], 1)
                elif hop == RESIDUAL:
                    dve.wait_ge(i_less_t[x], s + 1)
                    tt(R[x][:].rearrange("p h t -> p (h t)"), U[u][x][:].rearrange("p h t -> p (h t)"), out[:],
                       ALU.subtract).then_inc(inv_done[x], 1)
                elif hop == RESIDUAL + 1:
                    tt(G_hi[x][:].rearrange("p h t -> p (h t)"),
                       U_hi[x][:].bitcast(F32).rearrange("p h t -> p (h t)"), out[:], ALU.add)\
                        .then_inc(inv_done[x], 1)
                elif hop % 2 == 1:
                    i = (hop - 3) // 2
                    m = LEVELS[i]
                    mask = level_masks[m][:].rearrange("p (b j) -> p b j", j=m)\
                        .unsqueeze(1).broadcast_to([P, HG, P // (2 * m), m])
                    dve.wait_ge(y_clear[x], len(LEVELS) * s + i + 1)
                    tt(first_half(Y[x][i % 2][:], m), packed(out[:, 0:256], m), mask, ALU.mult)\
                        .then_inc(inv_done[x], 1)
                else:
                    m = LEVELS[(hop - 3) // 2]
                    T, U2 = first_half(T_hi[x][:], m), second_half(U_hi[x][:], m)
                    tt(T, T.bitcast(F32), packed(out[:, 0:256], m), ALU.subtract)
                    tt(U2, U2.bitcast(F32), packed(out[:, 256:512], m), ALU.subtract).then_inc(inv_done[x], 1)

            def values(s, c, x):
                u = c % 2
                dve.wait_ge(v_mm, 2 * s + x + 1)
                tt(v_nat[u][x][:], ps_vp[:], per_head(v_scale, x), ALU.mult).then_inc(v_done, 1)

            def scores(s, c, x):
                u = c % 2
                dve.wait_ge(p_mm, 2 * s + x + 1)
                if not (isinstance(s, int) and s < 2):
                    dve.wait_ge(o_mm, 2 * (s - 2) + x + 1)
                tt(pT[u][x][:], ps_vp[:], all_heads(upper_diag, P), ALU.mult).then_inc(p_done, 1)

            def residual(r, c, x):
                n = 2 * r + x
                dve.wait_ge(ks_mm, n + 1)
                if not (isinstance(r, int) and n == 0):
                    dve.wait_ge(upd_mm, n)
                dve.wait_ge(v_done, n + 1)
                tt(resid[:], v_nat[c % 2][x][:], ps_s[0][:], ALU.subtract).then_inc(resid_done, 1)

            def new_state(r, c, x):
                n = 2 * r + x
                dve.wait_ge(state_mm, n + 1)
                if c == SPG - 1 and x == 1:
                    dve.wait_ge(o_mm, n)
                    nc.vector.memset(state[0][:], 0.0).then_inc(state_done, 1)
                    return
                if not (isinstance(r, int) and n == 0):
                    dve.wait_ge(o_mm, n)
                dve.wait_ge(state_done, n + 1)
                tt(state[1 - x][:], state[x][:], ps_s[0][:], ALU.add).then_inc(state_done, 1)

            def sum_o(r, c, x):
                n = 2 * r + x
                dve.wait_ge(osq_done, n + 1)
                nc.vector.reduce_sum(o_sum[x][:], o_work[:], AX_X).then_inc(osum_steps, 1)
                dve.wait_ge(osum_steps, 2 * n + 1)
                dve.wait_ge(qsum_read, r + 1)
                if not (isinstance(r, int) and r == 0):
                    dve.wait_ge(ofac_done, n - 1)
                nc.vector.scalar_tensor_tensor(o_var[x][:], o_sum[x][:], 1.0 / HD, q_term[c][:, x, :],
                                               ALU.mult, ALU.add).then_inc(osum_steps, 1)

            for j in range(PAIRS):
                split_w(0, j)

            def slot(s, c, A, INV, SCAN, POST):
                for hop in range(HOPS):
                    r, rc = s - 1, (c - 1) % 4
                    if INV and (hop in (0, RESIDUAL, RESIDUAL + 1) or 2 <= hop <= 10):
                        for x in two:
                            inverse(s, c, x, hop)
                    if SCAN and hop == 1:
                        residual(r, rc, 0)
                    if INV and hop in (1, 2):
                        values(s, c, hop - 1)
                    if INV and hop == 3:
                        dve.wait_ge(qsum_mm, 2 * s + 2)
                        nc.vector.tensor_scalar(q_term[c][:], ps_sum[:, 1], L2_EPS, HD * RMS_EPS,
                                                ALU.add, ALU.mult).then_inc(qsum_read, 1)
                    if INV and hop in (3, 4):
                        scores(s, c, hop - 3)
                    if SCAN and hop == 4:
                        new_state(r, rc, 0)
                    if SCAN and hop == 6:
                        residual(r, rc, 1)
                        sum_o(r, rc, 0)
                    if SCAN and hop == 9:
                        new_state(r, rc, 1)
                    if SCAN and hop == 14:
                        sum_o(r, rc, 1)
                    for half, hops in ((1, CONV_B), (0, CONV_A)):
                        if A and hop in hops:
                            convolve(s + 1, (c + 1) % 4, hops.index(hop), half)
                    if A and hop == 13:
                        dve.wait_ge(ksum_mm, 2 * (s + 1) + 2)
                        if not (isinstance(s, int) and s < 0):
                            dve.wait_ge(kpow_done, s + 1)
                        nc.vector.tensor_scalar(k_sum[:], ps_sum[:, 0], L2_EPS, None, ALU.add)\
                            .then_inc(ksum_read, 1)
                    if A and hop == 15:
                        dve.wait_ge(kpow_done, s + 2)
                        root = sqrt_beta[:].rearrange("p g t -> p (g t)")[:, bass.ds(8 * (s + 1), 8)]
                        tt(k_scale[:].rearrange("p x h -> p (x h)"),
                           k_rsqrt[:].rearrange("p x h -> p (x h)"), root, ALU.mult)\
                            .then_inc(kscale_ready, 1)
                        nc.vector.tensor_copy(v_scale[:].rearrange("p x h -> p (x h)"), root)\
                            .then_inc(kscale_ready, 1)
                    if c == 2 and A and hop in SPLIT_LO and not (isinstance(s, int) and s + 2 >= STEPS):
                        split_w((s + 2) // SPG, SPLIT_LO.index(hop))
                    if c == 3 and hop == 2 and A and not (isinstance(s, int) and s < 0):
                        split_w((s + 1) // SPG, 5)

            run_slots(slot, dve)


def phase_feed_forward(nc, ctx, x, wf, xT, part, out):
    TB = 512
    NJ = DH // P
    NT = TB // P
    NB = B * S // TB
    TILES_AHEAD, BLOCK_AHEAD = 2, 2 * NT
    with ExitStack() as own:
        sb = lambda name, shape, dt=F32: own.enter_context(nc.sbuf_tensor(name, shape, dt))
        sem = lambda name: ctx.enter_context(nc.semaphore(name))
        bank = lambda name, shape: own.enter_context(nc.psum_tensor(name, shape, F32))
        two = range(2)
        wf_sb = sb("wf_sb", [P, NJ, 3 * DM])
        gu_hi = [sb(f"f_guhi{u}", [P, 2 * DM], F32R) for u in two]
        gu_lo = [sb(f"f_gulo{u}", [P, 2 * DM], F32R) for u in two]
        dn_hi = [sb(f"f_dnhi{u}", [P, DM], F32R) for u in two]
        dn_lo = [sb(f"f_dnlo{u}", [P, DM], F32R) for u in two]
        xb = [sb(f"f_x{u}", [P, 2, 2, KT, BLK], F32R) for u in two]
        act_g = [sb(f"f_g{u}", [P, TB]) for u in two]
        hid = [sb(f"f_hid{u}", [P, TB]) for u in two]
        h_hi = [sb(f"f_hhi{u}", [P, TB], F32R) for u in two]
        h_lo = [sb(f"f_hlo{u}", [P, TB], F32R) for u in two]
        parts = [sb(f"f_part{u}", [P, NG, DM]) for u in two]
        x_res = [sb(f"f_xres{u}", [P, DM]) for u in two]
        gate = [sb(f"f_gate{t}", [P, DM]) for t in range(NT)]
        total = [sb(f"f_total{u}", [P, DM]) for u in two]
        ps_g = [bank(f"f_psg{u}", [P, TB]) for u in two]
        ps_u = [bank(f"f_psu{u}", [P, TB]) for u in two]
        ps_o = [bank(f"f_pso{t}", [P, DM]) for t in range(NT)]
        wf_loaded = [sem(f"f_wf_loaded{j}") for j in range(NJ)]
        x_loaded = [sem(f"f_x_loaded{u}") for u in two]
        part_loaded = [sem(f"f_part_loaded{u}") for u in two]
        gu_hi_done, gu_lo_done, dn_hi_done, dn_lo_done = (sem(n) for n in (
            "f_gu_hi_done", "f_gu_lo_done", "f_dn_hi_done", "f_dn_lo_done"))
        g_mm, u_mm, g_done, hid_done, hhi_done, hlo_done, down_mm = (sem(n) for n in (
            "f_g_mm", "f_u_mm", "f_g_done", "f_hid_done", "f_hhi_done", "f_hlo_done", "f_down_mm"))
        gate_done, sums, res_done = sem("f_gate_done"), sem("f_sums"), sem("f_res_done")
        out_stored = [sem(f"f_out_stored{u}") for u in two]
        block = own.enter_context(nc.Block())

        @block.sync
        def _(sp):
            for u in two:
                sp.sem_inc(out_stored[u], DMA_AHEAD)

            def load_x(b, u):
                for i in range(2):
                    sp.dma_start(xb[u][:, i].bitcast(F32), xT[2 * b + i]).then_inc(x_loaded[u], 16)

            def load_parts(m, u):
                sp.dma_start(parts[u][:], part.rearrange("(g q) p d -> q p g d", g=NG)[m])\
                    .then_inc(part_loaded[u], 16)
                sp.dma_start(x_res[u][:], x[m]).then_inc(part_loaded[u], 16)

            sp.dma_start(wf_sb[:, 0], wf[:, 0]).then_inc(wf_loaded[0], 16)
            load_x(0, 0)
            for j in range(1, NJ):
                sp.dma_start(wf_sb[:, j], wf[:, j]).then_inc(wf_loaded[j], 16)
            load_x(1, 1)
            with sp.Fori(0, NB // 2) as p:
                for u in two:
                    b = 2 * p + u
                    for t in two:
                        load_parts(NT * b + t, t)
                    sp.wait_ge(u_mm, TILES_AHEAD + NJ * (b + 1))
                    load_x((b + 2) % NB, u)
                    for t in range(NT):
                        m = NT * b + t
                        sp.wait_ge(res_done, BLOCK_AHEAD + 2 * m + 2)
                        sp.dma_start(out[m], total[t % 2][:]).then_inc(out_stored[t % 2], 16)
                        if t < 2:
                            load_parts(m + 2, t)
            for u in two:
                sp.wait_ge(out_stored[u], DMA_AHEAD + 16 * NB * NT // 2)
                sp.wait_ge(x_loaded[u], 32 * (NB // 2 + 1))

        @block.tensor
        def _(pe):
            pe.sem_inc(down_mm, TILES_AHEAD)
            pe.sem_inc(u_mm, TILES_AHEAD)

            def gate_up(p, jj):
                u, n, x_u = jj % 2, 2 * NJ * p + jj, jj // NJ
                if jj % NJ == 0:
                    pe.wait_ge(x_loaded[x_u], 32 * (p + 1))
                pe.wait_ge(gu_lo_done, n + 1)
                pe.wait_ge(hid_done, TILES_AHEAD + n - 1)
                for i, ps in enumerate((ps_g[u], ps_u[u])):
                    for k in range(KT):
                        for r in range(3):
                            w = (gu_hi, gu_hi, gu_lo)[r][u]
                            last = nc.tensor.matmul(
                                ps[:].rearrange("p (b t) -> p b t", b=2),
                                w[:, i * DM + k * P:i * DM + (k + 1) * P],
                                xb[x_u][:, :, (0, 1, 0)[r], k, :],
                                start=(k == 0 and r == 0), stop=(k == KT - 1 and r == 2))
                    last.then_inc(u_mm if i else g_mm, 1)

            def down(p, jj):
                u, j, n = jj % 2, jj % NJ, 2 * NJ * p + jj
                pe.wait_ge(dn_lo_done, n + 1)
                pe.wait_ge(hlo_done, n + 1)
                if j == 0:
                    pe.wait_ge(gate_done, AHEAD + NT * (2 * p + jj // NJ))
                for t in range(NT):
                    for r in range(3):
                        h = (h_hi, h_hi, h_lo)[r][u]
                        w = (dn_hi, dn_lo, dn_hi)[r][u]
                        last = nc.tensor.matmul(ps_o[t][:], h[:, t * P:(t + 1) * P], w[:],
                                                start=(j == 0 and r == 0), stop=(j == NJ - 1 and r == 2))
                last.then_inc(down_mm, 1)

            with pe.Fori(0, NB // 2) as p:
                gate_up(p, 0)
                for jj in range(2 * NJ):
                    if jj + 1 < 2 * NJ:
                        gate_up(p, jj + 1)
                    down(p, jj)

        @block.scalar
        def _(act):
            act.sem_inc(gate_done, AHEAD)

            def split_gate_up(n, j):
                act.wait_ge(u_mm, TILES_AHEAD + n - 1)
                nc.scalar.activation(gu_hi[j % 2][:], wf_sb[:, j, 0:2 * DM], ACT.Copy).then_inc(gu_hi_done, 1)

            def split_down(n, j):
                act.wait_ge(down_mm, TILES_AHEAD + n - 1)
                nc.scalar.activation(dn_hi[j % 2][:], wf_sb[:, j, 2 * DM:], ACT.Copy).then_inc(dn_hi_done, 1)

            act.wait_ge(wf_loaded[0], 16)
            split_gate_up(0, 0)
            split_down(0, 0)
            act.wait_ge(wf_loaded[1], 16)
            split_gate_up(1, 1)
            with act.Fori(0, NB // 2) as p:
                for jj in range(2 * NJ):
                    u, j, n = jj % 2, jj % NJ, 2 * NJ * p + jj
                    act.wait_ge(g_mm, n + 1)
                    act.wait_ge(hid_done, TILES_AHEAD + n - 1)
                    nc.scalar.activation(act_g[u][:], ps_g[u][:], ACT.Silu).then_inc(g_done, 1)
                    if jj + 2 < NJ:
                        act.wait_ge(wf_loaded[j + 2], 16)
                    split_gate_up(n + 2, (j + 2) % NJ)
                    act.wait_ge(hid_done, TILES_AHEAD + n + 1)
                    act.wait_ge(down_mm, TILES_AHEAD + n - 1)
                    nc.scalar.activation(h_hi[u][:], hid[u][:], ACT.Copy).then_inc(hhi_done, 1)
                    split_down(n + 1, (j + 1) % NJ)
                    if j == NJ - 1:
                        act.wait_ge(down_mm, TILES_AHEAD + n + 1)
                        for t in range(NT):
                            m = NT * (2 * p + jj // NJ) + t
                            act.wait_ge(res_done, BLOCK_AHEAD + 2 * (m - NT) + 1)
                            nc.scalar.activation(gate[t][:], ps_o[t][:], ACT.Silu).then_inc(gate_done, 1)

        @block.vector
        def _(dve):
            dve.sem_inc(hid_done, TILES_AHEAD)
            tt = nc.vector.tensor_tensor

            def low_gate_up(n, j):
                dve.wait_ge(gu_hi_done, n + 1)
                tt(gu_lo[j % 2][:], wf_sb[:, j, 0:2 * DM], gu_hi[j % 2][:].bitcast(F32), ALU.subtract)\
                    .then_inc(gu_lo_done, 1)

            def low_down(n, j):
                dve.wait_ge(dn_hi_done, n + 1)
                tt(dn_lo[j % 2][:], wf_sb[:, j, 2 * DM:], dn_hi[j % 2][:].bitcast(F32), ALU.subtract)\
                    .then_inc(dn_lo_done, 1)

            low_gate_up(0, 0)
            low_down(0, 0)
            low_gate_up(1, 1)
            with dve.Fori(0, NB // 2) as p:
                for jj in range(2 * NJ):
                    u, j, n = jj % 2, jj % NJ, 2 * NJ * p + jj
                    dve.wait_ge(g_done, n + 1)
                    dve.wait_ge(u_mm, TILES_AHEAD + n + 1)
                    tt(hid[u][:], act_g[u][:], ps_u[u][:], ALU.mult).then_inc(hid_done, 1)
                    dve.wait_ge(hhi_done, n + 1)
                    tt(h_lo[u][:], hid[u][:], h_hi[u][:].bitcast(F32), ALU.subtract).then_inc(hlo_done, 1)
                    low_gate_up(n + 2, (j + 2) % NJ)
                    low_down(n + 1, (j + 1) % NJ)

        @block.gpsimd
        def _(pool):
            pool.sem_inc(res_done, BLOCK_AHEAD)
            tt = nc.gpsimd.tensor_tensor
            with pool.Fori(0, NB) as b:
                for t in range(NT):
                    u = t % 2
                    m = NT * b + t
                    pool.wait_ge(part_loaded[u], 32 * (2 * b + t // 2 + 1))
                    pool.wait_ge(out_stored[u], DMA_AHEAD + 16 * (2 * b + t // 2))
                    tt(total[u][:], parts[u][:, 0], parts[u][:, 1], ALU.add).then_inc(sums, 1)
                    for g in (2, 3):
                        pool.wait_ge(sums, 3 * m + g - 1)
                        tt(total[u][:], total[u][:], parts[u][:, g], ALU.add).then_inc(sums, 1)
                    pool.wait_ge(sums, 3 * m + 3)
                    pool.wait_ge(gate_done, AHEAD + m + 1)
                    tt(total[u][:], total[u][:], gate[t][:], ALU.mult).then_inc(res_done, 1)
                    pool.wait_ge(res_done, BLOCK_AHEAD + 2 * m + 1)
                    tt(total[u][:], total[u][:], x_res[u][:], ALU.add).then_inc(res_done, 1)


def build(nc, x, wqkv, wb, wo, rms, wf, out):
    with ExitStack() as ctx:
        sb = lambda name, shape: ctx.enter_context(nc.sbuf_tensor(name, shape, F32))
        xT = nc.dram_tensor("xT", (NBLK, P, 2, KT, BLK), F32, kind="Internal").ap()
        part = nc.dram_tensor("part", (2 * STEPS, P, DM), F32, kind="Internal").ap()
        ident = sb("ident", [P, P])
        upper = sb("upper", [P, P])
        upper_diag = sb("upper_diag", [P, P])
        below1 = sb("below1", [P, P // 2])
        above1 = sb("above1", [P, P // 2])
        level_masks = {m: sb(f"mask{m}", [P, P // 2]) for m in LEVELS if m < 32}
        sqrt_beta = sb("sqrt_beta", [P, NG, 2 * NBLK * HG])
        const = {"masks": (ident, upper, upper_diag, below1, above1, level_masks), "ident": ident,
                 "masks_n": 2 + len(level_masks) + 3 + 5 + 2 * len(level_masks)}
        phase_normalise(nc, ctx, x, wb, xT, const, sqrt_beta)
        phase_attention(nc, ctx, wqkv, wo, rms, xT, part, const, sqrt_beta)
        phase_feed_forward(nc, ctx, x, wf, xT, part, out)


def kernel(L0_attn_x, L0_attn_Wq, L0_attn_Wk, L0_attn_Wv, L0_attn_Wb, L0_attn_Wo, L0_attn_conv_q,
           L0_attn_conv_k, L0_attn_conv_v, L0_attn_rms_w, L0_ffn_w_gate, L0_ffn_w_up, L0_ffn_w_down):
    import numpy as np
    import concourse.bacc as bacc
    from concourse.bass_utils import run_bass_kernel_spmd as run

    def a(v):
        return np.asarray(v)

    xs = a(L0_attn_x).reshape(B * S // P, P, DM)
    tiles = []
    for w, cw in ((L0_attn_Wk, L0_attn_conv_k), (L0_attn_Wv, L0_attn_conv_v), (L0_attn_Wq, L0_attn_conv_q)):
        wt = a(w).reshape(NG, 2, 2, P, KT, P).transpose(0, 1, 5, 2, 4, 3).reshape(NG, 2, P, 2, KT * P)
        ct = a(cw).reshape(NG, 2, 2, P, KW).transpose(0, 1, 3, 2, 4)
        tiles.append(np.concatenate([wt, ct], axis=-1))
    wqkv = np.ascontiguousarray(np.stack(tiles, axis=1).reshape(NG, PAIRS, P, 2, KT * P + KW))
    wb = np.ascontiguousarray(a(L0_attn_Wb).reshape(NH, KT, P).transpose(2, 1, 0).reshape(P, KT * NH))
    wo = np.ascontiguousarray(a(L0_attn_Wo).reshape(DM, NG, HG, P).transpose(1, 3, 2, 0))
    rms = np.ascontiguousarray(a(L0_attn_rms_w).reshape(P, 1))
    nj = DH // P
    gu = [a(w).reshape(nj, P, KT, P).transpose(3, 0, 2, 1).reshape(P, nj, DM)
          for w in (L0_ffn_w_gate, L0_ffn_w_up)]
    down = a(L0_ffn_w_down).reshape(DM, nj, P).transpose(2, 1, 0)
    wf = np.ascontiguousarray(np.concatenate([*gu, down], axis=-1))

    nc = bacc.Bacc("TRN2", target_bir_lowering=False, num_devices=1)
    arrays, aps = {}, []
    for name, v in (("x", xs), ("wqkv", wqkv), ("wb", wb), ("wo", wo), ("rms", rms), ("wf", wf)):
        arrays[name] = v
        aps.append(nc.dram_tensor(name, v.shape, mybir.dt.from_np(v.dtype), kind="ExternalInput").ap())
    out = nc.dram_tensor("out", (B * S // P, P, DM), F32, kind="ExternalOutput").ap()
    build(nc, *aps, out)
    r = run(nc, [arrays], core_ids=[0])
    return r.results[0]["out"].reshape(B, S, DM)
```

```python
from contextlib import ExitStack

import concourse.bass as bass
from concourse import mybir

F32 = mybir.dt.float32
F32R = mybir.dt.float32r
ALU = mybir.AluOpType
ACT = mybir.ActivationFunctionType
AX_X = mybir.AxisListType.X

P = 128
B, S, DM = 2, 1024, 512
NH, HD, KW = 16, 128, 4
DH = 2048
KT = DM // P
HG = 4
NG = NH // HG
BLK = 2 * P
NBLK = B * S // BLK
SPG = S // BLK
STEPS = NG * B * SPG
GROUPS = STEPS // SPG
PAIRS = 3 * HG // 2
PIECES = PAIRS + HG // 2
LEVELS = [2, 4, 8, 16, 32, 64]
RESIDUAL = 2 + 2 * len(LEVELS)
HOPS = RESIDUAL + 3
AHEAD, DMA_AHEAD = 2, 16
LN_EPS, RMS_EPS, L2_EPS = 1e-5, 1e-5, 1e-6


def causal_masks(nc, eng, done, ident, upper, upper_diag, below1, above1, level_masks):
    n = 0

    def keep(t, op, base, pattern, mult, fill=0.0):
        nonlocal n
        eng.wait_ge(done, n)
        eng.affine_select(out=t, in_=t, compare_op=op, fill=fill, base=base, pattern=pattern,
                          channel_multiplier=mult).then_inc(done, 1)
        n += 1

    ones = [upper, upper_diag, *level_masks.values()]
    for t in ones:
        eng.memset(t[:], 1.0).then_inc(done, 1)
        n += 1
    for t in (ident, below1, above1):
        eng.memset(t[:], 0.0).then_inc(done, 1)
        n += 1
    keep(ident[:], ALU.not_equal, 0, [[-1, P]], 1, 1.0)
    keep(upper[:], ALU.is_gt, 0, [[1, P]], -1)
    keep(upper_diag[:], ALU.is_ge, 0, [[1, P]], -1)
    keep(below1[:], ALU.not_equal, -1, [[-2, P // 2]], 1, 1.0)
    keep(above1[:], ALU.not_equal, 0, [[-2, P // 2]], 1, 1.0)
    for m, t in level_masks.items():
        v = t[:].rearrange("p (b j) -> p b j", j=m)
        keep(v, ALU.is_ge, -m, [[-2 * m, P // (2 * m)], [0, m]], 1)
        keep(v, ALU.is_ge, 2 * m - 1, [[2 * m, P // (2 * m)], [0, m]], -1)
    return n


def phase_normalise(nc, ctx, x, wb, xT, const, sqrt_beta):
    NT = B * S // P
    with ExitStack() as own:
        sb = lambda name, shape, dt=F32: own.enter_context(nc.sbuf_tensor(name, shape, dt))
        sem = lambda name: ctx.enter_context(nc.semaphore(name))
        two = range(2)
        xt = sb("n_x", [P, NT, DM])
        stats = sb("n_stats", [P, NT, 6])
        mv = sb("n_mv", [P, NT, 2])
        veps = sb("n_veps", [P, NT])
        rstd = sb("n_rstd", [P, NT])
        xn = [sb(f"n_xn{u}", [P, DM]) for u in two]
        hi = [sb(f"n_hi{u}", [P, KT, P], F32R) for u in two]
        lo = [sb(f"n_lo{u}", [P, KT, P], F32R) for u in two]
        beta = [sb(f"n_beta{u}", [P, NH]) for u in two]
        wb_in = sb("n_wb", [P, KT * NH])
        wb_hi = sb("n_wbhi", [P, KT, NH], F32R)
        wb_lo = sb("n_wblo", [P, KT, NH], F32R)
        power = sb("n_power", [P, 2 * NH])
        ps_t = [own.enter_context(nc.psum_tensor(f"n_pst{u}", [P, KT, P], F32)) for u in two]
        ps_b = [own.enter_context(nc.psum_tensor(f"n_psb{u}", [P, 512], F32)) for u in two]
        masks_done, powers = sem("n_masks"), sem("n_powers")
        wb_loaded, wb_split = sem("n_wb_loaded"), sem("n_wb_split")
        loaded = [sem(f"n_loaded{t}") for t in range(NT)]
        veps_ready, rstd_ready, xn_ready = sem("n_veps_ready"), sem("n_rstd_ready"), sem("n_xn_ready")
        transposed, hi_ready, lo_ready = sem("n_transposed"), sem("n_hi_ready"), sem("n_lo_ready")
        logits, beta_ready, root_ready = sem("n_logits"), sem("n_beta_ready"), sem("n_root_ready")
        hi_stored = [sem(f"n_hi_stored{u}") for u in two]
        lo_stored = [sem(f"n_lo_stored{u}") for u in two]
        block = own.enter_context(nc.Block())

        @block.sync
        def _(sp):
            for u in two:
                sp.sem_inc(hi_stored[u], DMA_AHEAD)
                sp.sem_inc(lo_stored[u], DMA_AHEAD)
            for t in range(NT):
                sp.dma_start(xt[:, t], x[t]).then_inc(loaded[t], 16)
            sp.dma_start(wb_in[:], wb).then_inc(wb_loaded, 16)
            with sp.Fori(0, NBLK) as i:
                for u in two:
                    sp.wait_ge(hi_ready, AHEAD + 2 * i + u + 1)
                    sp.dma_start(xT[i][:, 0, :, u * P:(u + 1) * P], hi[u][:].bitcast(F32))\
                        .then_inc(hi_stored[u], 16)
                    sp.wait_ge(lo_ready, AHEAD + 2 * i + u + 1)
                    sp.dma_start(xT[i][:, 1, :, u * P:(u + 1) * P], lo[u][:].bitcast(F32))\
                        .then_inc(lo_stored[u], 16)
            for u in two:
                sp.wait_ge(hi_stored[u], DMA_AHEAD + 16 * NBLK)
                sp.wait_ge(lo_stored[u], DMA_AHEAD + 16 * NBLK)

        @block.gpsimd
        def _(pool):
            pool.sem_inc(root_ready, AHEAD)
            nc.gpsimd.memset(power[:, 0:NH], -0.5).then_inc(powers, 1)
            nc.gpsimd.memset(power[:, NH:], 0.5).then_inc(powers, 1)
            n = causal_masks(nc, pool, masks_done, *const["masks"])
            pool.wait_ge(masks_done, n)
            pool.wait_ge(powers, 2)
            for q in range(4):
                pool.wait_ge(veps_ready, q + 1)
                nc.gpsimd.tensor_tensor(rstd[:, 4 * q:4 * q + 4], veps[:, 4 * q:4 * q + 4],
                                        power[:, 0:4], ALU.pow).then_inc(rstd_ready, 1)
            with pool.Fori(0, NBLK) as i:
                for u in two:
                    pool.wait_ge(beta_ready, AHEAD + 2 * i + u + 1)
                    nc.gpsimd.tensor_tensor(
                        sqrt_beta[:, :, bass.ds(8 * i + 4 * u, 4)],
                        beta[u][:].rearrange("p (g h) -> p g h", h=HG),
                        power[:, NH:].rearrange("p (g h) -> p g h", h=HG), ALU.pow).then_inc(root_ready, 1)

        @block.vector
        def _(dve):
            dve.sem_inc(lo_ready, AHEAD)
            dve.sem_inc(hi_ready, AHEAD)
            for q in range(4):
                for t in range(4 * q, 4 * q + 4):
                    dve.wait_ge(loaded[t], 16)
                    nc.vector.bn_stats(stats[:, t], xt[:, t])
                dve.drain()
                for t in range(4 * q, 4 * q + 4):
                    nc.vector.bn_aggr(mv[:, t], stats[:, t])
                dve.drain()
                nc.vector.tensor_scalar(veps[:, 4 * q:4 * q + 4], mv[:, 4 * q:4 * q + 4, 1], LN_EPS, None,
                                        ALU.add).then_inc(veps_ready, 1)
            dve.wait_ge(wb_loaded, 16)
            nc.vector.tensor_copy(wb_hi[:].rearrange("p k h -> p (k h)"), wb_in[:]).then_inc(wb_split, 1)
            dve.wait_ge(wb_split, 1)
            nc.vector.tensor_tensor(wb_lo[:].rearrange("p k h -> p (k h)"), wb_in[:],
                                    wb_hi[:].bitcast(F32).rearrange("p k h -> p (k h)"), ALU.subtract)\
                .then_inc(wb_split, 1)
            dve.wait_ge(rstd_ready, 4)

            def normalise(t, u):
                nc.vector.tensor_scalar(xn[u][:], xt[:, bass.ds(t, 1), :].rearrange("p o d -> p (o d)"),
                                        mv[:, bass.ds(t, 1), 0], rstd[:, bass.ds(t, 1)],
                                        ALU.subtract, ALU.mult).then_inc(xn_ready, 1)

            for u in two:
                normalise(u, u)
            with dve.Fori(0, NBLK) as i:
                for u in two:
                    dve.wait_ge(hi_stored[u], DMA_AHEAD + 16 * i)
                    dve.wait_ge(logits, AHEAD + 2 * i + u - 1)
                    dve.wait_ge(transposed, 2 * i + u + 1)
                    nc.vector.tensor_copy(hi[u][:], ps_t[u][:]).then_inc(hi_ready, 1)
                    dve.wait_ge(lo_stored[u], DMA_AHEAD + 16 * i)
                    dve.wait_ge(hi_ready, AHEAD + 2 * i + u + 1)
                    nc.vector.tensor_tensor(lo[u][:], ps_t[u][:], hi[u][:].bitcast(F32), ALU.subtract)\
                        .then_inc(lo_ready, 1)
                    normalise((2 * i + u + 2) % NT, u)

        @block.scalar
        def _(act):
            act.sem_inc(beta_ready, AHEAD)
            with act.Fori(0, NBLK) as i:
                for u in two:
                    act.wait_ge(root_ready, AHEAD + 2 * i + u - 1)
                    act.wait_ge(logits, AHEAD + 2 * i + u + 1)
                    nc.scalar.activation(beta[u][:], ps_b[u][:, 0:NH], ACT.Sigmoid).then_inc(beta_ready, 1)

        @block.tensor
        def _(pe):
            pe.sem_inc(logits, AHEAD)
            ident = const["ident"]
            pe.wait_ge(masks_done, const["masks_n"])
            pe.wait_ge(wb_split, 2)
            def turn(t, u):
                pe.wait_ge(xn_ready, t + 1)
                for k in range(KT):
                    last = nc.tensor.transpose(ps_t[u][:, k, :], xn[u][:, k * P:(k + 1) * P], ident[:])
                last.then_inc(transposed, 1)

            for u in two:
                turn(u, u)
            with pe.Fori(0, NBLK) as i:
                for u in two:
                    pe.wait_ge(lo_ready, AHEAD + 2 * i + u + 1)
                    turn(2 * i + u + 2, u)
                    pe.wait_ge(beta_ready, AHEAD + 2 * i + u - 1)
                    for k in range(KT):
                        for n, (a, w) in enumerate(((hi, wb_hi), (lo, wb_hi), (hi, wb_lo))):
                            last = nc.tensor.matmul(ps_b[u][:, 0:NH], a[u][:, k, :], w[:, k, :],
                                                    start=(k == 0 and n == 0),
                                                    stop=(k == KT - 1 and n == 2))
                    last.then_inc(logits, 1)


def phase_attention(nc, ctx, w, wo, rms, xT, part, const, sqrt_beta):
    with ExitStack() as own:
        sb = lambda name, shape, dt=F32: own.enter_context(nc.sbuf_tensor(name, shape, dt))
        sem = lambda name: ctx.enter_context(nc.semaphore(name))
        bank = lambda name, shape: own.enter_context(nc.psum_tensor(name, shape, F32))

        xb = [sb(f"xb{u}", [P, 2, KT, BLK], F32R) for u in range(2)]
        w_in = [sb(f"w_in{u}", [P, 2, KT * P + KW]) for u in range(2)]
        w_hi = sb("w_hi", [P, PAIRS, 2, KT, P], F32R)
        w_lo = sb("w_lo", [P, PAIRS, 2, KT, P], F32R)
        taps = sb("taps", [P, PAIRS, 2, KW])
        wo_hi = sb("wo_hi", [P, HG, DM], F32R)
        wo_lo = sb("wo_lo", [P, HG, DM], F32R)
        rms_sb = sb("rms_sb", [P, 1])
        raw = [sb(f"raw{u}", [P, 2, BLK + KW - 1]) for u in range(2)]
        halo = sb("halo", [P, PAIRS, 2, KW - 1])
        conv = [sb(f"conv{u}", [P, 2, BLK]) for u in range(2)]
        squares = [sb(f"squares{u}", [P, 2, BLK]) for u in range(2)]
        kT = sb("kT", [P, HG, BLK])
        vT = sb("vT", [P, HG, BLK])
        qT = [sb(f"qT{u}", [P, HG, BLK]) for u in range(2)]
        k_sum = sb("k_sum", [P, 2, HG])
        k_rsqrt = sb("k_rsqrt", [P, 2, HG])
        k_scale = sb("k_scale", [P, 2, HG])
        v_scale = sb("v_scale", [P, 2, HG])
        q_term = [sb(f"q_term{u}", [P, 2, HG]) for u in range(4)]
        two = range(2)
        k_nat = [[sb(f"k_nat{u}{x}", [P, HG, P]) for x in two] for u in two]
        k_chn = [[sb(f"k_chn{u}{x}", [P, HG, P]) for x in two] for u in two]
        v_nat = [sb(f"v_nat{x}", [P, HG, P]) for x in two]
        pT = [sb(f"pT{x}", [P, HG, P]) for x in two]
        M = [sb(f"M{x}", [P, HG, P]) for x in two]
        G_hi = [sb(f"G_hi{x}", [P, HG, P], F32R) for x in two]
        T_hi = [sb(f"T_hi{x}", [P, HG, P], F32R) for x in two]
        U_hi = [sb(f"U_hi{x}", [P, HG, P], F32R) for x in two]
        Y = [[sb(f"Y{x}{u}", [P, HG, P], F32R) for u in two] for x in two]
        R = [sb(f"R{x}", [P, HG, P], F32R) for x in two]
        U = [[sb(f"U{u}{x}", [P, HG, P]) for x in two] for u in two]
        ident_hi = sb("ident_hi", [P, P], F32R)
        state = [sb(f"state{u}", [P, HG, P]) for u in two]
        resid = sb("resid", [P, HG, P])
        upd = sb("upd", [P, HG, P])
        o_raw = [sb(f"o_raw{x}", [P, HG, P]) for x in two]
        o_sum = [sb(f"o_sum{x}", [P, HG]) for x in two]
        o_var = [sb(f"o_var{x}", [P, HG]) for x in two]
        o_fac = [sb(f"o_fac{x}", [P, HG]) for x in two]
        o_work = sb("o_work", [P, HG, P])
        o_hi = sb("o_hi", [P, HG, P], F32R)
        o_lo = sb("o_lo", [P, HG, P], F32R)
        staged = sb("staged", [P, DM])
        power = sb("a_power", [P, 2 * HG])
        ones = sb("a_ones", [P, 1])
        zero = sb("a_zero", [P, HG])

        ps_a = [bank(f"ps_a{u}", [P, 2, BLK]) for u in two]
        ps_sum = bank("ps_sum", [P, 2, HG])
        ps_inv = [bank(f"ps_inv{x}", [P, 512]) for x in two]
        ps_vp = bank("ps_vp", [P, HG, P])
        ps_s = [bank(f"ps_s{u}", [P, HG, P]) for u in two]

        x_loaded = [sem(f"x_loaded{u}") for u in two]
        w_loaded = [sem(f"w_loaded{u}") for u in two]
        w_hi_done, w_lo_done = sem("w_hi_done"), sem("w_lo_done")
        rms_loaded, o_hi_done = sem("rms_loaded"), sem("o_hi_done")
        stored = sem("a_stored")
        consts, zeros, ident_done = sem("a_consts"), sem("a_zeros"), sem("a_ident_done")
        proj_mm, raw_done, conv_steps, silu_done = (sem(n) for n in (
            "proj_mm", "raw_done", "conv_steps", "silu_done"))
        k_turned, k_raw_done, k_squared, k_summed, kpow_done, kscale_ready, k_scaled = (sem(n) for n in (
            "k_turned", "k_raw_done", "k_squared", "k_summed", "kpow_done", "kscale_ready", "k_scaled"))
        q_squared, qsum_mm, qsum_read = sem("q_squared"), sem("qsum_mm"), sem("qsum_read")
        inv_mm = [sem(f"inv_mm{x}") for x in two]
        inv_done = [sem(f"inv_done{x}") for x in two]
        base_steps = [sem(f"base_steps{x}") for x in two]
        g_hi_done = [sem(f"g_hi_done{x}") for x in two]
        m_masked = [sem(f"m_masked{x}") for x in two]
        diag_done = [sem(f"diag_done{x}") for x in two]
        y_clear = [sem(f"y_clear{x}") for x in two]
        i_less_t = [sem(f"i_less_t{x}") for x in two]
        v_mm, v_done, p_mm, p_done = sem("v_mm"), sem("v_done"), sem("p_mm"), sem("p_done")
        ks_mm, resid_done, upd_mm, upd_done, state_mm, state_done, o_mm, o_done = (sem(n) for n in (
            "ks_mm", "resid_done", "upd_mm", "upd_done", "state_mm", "state_done", "o_mm", "o_done"))
        osq_done, osum_steps, ofac_done, onorm_done = (sem(n) for n in (
            "osq_done", "osum_steps", "ofac_done", "onorm_done"))
        turn_mm, turn_done, out_mm, out_done = (sem(n) for n in (
            "turn_mm", "turn_done", "out_mm", "out_done"))
        block = own.enter_context(nc.Block())

        ident, upper, upper_diag, below1, above1, level_masks = const["masks"]
        PROJECT = [8, 20, 4, 18, 2, 4, 12, 4, 4, 4, 14, 12, 0, 16, 12, 10, 0]
        RAW = [3, 7, 10, 12, 15, 16]
        CONV_A, CONV_B = [4, 8, 11, 13, 16, 17], [5, 9, 12, 14, 16, 18]
        SILU = [6, 10, 13, 15, 17, 19]

        def due(tables, hop, s, c, A, INV):
            found = []
            for exists, step, base in ((INV, (s, c), HOPS), (A, (s + 1, (c + 1) % 4), 0)):
                if exists:
                    found += [(*step, j, n) for j in range(PAIRS) for n, hops in enumerate(tables)
                              if hops[j] == hop + base]
            return found

        SPLIT_HI = {2: {8: 0, 10: 1}, 3: {0: 2, 3: 3, 6: 4, 9: 5}, 1: {2: 6, 5: 7}}
        SPLIT_LO = {2: {9: 0, 11: 1}, 3: {1: 2, 4: 3, 7: 4, 10: 5}, 1: {3: 6, 6: 7}}
        CONV_STEPS = 2 * KW
        KINDS = "kkvvqq"

        def dest(j, u):
            t = {"k": kT, "v": vT, "q": qT[u]}[KINDS[j]]
            return t[:, 2 * (j % 2):2 * (j % 2) + 2, :]

        def per_head(t, x):
            return t[:, x, :].unsqueeze(2).broadcast_to([P, HG, P])

        def all_heads(t, n):
            return t[:].unsqueeze(1).broadcast_to([P, HG, n])

        def first_half(t, m):
            return t.rearrange("p h (b k j) -> p h b k j", k=2, j=m)[:, :, :, 0, :]

        def second_half(t, m):
            return t.rearrange("p h (b k j) -> p h b k j", k=2, j=m)[:, :, :, 1, :]

        def packed(t, m):
            return t.rearrange("p (h b j) -> p h b j", h=HG, j=m)

        def run_slots(emit, eng):
            emit(-1, 3, True, False, False)
            emit(0, 0, True, True, False)
            emit(1, 1, True, True, True)
            with eng.Fori(0, GROUPS - 1) as g:
                for c in (2, 3, 4, 5):
                    emit(4 * g + c, c % 4, True, True, True)
            emit(STEPS - 2, 2, True, True, True)
            emit(STEPS - 1, 3, False, True, True)
            emit(STEPS, 0, False, False, True)

        @block.sync
        def _(sp):
            def load_x(s, c):
                sp.dma_start(xb[c % 2][:].bitcast(F32), xT[(s // 4) % 2 * 4 + c])\
                    .then_inc(x_loaded[c % 2], 16)

            def load_w(grp, j):
                if j < PAIRS:
                    sp.dma_start(w_in[j % 2][:], w[grp // 2, j]).then_inc(w_loaded[j % 2], 16)
                else:
                    heads = slice(2 * (j - PAIRS), 2 * (j - PAIRS) + 2)
                    sp.dma_start(w_in[j % 2][:, :, 0:DM], wo[grp // 2][:, heads]).then_inc(w_loaded[j % 2], 16)

            sp.dma_start(rms_sb[:], rms).then_inc(rms_loaded, 16)
            load_w(0, 0)
            load_x(0, 0)
            load_w(0, 1)
            load_x(1, 1)
            sp.wait_ge(w_lo_done, 1)
            load_w(0, 2)

            def slot(s, c, A, INV, SCAN):
                def load_more(grp, pieces):
                    for j in pieces:
                        sp.wait_ge(w_lo_done, PIECES * grp + j - 1)
                        load_w(grp, j)

                following = (s - c) // SPG + 1

                next_group = A and not (isinstance(s, int) and s >= STEPS - 2)
                if A and not (isinstance(s, int) and s + 2 >= STEPS):
                    if not (isinstance(s, int) and s < 0):
                        sp.wait_ge(proj_mm, PAIRS * (s + 1))
                        load_x(s + 2, (c + 2) % 4)
                if next_group and c == 2:
                    load_more(following, (0, 1))
                if next_group and c == 3:
                    load_more(following, (3,))
                if c == 0 and INV:
                    load_more(s // SPG, (6, 7))
                if next_group and c == 2:
                    load_more(following, (2,))
                if next_group and c == 3:
                    load_more(following, (4, 5))
                if SCAN:
                    for x in two:
                        sp.wait_ge(out_done, 2 * (s - 1) + x + 1)
                        sp.dma_start(part[2 * (s - 1) + x], staged[:]).then_inc(stored, 16)

            run_slots(slot, sp)
            sp.wait_ge(stored, 32 * STEPS)

        @block.tensor
        def _(pe):
            mm = nc.tensor.matmul
            pe.wait_ge(consts, 3)
            pe.wait_ge(ident_done, 1)

            def project(s, c, lo, hi):
                for n in range(lo, hi):
                    j, r = divmod(n, 24)
                    t, r = divmod(r, 12)
                    k, r = divmod(r, 3)
                    u = j % 2
                    if n % 24 == 0:
                        if j == 0:
                            pe.wait_ge(x_loaded[c % 2], 16 * ((s - c % 2) // 2 + 1))
                        pe.wait_ge(w_lo_done, PIECES * (s // SPG) + j + 1)
                        if not (isinstance(s, int) and s == 0 and j < 2):
                            pe.wait_ge(raw_done, PAIRS * s + j - 1)
                    weights = (w_hi, w_hi, w_lo)[r]
                    last = mm(ps_a[u][:, t, :], weights[:, j, t, k, :], xb[c % 2][:, (0, 1, 0)[r], k, :],
                              start=(k == 0 and r == 0), stop=(k == KT - 1 and r == 2))
                    if n % 24 == 23:
                        last.then_inc(proj_mm, 1)

            def sum_squares(s, i):
                pe.wait_ge(q_squared, 2 * s + i + 1)
                if i == 0 and not (isinstance(s, int) and s == 0):
                    pe.wait_ge(qsum_read, s)
                for t in range(2):
                    for x in two:
                        last = mm(ps_sum[:, x, 2 * i + t:2 * i + t + 1],
                                  squares[i][:, t, x * P:(x + 1) * P], ones[:], start=True, stop=True)
                last.then_inc(qsum_mm, 1)

            def turn_k(s, c, x):
                if x == 0:
                    pe.wait_ge(silu_done, PAIRS * s + 2)
                    if not (isinstance(s, int) and s == 0):
                        pe.wait_ge(p_done, 2 * s)
                else:
                    pe.wait_ge(k_raw_done, 2 * s + 1)
                for h in range(HG):
                    last = nc.tensor.transpose(ps_vp[:, h, :], kT[:, h, x * P:(x + 1) * P], ident[:])
                last.then_inc(k_turned, 1)

            def inverse(s, c, x, hop):
                u = c % 2
                out = ps_inv[x]
                if not (isinstance(s, int) and s == 0 and hop == 0):
                    pe.wait_ge(inv_done[x], HOPS * s + hop)
                if hop == 0:
                    pe.wait_ge(k_scaled, 2 * s + x + 1)
                    for h in range(HG):
                        last = nc.tensor.transpose(out[:, h * P:(h + 1) * P], k_nat[u][x][:, h, :], ident[:])
                elif hop == 1:
                    for h in range(HG):
                        last = mm(out[:, h * P:(h + 1) * P], k_chn[u][x][:, h, :], k_chn[u][x][:, h, :],
                                  start=True, stop=True)
                elif hop < RESIDUAL and hop % 2 == 0:
                    i = (hop - 2) // 2
                    if hop == 2:
                        pe.wait_ge(g_hi_done[x], s + 1)
                        pe.wait_ge(diag_done[x], s + 1)
                    for h in range(HG):
                        last = mm(out[:, 64 * h:64 * h + 64], G_hi[x][:, h, :],
                                  first_half(T_hi[x][:], LEVELS[i])[:, h], start=True, stop=True)
                elif hop < RESIDUAL:
                    i = (hop - 2) // 2
                    y = Y[x][i % 2]
                    for h in range(HG):
                        mm(out[:, 64 * h:64 * h + 64], U_hi[x][:, h, :],
                           first_half(y[:], LEVELS[i])[:, h], start=True, stop=True)
                    for h in range(HG):
                        last = mm(out[:, 256 + 64 * h:320 + 64 * h], y[:, h, :],
                                  second_half(U_hi[x][:], LEVELS[i])[:, h], start=True, stop=True)
                elif hop == RESIDUAL:
                    pe.wait_ge(m_masked[x], s + 1)
                    for h in range(HG):
                        last = mm(out[:, h * P:(h + 1) * P], M[x][:, h, :], T_hi[x][:, h, :].bitcast(F32),
                                  start=True, stop=True)
                elif hop == RESIDUAL + 1:
                    for h in range(HG):
                        last = mm(out[:, h * P:(h + 1) * P], R[x][:, h, :], U_hi[x][:, h, :],
                                  start=True, stop=True)
                else:
                    for h in range(HG):
                        mm(out[:, h * P:(h + 1) * P], T_hi[x][:, h, :], ident_hi[:], start=True, stop=False)
                        last = mm(out[:, h * P:(h + 1) * P], R[x][:, h, :], G_hi[x][:, h, :],
                                  start=False, stop=True)
                last.then_inc(inv_mm[x], 1)

            def values(s, c, x):
                if x == 0:
                    pe.wait_ge(silu_done, PAIRS * s + 4)
                if x:
                    pe.wait_ge(p_done, 2 * s + 1)
                else:
                    pe.wait_ge(k_raw_done, 2 * s + 2)
                for h in range(HG):
                    last = nc.tensor.transpose(ps_vp[:, h, :], vT[:, h, x * P:(x + 1) * P], ident[:])
                last.then_inc(v_mm, 1)

            def scores(s, c, x):
                u = c % 2
                if x == 0:
                    pe.wait_ge(silu_done, PAIRS * s + 6)
                pe.wait_ge(v_done, 2 * s + x + 1)
                pe.wait_ge(inv_done[x], HOPS * s + 1)
                for h in range(HG):
                    last = mm(ps_vp[:, h, :], k_chn[u][x][:, h, :], qT[u][:, h, x * P:(x + 1) * P],
                              start=True, stop=True)
                last.then_inc(p_mm, 1)

            def scan_ks(r, c, x):
                u, n = c % 2, 2 * r + x
                if x == 0:
                    for y in two:
                        pe.wait_ge(inv_done[y], HOPS * (r + 1))
                pe.wait_ge(state_done, n + 1)
                if x == 0 and not (isinstance(r, int) and r == 0):
                    pe.wait_ge(turn_done, 2 * r)
                for h in range(HG):
                    last = mm(ps_s[0][:, h, :], k_chn[u][x][:, h, :], state[x][:, h, :], start=True, stop=True)
                last.then_inc(ks_mm, 1)

            def scan_upd(r, c, x):
                u, n = c % 2, 2 * r + x
                pe.wait_ge(resid_done, n + 1)
                if x == 1:
                    pe.wait_ge(o_done, n)
                elif not (isinstance(r, int) and r == 0):
                    pe.wait_ge(out_done, 2 * r)
                for h in range(HG):
                    last = mm(ps_s[1][:, h, :], U[u][x][:, h, :], resid[:, h, :], start=True, stop=True)
                last.then_inc(upd_mm, 1)

            def scan_state_out(r, c, x):
                u, n = c % 2, 2 * r + x
                pe.wait_ge(upd_done, n + 1)
                for h in range(HG):
                    last = mm(ps_s[0][:, h, :], k_nat[u][x][:, h, :], upd[:, h, :], start=True, stop=True)
                last.then_inc(state_mm, 1)
                pe.wait_ge(p_done, 2 * r + x + 1)
                for h in range(HG):
                    mm(ps_s[1][:, h, :], qT[u][:, h, x * P:(x + 1) * P], state[x][:, h, :],
                       start=True, stop=False)
                    last = mm(ps_s[1][:, h, :], pT[x][:, h, :], upd[:, h, :], start=False, stop=True)
                last.then_inc(o_mm, 1)

            def turn(r, x):
                n = 2 * r + x
                pe.wait_ge(onorm_done, n + 1)
                if x == 0:
                    pe.wait_ge(state_done, 2 * r + 3)
                else:
                    pe.wait_ge(turn_done, n)
                for h in range(HG):
                    last = nc.tensor.transpose(ps_s[0][:, h, :], o_work[:, h, :], ident[:])
                last.then_inc(turn_mm, 1)

            def project_out(r, x, heads):
                n = 2 * r + x
                if heads[0] == 0:
                    pe.wait_ge(turn_done, n + 1)
                    pe.wait_ge(w_lo_done, PIECES * (r // SPG) + PIECES)
                    if x == 0:
                        pe.wait_ge(o_done, n + 2)
                    else:
                        pe.wait_ge(out_done, n)
                for h in heads:
                    for n, (a, w) in enumerate(((o_hi, wo_hi), (o_hi, wo_lo), (o_lo, wo_hi))):
                        last = mm(ps_s[1][:].rearrange("p h d -> p (h d)"), a[:, h, :], w[:, h, :],
                                  start=(h == 0 and n == 0), stop=(h == HG - 1 and n == 2))
                if heads[-1] == HG - 1:
                    last.then_inc(out_mm, 1)

            def slot(s, c, A, INV, SCAN):
                for hop in range(HOPS):
                    if INV:
                        for x in two:
                            inverse(s, c, x, hop)
                    r, rc = s - 1, (c - 1) % 4
                    if SCAN and hop == 0:
                        scan_ks(r, rc, 0)
                    if INV and hop in (0, 6):
                        values(s, c, hop // 6)
                    if INV and hop in (5, 6):
                        sum_squares(s, hop - 5)
                    if SCAN and hop == 2:
                        scan_upd(r, rc, 0)
                    if SCAN and hop == 4:
                        scan_state_out(r, rc, 0)
                    if INV and hop in (5, 9):
                        scores(s, c, hop // 9)
                    if SCAN and hop == 5:
                        scan_ks(r, rc, 1)
                    if SCAN and hop == 7:
                        scan_upd(r, rc, 1)
                    if SCAN and hop == 8:
                        scan_state_out(r, rc, 1)
                    if SCAN and hop == 9:
                        turn(r, 0)
                    if SCAN and hop == 12:
                        project_out(r, 0, (0, 1, 2, 3))
                    if SCAN and hop == 13:
                        turn(r, 1)
                    if SCAN and hop in (15, 16):
                        project_out(r, 1, ((0, 1), (2, 3))[hop - 15])
                    if A and hop in (11, 12):
                        turn_k(s + 1, (c + 1) % 4, hop - 11)
                    if A:
                        project(s + 1, (c + 1) % 4, sum(PROJECT[:hop]), sum(PROJECT[:hop + 1]))

            run_slots(slot, pe)

        @block.scalar
        def _(act):
            act.wait_ge(rms_loaded, 16)

            def split_w(grp, j):
                act.wait_ge(w_loaded[j % 2], 16 * (PIECES // 2 * grp + j // 2 + 1))
                if not (isinstance(grp, int) and grp == 0):
                    if j < PAIRS:
                        act.wait_ge(proj_mm, PAIRS * (SPG * grp - 1) + j + 1)
                    else:
                        act.wait_ge(out_mm, 2 * SPG * grp)
                if j >= PAIRS:
                    nc.scalar.activation(wo_hi[:, 2 * (j - PAIRS):2 * (j - PAIRS) + 2], w_in[j % 2][:, :, 0:DM],
                                         ACT.Copy).then_inc(w_hi_done, 1)
                    return
                nc.scalar.activation(w_hi[:, j].rearrange("p t k c -> p t (k c)"), w_in[j % 2][:, :, 0:KT * P],
                                     ACT.Copy).then_inc(w_hi_done, 1)

            def copy_raw(s, c, j):
                act.wait_ge(proj_mm, PAIRS * s + j + 1)
                if not (isinstance(s, int) and s == 0 and j < 2):
                    act.wait_ge(conv_steps, CONV_STEPS * (PAIRS * s + j - 1))
                    act.wait_ge(silu_done, PAIRS * s + j - 1)
                act.wait_ge(w_lo_done, PIECES * (s // SPG) + j + 1)
                for t in range(2):
                    nc.scalar.activation(conv[j % 2][:, t, :], ps_a[j % 2][:, t, :], ACT.Copy,
                                         scale=taps[:, j, t, KW - 1:])
                nc.scalar.activation(raw[j % 2][:, :, KW - 1:], ps_a[j % 2][:], ACT.Copy)\
                    .then_inc(raw_done, 1)

            def silu(s, c, j):
                act.wait_ge(conv_steps, CONV_STEPS * (PAIRS * s + j + 1) - 1)
                if not (isinstance(s, int) and s == 0):
                    if KINDS[j] == "k":
                        act.wait_ge(k_turned, 2 * (s - 1) + 2)
                    elif KINDS[j] == "v":
                        act.wait_ge(v_mm, 2 * (s - 1) + 2)
                    elif not (isinstance(s, int) and s < 2):
                        act.wait_ge(o_mm, 2 * (s - 2) + 2)
                nc.scalar.activation(dest(j, c % 2), conv[j % 2][:], ACT.Silu).then_inc(silu_done, 1)

            def inverse(s, c, x, hop):
                u = c % 2
                out = ps_inv[x]
                act.wait_ge(inv_mm[x], HOPS * s + hop + 1)
                if hop == 0:
                    if not (isinstance(s, int) and s < 2):
                        act.wait_ge(ks_mm, 2 * (s - 2) + x + 1)
                    last = nc.scalar.activation(k_chn[u][x][:].rearrange("p h t -> p (h t)"), out[:], ACT.Copy)
                elif hop == 1:
                    act.wait_ge(base_steps[x], 2 * s + 2)
                    nc.scalar.activation(M[x][:].rearrange("p h t -> p (h t)"), out[:], ACT.Copy)
                    nc.scalar.activation(G_hi[x][:].rearrange("p h t -> p (h t)"), out[:], ACT.Copy)\
                        .then_inc(g_hi_done[x], 1)
                    return
                elif hop == HOPS - 1:
                    last = nc.scalar.activation(U[u][x][:].rearrange("p h t -> p (h t)"), out[:], ACT.Copy)
                else:
                    i = (hop - 2) // 2
                    m, y = LEVELS[i], Y[x][i % 2]
                    ps = [out[:, k:k + 256].rearrange("p (h b j) -> p h b j", h=HG, j=m) for k in (0, 256)]
                    if hop % 2 == 0:
                        act.wait_ge(y_clear[x], len(LEVELS) * s + i + 1)
                    for b in range(P // (2 * m)):
                        first = slice(2 * m * b, 2 * m * b + m)
                        second = slice(2 * m * b + m, 2 * m * (b + 1))
                        if hop % 2 == 0:
                            last = nc.scalar.activation(y[second, :, first], ps[0][second, :, b, :], ACT.Copy)
                        else:
                            nc.scalar.activation(T_hi[x][second, :, first], ps[0][second, :, b, :],
                                                 ACT.Copy, scale=-1.0)
                            last = nc.scalar.activation(U_hi[x][first, :, second], ps[1][first, :, b, :],
                                                        ACT.Copy, scale=-1.0)
                last.then_inc(inv_done[x], 1)

            def copy_k(s, c, x):
                act.wait_ge(k_turned, 2 * s + x + 1)
                if not (isinstance(s, int) and s < 2):
                    act.wait_ge(state_mm, 2 * (s - 2) + x + 1)
                nc.scalar.activation(k_nat[c % 2][x][:], ps_vp[:], ACT.Copy).then_inc(k_raw_done, 1)

            def copy_upd(r, x):
                n = 2 * r + x
                act.wait_ge(upd_mm, n + 1)
                if not (isinstance(r, int) and n == 0):
                    act.wait_ge(o_mm, n)
                nc.scalar.activation(upd[:], ps_s[1][:], ACT.Copy).then_inc(upd_done, 1)

            def copy_o(r, x):
                n = 2 * r + x
                act.wait_ge(o_mm, n + 1)
                if not (isinstance(r, int) and r == 0):
                    act.wait_ge(onorm_done, n - 1)
                nc.scalar.activation(o_raw[x][:], ps_s[1][:], ACT.Copy).then_inc(o_done, 1)

            def copy_turned(r, x):
                n = 2 * r + x
                act.wait_ge(turn_mm, n + 1)
                if not (isinstance(r, int) and n == 0):
                    act.wait_ge(out_mm, n)
                nc.scalar.activation(o_hi[:], ps_s[0][:], ACT.Copy, scale=rms_sb[:]).then_inc(o_hi_done, 1)

            def copy_out(r, x):
                n = 2 * r + x
                act.wait_ge(out_mm, n + 1)
                if not (isinstance(r, int) and n == 0):
                    act.wait_ge(stored, 16 * n)
                nc.scalar.activation(staged[:], ps_s[1][:].rearrange("p h d -> p (h d)"), ACT.Copy)\
                    .then_inc(out_done, 1)

            for j in range(2):
                split_w(0, j)

            def slot(s, c, A, INV, SCAN):
                for hop in range(HOPS):
                    if INV and hop in (0, 1, 10, 11, 12, 13, HOPS - 1):
                        for x in two:
                            inverse(s, c, x, hop)
                    r = s - 1
                    if SCAN and hop == 2:
                        copy_upd(r, 0)
                    if SCAN and hop == 4:
                        copy_o(r, 0)
                    if SCAN and hop == 7:
                        copy_upd(r, 1)
                    if SCAN and hop == 8:
                        copy_o(r, 1)
                    if SCAN and hop == 9:
                        copy_turned(r, 0)
                    if SCAN and hop == 12:
                        copy_out(r, 0)
                    if SCAN and hop == 13:
                        copy_turned(r, 1)
                    if SCAN and hop == 16:
                        copy_out(r, 1)
                    if A and hop in (11, 12):
                        copy_k(s + 1, (c + 1) % 4, hop - 11)
                    for step, sc, j, what in due((RAW, SILU), hop, s, c, A, INV):
                        if what == 0:
                            copy_raw(step, sc, j)
                        else:
                            silu(step, sc, j)
                    if A and c in SPLIT_HI and hop in SPLIT_HI[c] and \
                            not (isinstance(s, int) and s >= STEPS - 2):
                        split_w((s - c) // SPG + (1 if c >= 2 else 0), SPLIT_HI[c][hop])

            run_slots(slot, act)

        @block.gpsimd
        def _(pool):
            nc.gpsimd.memset(power[:], -0.5).then_inc(consts, 1)
            nc.gpsimd.memset(ones[:], 1.0).then_inc(consts, 1)
            nc.gpsimd.memset(zero[:], 0.0).then_inc(consts, 1)
            for x in two:
                for u in two:
                    nc.gpsimd.memset(Y[x][u][:].bitcast(F32), 0.0).then_inc(y_clear[x], 1)
            nc.gpsimd.memset(state[0][:], 0.0).then_inc(zeros, 1)
            nc.gpsimd.memset(halo[:], 0.0).then_inc(zeros, 1)
            pool.wait_ge(consts, 3)

            def clear_y(s, x, i):
                m = LEVELS[(i + 2) % len(LEVELS)]
                none = zero[:].unsqueeze(2).unsqueeze(3).broadcast_to([P, HG, P // (2 * m), m])
                pool.wait_ge(inv_mm[x], HOPS * s + 4 + 2 * i)
                nc.gpsimd.tensor_tensor(second_half(Y[x][i % 2][:], m), none, none, ALU.add)\
                    .then_inc(y_clear[x], 1)

            def ident_less_t(s, c, x):
                pool.wait_ge(inv_done[x], HOPS * s + RESIDUAL)
                if not (isinstance(s, int) and s < 2):
                    pool.wait_ge(upd_mm, 2 * (s - 2) + x + 1)
                nc.gpsimd.tensor_tensor(U[c % 2][x][:], all_heads(ident, P), T_hi[x][:].bitcast(F32),
                                        ALU.subtract).then_inc(i_less_t[x], 1)

            def diagonals(s, x):
                if not (isinstance(s, int) and s == 0):
                    pool.wait_ge(inv_mm[x], HOPS * s)
                for k, t in ((1, T_hi[x]), (0, U_hi[x])):
                    column = ident[:].rearrange("p (c k) -> p c k", k=2)[:, :, k]
                    last = nc.gpsimd.tensor_tensor(t[:].rearrange("p h (c k) -> p h c k", k=2)[:, :, :, k],
                                                   column.unsqueeze(1).broadcast_to([P, HG, P // 2]),
                                                   zero[:].unsqueeze(2).broadcast_to([P, HG, P // 2]), ALU.add)
                last.then_inc(diag_done[x], 1)

            def mask_m(s, x):
                pool.wait_ge(g_hi_done[x], s + 1)
                nc.gpsimd.tensor_tensor(M[x][:], M[x][:], all_heads(upper, P), ALU.mult).then_inc(m_masked[x], 1)

            def square_k(s, c, x):
                pool.wait_ge(k_raw_done, 2 * s + x + 1)
                if not (isinstance(s, int) and s == 0):
                    pool.wait_ge(qsum_mm, 2 * (s - 1) + x + 1)
                src = k_nat[c % 2][x][:].rearrange("p h d -> p (h d)")
                nc.gpsimd.tensor_tensor(squares[x][:].rearrange("p t d -> p (t d)"), src, src, ALU.mult)\
                    .then_inc(k_squared, 1)

            def square_q(s, c, i):
                pool.wait_ge(silu_done, PAIRS * s + 5 + i)
                pool.wait_ge(k_summed, 3 * s + i + 1)
                src = dest(4 + i, c % 2)
                nc.gpsimd.tensor_tensor(squares[i][:], src, src, ALU.mult).then_inc(q_squared, 1)

            def norm_o(r, c, x):
                n = 2 * r + x
                pool.wait_ge(osum_steps, 2 * n + 2)
                nc.gpsimd.tensor_tensor(o_fac[x][:], o_var[x][:], power[:, 0:HG], ALU.pow)\
                    .then_inc(ofac_done, 1)
                pool.wait_ge(ofac_done, n + 1)
                if not (isinstance(r, int) and n == 0):
                    pool.wait_ge(turn_mm, n)
                nc.gpsimd.tensor_tensor(o_work[:], o_raw[x][:],
                                        o_fac[x][:].unsqueeze(2).broadcast_to([P, HG, P]), ALU.mult)\
                    .then_inc(onorm_done, 1)

            def square_o(r, x):
                n = 2 * r + x
                pool.wait_ge(o_done, n + 1)
                if not (isinstance(r, int) and n == 0):
                    pool.wait_ge(turn_mm, n)
                nc.gpsimd.tensor_tensor(o_work[:], o_raw[x][:], o_raw[x][:], ALU.mult).then_inc(osq_done, 1)

            def slot(s, c, A, INV, SCAN):
                for hop in range(HOPS):
                    r = s - 1
                    if INV and hop == 0:
                        for x in two:
                            diagonals(s, x)
                    if INV and hop % 2 == 1 and 3 <= hop < RESIDUAL:
                        for x in two:
                            clear_y(s, x, (hop - 3) // 2)
                    if INV and hop in (2, 4):
                        mask_m(s, (hop - 2) // 2)
                    if INV and hop in (1, 3):
                        square_q(s, c, hop // 2)
                    if INV and hop == RESIDUAL - 1:
                        for x in two:
                            ident_less_t(s, c, x)
                    if SCAN and hop == 5:
                        square_o(r, 0)
                    if SCAN and hop == 7:
                        norm_o(r, (c - 1) % 4, 0)
                    if SCAN and hop == 10:
                        square_o(r, 1)
                    if SCAN and hop == 12:
                        norm_o(r, (c - 1) % 4, 1)
                    if A and hop in (12, 13):
                        square_k(s + 1, (c + 1) % 4, hop - 12)
                    if A and hop == 15:
                        pool.wait_ge(k_summed, 3 * (s + 1) + 3)
                        if not (isinstance(s, int) and s < 0):
                            pool.wait_ge(kscale_ready, 2 * (s + 1))
                        nc.gpsimd.tensor_tensor(k_rsqrt[:].rearrange("p x h -> p (x h)"),
                                                k_sum[:].rearrange("p x h -> p (x h)"), power[:],
                                                ALU.pow).then_inc(kpow_done, 1)

            run_slots(slot, pool)

        @block.vector
        def _(dve):
            tt = nc.vector.tensor_tensor
            dve.wait_ge(zeros, 2)
            dve.wait_ge(rms_loaded, 16)
            nc.vector.tensor_copy(ident_hi[:], ident[:]).then_inc(ident_done, 1)

            nc.vector.tensor_copy(state[0][:], state[0][:]).then_inc(state_done, 1)

            def split_w(grp, j):
                dve.wait_ge(w_hi_done, PIECES * grp + j + 1)
                if j >= PAIRS:
                    heads = slice(2 * (j - PAIRS), 2 * (j - PAIRS) + 2)
                    if not (isinstance(grp, int) and grp == 0):
                        dve.wait_ge(out_mm, 2 * SPG * grp)
                    tt(wo_lo[:, heads], w_in[j % 2][:, :, 0:DM], wo_hi[:, heads].bitcast(F32), ALU.subtract)\
                        .then_inc(w_lo_done, 1)
                    return
                if not (isinstance(grp, int) and grp == 0):
                    dve.wait_ge(proj_mm, PAIRS * (SPG * grp - 1) + j + 1)
                    dve.wait_ge(conv_steps, CONV_STEPS * (PAIRS * (SPG * grp - 1) + j + 1))
                nc.vector.tensor_copy(taps[:, j], w_in[j % 2][:, :, KT * P:])
                tt(w_lo[:, j].rearrange("p t k c -> p t (k c)"), w_in[j % 2][:, :, 0:KT * P],
                   w_hi[:, j].bitcast(F32).rearrange("p t k c -> p t (k c)"), ALU.subtract).then_inc(w_lo_done, 1)

            def convolve(s, c, j, half):
                u = j % 2
                n = CONV_STEPS * (PAIRS * s + j)
                if half == 0:
                    dve.wait_ge(raw_done, PAIRS * s + j + 1)
                    if c == 0:
                        nc.vector.memset(raw[u][:, :, 0:KW - 1], 0.0).then_inc(conv_steps, 1)
                    else:
                        nc.vector.tensor_copy(raw[u][:, :, 0:KW - 1], halo[:, j]).then_inc(conv_steps, 1)
                    dve.wait_ge(w_lo_done, PIECES * (s // SPG) + j + 1)
                    dve.wait_ge(conv_steps, n + 1)
                for k in range(3 * half, 3 * half + 3):
                    i, t = divmod(k, 2)
                    if i:
                        dve.wait_ge(conv_steps, n + k)
                    nc.vector.scalar_tensor_tensor(
                        conv[u][:, t, :], raw[u][:, t, i:i + BLK], taps[:, j, t, i:i + 1],
                        conv[u][:, t, :], ALU.mult, ALU.add).then_inc(conv_steps, 1)
                if half == 1:
                    nc.vector.tensor_copy(halo[:, j], raw[u][:, :, BLK:]).then_inc(conv_steps, 1)

            def below_above(x):
                halves = R[x][:].rearrange("p h (k c) -> p h k c", k=2)
                return ((halves[:, :, 0], below1, T_hi[x]), (halves[:, :, 1], above1, U_hi[x]))

            def mask_pairs(s, x):
                dve.wait_ge(inv_mm[x], HOPS * s + 2)
                ps = ps_inv[x][:].rearrange("p (h c k) -> p h c k", h=HG, k=2)
                for k, (half, mask, _) in enumerate(below_above(x)):
                    tt(half, ps[:, :, :, k], all_heads(mask, P // 2), ALU.mult).then_inc(base_steps[x], 1)

            def base(s, x):
                for k, (half, _, t) in enumerate(below_above(x)):
                    dve.wait_ge(base_steps[x], 2 * s + 1 + k)
                    column = ident[:].rearrange("p (c k) -> p c k", k=2)[:, :, k]
                    last = tt(t[:].rearrange("p h (c k) -> p h c k", k=2)[:, :, :, k],
                              column.unsqueeze(1).broadcast_to([P, HG, P // 2]), half.bitcast(F32), ALU.subtract)
                last.then_inc(inv_done[x], 1)

            def inverse(s, c, x, hop):
                u = c % 2
                out = ps_inv[x]
                dve.wait_ge(inv_mm[x], HOPS * s + hop + 1)
                if hop == RESIDUAL:
                    dve.wait_ge(i_less_t[x], s + 1)
                    tt(R[x][:].rearrange("p h t -> p (h t)"), U[u][x][:].rearrange("p h t -> p (h t)"), out[:],
                       ALU.subtract).then_inc(inv_done[x], 1)
                elif hop == RESIDUAL + 1:
                    tt(G_hi[x][:].rearrange("p h t -> p (h t)"),
                       U_hi[x][:].bitcast(F32).rearrange("p h t -> p (h t)"), out[:], ALU.add)\
                        .then_inc(inv_done[x], 1)
                elif hop % 2 == 0:
                    i = (hop - 2) // 2
                    m = LEVELS[i]
                    mask = level_masks[m][:].rearrange("p (b j) -> p b j", j=m)\
                        .unsqueeze(1).broadcast_to([P, HG, P // (2 * m), m])
                    dve.wait_ge(y_clear[x], len(LEVELS) * s + i + 1)
                    tt(first_half(Y[x][i % 2][:], m), packed(out[:, 0:256], m), mask, ALU.mult)\
                        .then_inc(inv_done[x], 1)
                else:
                    m = LEVELS[(hop - 2) // 2]
                    T, U2 = first_half(T_hi[x][:], m), second_half(U_hi[x][:], m)
                    tt(T, T.bitcast(F32), packed(out[:, 0:256], m), ALU.subtract)
                    tt(U2, U2.bitcast(F32), packed(out[:, 256:512], m), ALU.subtract).then_inc(inv_done[x], 1)

            def values(s, c, x):
                dve.wait_ge(v_mm, 2 * s + x + 1)
                if not (isinstance(s, int) and s == 0):
                    dve.wait_ge(resid_done, 2 * (s - 1) + x + 1)
                tt(v_nat[x][:], ps_vp[:], per_head(v_scale, x), ALU.mult).then_inc(v_done, 1)

            def sum_k(s, x):
                dve.wait_ge(k_squared, 2 * s + x + 1)
                if x == 0 and not (isinstance(s, int) and s == 0):
                    dve.wait_ge(kpow_done, s)
                nc.vector.reduce_sum(k_sum[:, x], squares[x][:].rearrange("p t (a d) -> p (t a) d", d=HD), AX_X)\
                    .then_inc(k_summed, 1)
                if x == 1:
                    dve.wait_ge(k_summed, 3 * s + 2)
                    nc.vector.tensor_scalar(k_sum[:], k_sum[:], L2_EPS, None, ALU.add).then_inc(k_summed, 1)

            def scale_k(s, c):
                dve.wait_ge(kpow_done, s + 1)
                root = sqrt_beta[:].rearrange("p g t -> p (g t)")[:, bass.ds(8 * s, 8)]
                tt(k_scale[:].rearrange("p x h -> p (x h)"), k_rsqrt[:].rearrange("p x h -> p (x h)"), root,
                   ALU.mult).then_inc(kscale_ready, 1)
                nc.vector.tensor_copy(v_scale[:].rearrange("p x h -> p (x h)"), root).then_inc(kscale_ready, 1)
                dve.wait_ge(kscale_ready, 2 * (s + 1))
                for x in two:
                    k = k_nat[c % 2][x][:]
                    dve.wait_ge(k_squared, 2 * s + x + 1)
                    tt(k, k, per_head(k_scale, x), ALU.mult).then_inc(k_scaled, 1)

            def scores(s, c, x):
                dve.wait_ge(p_mm, 2 * s + x + 1)
                if not (isinstance(s, int) and s == 0):
                    dve.wait_ge(o_mm, 2 * (s - 1) + x + 1)
                tt(pT[x][:], ps_vp[:], all_heads(upper_diag, P), ALU.mult).then_inc(p_done, 1)

            def split_turned(r, x):
                n = 2 * r + x
                dve.wait_ge(o_hi_done, n + 1)
                if not (isinstance(r, int) and n == 0):
                    dve.wait_ge(out_mm, n)
                nc.vector.scalar_tensor_tensor(o_lo[:], ps_s[0][:], rms_sb[:], o_hi[:].bitcast(F32),
                                               ALU.mult, ALU.subtract).then_inc(turn_done, 1)

            def residual(r, c, x):
                n = 2 * r + x
                dve.wait_ge(ks_mm, n + 1)
                if not (isinstance(r, int) and n == 0):
                    dve.wait_ge(upd_mm, n)
                dve.wait_ge(v_done, n + 1)
                tt(resid[:], v_nat[x][:], ps_s[0][:], ALU.subtract).then_inc(resid_done, 1)

            def new_state(r, c, x):
                n = 2 * r + x
                dve.wait_ge(state_mm, n + 1)
                if c == SPG - 1 and x == 1:
                    dve.wait_ge(o_mm, n)
                    nc.vector.memset(state[0][:], 0.0).then_inc(state_done, 1)
                    return
                if not (isinstance(r, int) and n == 0):
                    dve.wait_ge(o_mm, n)
                dve.wait_ge(state_done, n + 1)
                tt(state[1 - x][:], state[x][:], ps_s[0][:], ALU.add).then_inc(state_done, 1)

            def sum_o(r, c, x):
                n = 2 * r + x
                dve.wait_ge(osq_done, n + 1)
                nc.vector.reduce_sum(o_sum[x][:], o_work[:], AX_X).then_inc(osum_steps, 1)
                dve.wait_ge(osum_steps, 2 * n + 1)
                dve.wait_ge(qsum_read, r + 1)
                if not (isinstance(r, int) and r == 0):
                    dve.wait_ge(ofac_done, n - 1)
                nc.vector.scalar_tensor_tensor(o_var[x][:], o_sum[x][:], 1.0 / HD, q_term[c][:, x, :],
                                               ALU.mult, ALU.add).then_inc(osum_steps, 1)

            for j in range(2):
                split_w(0, j)

            def slot(s, c, A, INV, SCAN):
                for hop in range(HOPS):
                    r, rc = s - 1, (c - 1) % 4
                    if INV and hop == 1:
                        for x in two:
                            mask_pairs(s, x)
                        for x in two:
                            base(s, x)
                    if INV and (hop in (RESIDUAL, RESIDUAL + 1) or 2 <= hop <= 9):
                        for x in two:
                            inverse(s, c, x, hop)
                    if SCAN and hop == 0:
                        residual(r, rc, 0)
                    if INV and hop in (0, 6):
                        values(s, c, hop // 6)
                    if INV and hop == 7:
                        dve.wait_ge(qsum_mm, 2 * s + 2)
                        nc.vector.tensor_scalar(q_term[c][:], ps_sum[:], L2_EPS, HD * RMS_EPS,
                                                ALU.add, ALU.mult).then_inc(qsum_read, 1)
                    if SCAN and hop == 4:
                        new_state(r, rc, 0)
                    if INV and hop in (5, 9):
                        scores(s, c, hop // 9)
                    if SCAN and hop in (10, 14):
                        split_turned(r, hop // 14)
                    if SCAN and hop == 5:
                        residual(r, rc, 1)
                    if SCAN and hop == 6:
                        sum_o(r, rc, 0)
                    if SCAN and hop == 8:
                        new_state(r, rc, 1)
                    if SCAN and hop == 11:
                        sum_o(r, rc, 1)
                    if A and hop in (13, 14):
                        sum_k(s + 1, hop - 13)
                    if A and hop == 16:
                        scale_k(s + 1, (c + 1) % 4)
                    for step, sc, j, half in due((CONV_A, CONV_B), hop, s, c, A, INV):
                        convolve(step, sc, j, half)
                    if A and c in SPLIT_LO and hop in SPLIT_LO[c] and \
                            not (isinstance(s, int) and s >= STEPS - 2):
                        split_w((s - c) // SPG + (1 if c >= 2 else 0), SPLIT_LO[c][hop])

            run_slots(slot, dve)


def phase_feed_forward(nc, ctx, x, wf, xT, part, out):
    TB = 512
    NJ = DH // P
    NT = TB // P
    NB = B * S // TB
    TILES_AHEAD, BLOCK_AHEAD, SUMS_AHEAD = 2, 2 * NT, 3
    with ExitStack() as own:
        sb = lambda name, shape, dt=F32: own.enter_context(nc.sbuf_tensor(name, shape, dt))
        sem = lambda name: ctx.enter_context(nc.semaphore(name))
        bank = lambda name, shape: own.enter_context(nc.psum_tensor(name, shape, F32))
        two = range(2)
        wf_sb = sb("wf_sb", [P, NJ, 3 * DM])
        gu_hi = [sb(f"f_guhi{u}", [P, 2 * DM], F32R) for u in two]
        gu_lo = [sb(f"f_gulo{u}", [P, 2 * DM], F32R) for u in two]
        dn_hi = [sb(f"f_dnhi{u}", [P, DM], F32R) for u in two]
        dn_lo = [sb(f"f_dnlo{u}", [P, DM], F32R) for u in two]
        xb = [sb(f"f_x{u}", [P, 2, 2, KT, BLK], F32R) for u in two]
        act_g = [sb(f"f_g{u}", [P, TB]) for u in two]
        hid = [sb(f"f_hid{u}", [P, TB]) for u in two]
        h_hi = [sb(f"f_hhi{u}", [P, TB], F32R) for u in two]
        h_lo = [sb(f"f_hlo{u}", [P, TB], F32R) for u in two]
        parts = sb("f_part", [P, NG, DM])
        x_res = [sb(f"f_xres{t}", [P, DM]) for t in range(NT)]
        gate = [sb(f"f_gate{t}", [P, DM]) for t in range(NT)]
        total = [sb(f"f_total{t}", [P, DM]) for t in range(NT)]
        ps_g = [bank(f"f_psg{u}", [P, TB]) for u in two]
        ps_u = [bank(f"f_psu{u}", [P, TB]) for u in two]
        ps_o = [bank(f"f_pso{t}", [P, DM]) for t in range(NT)]
        wf_loaded = [sem(f"f_wf_loaded{j}") for j in range(NJ)]
        x_loaded = [sem(f"f_x_loaded{u}") for u in two]
        part_loaded = sem("f_part_loaded")
        res_loaded = [sem(f"f_res_loaded{t}") for t in range(NT)]
        gu_hi_done, gu_lo_done, dn_hi_done, dn_lo_done = (sem(n) for n in (
            "f_gu_hi_done", "f_gu_lo_done", "f_dn_hi_done", "f_dn_lo_done"))
        g_mm, u_mm, g_done, hid_done, hhi_done, hlo_done, down_mm = (sem(n) for n in (
            "f_g_mm", "f_u_mm", "f_g_done", "f_hid_done", "f_hhi_done", "f_hlo_done", "f_down_mm"))
        gate_done, sums, res_done = sem("f_gate_done"), sem("f_sums"), sem("f_res_done")
        out_stored = [sem(f"f_out_stored{t}") for t in range(NT)]
        block = own.enter_context(nc.Block())

        @block.sync
        def _(sp):
            for t in range(NT):
                sp.sem_inc(out_stored[t], DMA_AHEAD)

            def load_x(b, u):
                for i in range(2):
                    sp.dma_start(xb[u][:, i].bitcast(F32), xT[2 * b + i]).then_inc(x_loaded[u], 16)

            sp.dma_start(wf_sb[:, 0], wf[:, 0]).then_inc(wf_loaded[0], 16)
            load_x(0, 0)
            for j in range(1, NJ):
                sp.dma_start(wf_sb[:, j], wf[:, j]).then_inc(wf_loaded[j], 16)
            load_x(1, 1)
            with sp.Fori(0, NB // 2) as p:
                for u in two:
                    b = 2 * p + u
                    for t in range(NT):
                        m = NT * b + t
                        sp.wait_ge(sums, SUMS_AHEAD + 3 * m)
                        sp.dma_start(parts[:], part.rearrange("(g q) p d -> q p g d", g=NG)[m])\
                            .then_inc(part_loaded, 16)
                        sp.wait_ge(out_stored[t], DMA_AHEAD + 16 * b)
                        sp.dma_start(x_res[t][:], x[m]).then_inc(res_loaded[t], 16)
                    sp.wait_ge(u_mm, TILES_AHEAD + NJ * (b + 1))
                    load_x((b + 2) % NB, u)
                    for t in range(NT):
                        m = NT * b + t
                        sp.wait_ge(res_done, BLOCK_AHEAD + 2 * m + 2)
                        sp.dma_start(out[m], total[t][:]).then_inc(out_stored[t], 16)
            for t in range(NT):
                sp.wait_ge(out_stored[t], DMA_AHEAD + 16 * NB)
            for u in two:
                sp.wait_ge(x_loaded[u], 32 * (NB // 2 + 1))

        @block.tensor
        def _(pe):
            pe.sem_inc(down_mm, TILES_AHEAD)
            pe.sem_inc(u_mm, TILES_AHEAD)

            def gate_up(p, jj):
                u, n, x_u = jj % 2, 2 * NJ * p + jj, jj // NJ
                if jj % NJ == 0:
                    pe.wait_ge(x_loaded[x_u], 32 * (p + 1))
                pe.wait_ge(gu_lo_done, n + 1)
                pe.wait_ge(hid_done, TILES_AHEAD + n - 1)
                for i, ps in enumerate((ps_g[u], ps_u[u])):
                    for k in range(KT):
                        for r in range(3):
                            w = (gu_hi, gu_hi, gu_lo)[r][u]
                            last = nc.tensor.matmul(
                                ps[:].rearrange("p (b t) -> p b t", b=2),
                                w[:, i * DM + k * P:i * DM + (k + 1) * P],
                                xb[x_u][:, :, (0, 1, 0)[r], k, :],
                                start=(k == 0 and r == 0), stop=(k == KT - 1 and r == 2))
                    last.then_inc(u_mm if i else g_mm, 1)

            def down(p, jj):
                u, j, n = jj % 2, jj % NJ, 2 * NJ * p + jj
                pe.wait_ge(dn_lo_done, n + 1)
                pe.wait_ge(hlo_done, n + 1)
                if j == 0:
                    pe.wait_ge(gate_done, AHEAD + NT * (2 * p + jj // NJ))
                for t in range(NT):
                    for r in range(3):
                        h = (h_hi, h_hi, h_lo)[r][u]
                        w = (dn_hi, dn_lo, dn_hi)[r][u]
                        last = nc.tensor.matmul(ps_o[t][:], h[:, t * P:(t + 1) * P], w[:],
                                                start=(j == 0 and r == 0), stop=(j == NJ - 1 and r == 2))
                last.then_inc(down_mm, 1)

            with pe.Fori(0, NB // 2) as p:
                gate_up(p, 0)
                for jj in range(2 * NJ):
                    if jj + 1 < 2 * NJ:
                        gate_up(p, jj + 1)
                    down(p, jj)

        @block.scalar
        def _(act):
            act.sem_inc(gate_done, AHEAD)

            def split_gate_up(n, j):
                act.wait_ge(u_mm, TILES_AHEAD + n - 1)
                nc.scalar.activation(gu_hi[j % 2][:], wf_sb[:, j, 0:2 * DM], ACT.Copy).then_inc(gu_hi_done, 1)

            def split_down(n, j):
                act.wait_ge(down_mm, TILES_AHEAD + n - 1)
                nc.scalar.activation(dn_hi[j % 2][:], wf_sb[:, j, 2 * DM:], ACT.Copy).then_inc(dn_hi_done, 1)

            act.wait_ge(wf_loaded[0], 16)
            split_gate_up(0, 0)
            split_down(0, 0)
            act.wait_ge(wf_loaded[1], 16)
            split_gate_up(1, 1)
            with act.Fori(0, NB // 2) as p:
                for jj in range(2 * NJ):
                    u, j, n = jj % 2, jj % NJ, 2 * NJ * p + jj
                    act.wait_ge(g_mm, n + 1)
                    act.wait_ge(hid_done, TILES_AHEAD + n - 1)
                    nc.scalar.activation(act_g[u][:], ps_g[u][:], ACT.Silu).then_inc(g_done, 1)
                    if jj + 2 < NJ:
                        act.wait_ge(wf_loaded[j + 2], 16)
                    split_gate_up(n + 2, (j + 2) % NJ)
                    act.wait_ge(hid_done, TILES_AHEAD + n + 1)
                    act.wait_ge(down_mm, TILES_AHEAD + n - 1)
                    nc.scalar.activation(h_hi[u][:], hid[u][:], ACT.Copy).then_inc(hhi_done, 1)
                    split_down(n + 1, (j + 1) % NJ)
                    if j == NJ - 1:
                        act.wait_ge(down_mm, TILES_AHEAD + n + 1)
                        for t in range(NT):
                            m = NT * (2 * p + jj // NJ) + t
                            act.wait_ge(res_done, BLOCK_AHEAD + 2 * (m - NT) + 1)
                            nc.scalar.activation(gate[t][:], ps_o[t][:], ACT.Silu).then_inc(gate_done, 1)

        @block.vector
        def _(dve):
            dve.sem_inc(hid_done, TILES_AHEAD)
            dve.sem_inc(res_done, BLOCK_AHEAD)
            tt = nc.vector.tensor_tensor

            def low_gate_up(n, j):
                dve.wait_ge(gu_hi_done, n + 1)
                tt(gu_lo[j % 2][:], wf_sb[:, j, 0:2 * DM], gu_hi[j % 2][:].bitcast(F32), ALU.subtract)\
                    .then_inc(gu_lo_done, 1)

            def low_down(n, j):
                dve.wait_ge(dn_hi_done, n + 1)
                tt(dn_lo[j % 2][:], wf_sb[:, j, 2 * DM:], dn_hi[j % 2][:].bitcast(F32), ALU.subtract)\
                    .then_inc(dn_lo_done, 1)

            def result(b, t):
                m = NT * b + t
                dve.wait_ge(gate_done, AHEAD + m + 1)
                dve.wait_ge(sums, SUMS_AHEAD + 3 * m + 3)
                tt(total[t][:], total[t][:], gate[t][:], ALU.mult).then_inc(res_done, 1)
                dve.wait_ge(res_done, BLOCK_AHEAD + 2 * m + 1)
                dve.wait_ge(res_loaded[t], 16 * (b + 1))
                tt(total[t][:], total[t][:], x_res[t][:], ALU.add).then_inc(res_done, 1)

            low_gate_up(0, 0)
            low_down(0, 0)
            low_gate_up(1, 1)
            with dve.Fori(0, NB // 2) as p:
                for jj in range(2 * NJ):
                    u, j, n = jj % 2, jj % NJ, 2 * NJ * p + jj
                    dve.wait_ge(g_done, n + 1)
                    dve.wait_ge(u_mm, TILES_AHEAD + n + 1)
                    tt(hid[u][:], act_g[u][:], ps_u[u][:], ALU.mult).then_inc(hid_done, 1)
                    dve.wait_ge(hhi_done, n + 1)
                    tt(h_lo[u][:], hid[u][:], h_hi[u][:].bitcast(F32), ALU.subtract).then_inc(hlo_done, 1)
                    low_gate_up(n + 2, (j + 2) % NJ)
                    low_down(n + 1, (j + 1) % NJ)
                    if NJ <= jj < NJ + NT:
                        result(2 * p, jj - NJ)
                for t in range(NT):
                    result(2 * p + 1, t)

        @block.gpsimd
        def _(pool):
            pool.sem_inc(sums, SUMS_AHEAD)
            tt = nc.gpsimd.tensor_tensor
            with pool.Fori(0, NB) as b:
                for t in range(NT):
                    m = NT * b + t
                    pool.wait_ge(part_loaded, 16 * (m + 1))
                    pool.wait_ge(out_stored[t], DMA_AHEAD + 16 * b)
                    tt(total[t][:], parts[:, 0], parts[:, 1], ALU.add).then_inc(sums, 1)
                    for g in (2, 3):
                        pool.wait_ge(sums, SUMS_AHEAD + 3 * m + g - 1)
                        tt(total[t][:], total[t][:], parts[:, g], ALU.add).then_inc(sums, 1)


def build(nc, x, wqkv, wb, wo, rms, wf, out):
    with ExitStack() as ctx:
        sb = lambda name, shape: ctx.enter_context(nc.sbuf_tensor(name, shape, F32))
        xT = nc.dram_tensor("xT", (NBLK, P, 2, KT, BLK), F32, kind="Internal").ap()
        part = nc.dram_tensor("part", (2 * STEPS, P, DM), F32, kind="Internal").ap()
        ident = sb("ident", [P, P])
        upper = sb("upper", [P, P])
        upper_diag = sb("upper_diag", [P, P])
        below1 = sb("below1", [P, P // 2])
        above1 = sb("above1", [P, P // 2])
        level_masks = {m: sb(f"mask{m}", [P, P // 2]) for m in LEVELS if m < 32}
        sqrt_beta = sb("sqrt_beta", [P, NG, 2 * NBLK * HG])
        const = {"masks": (ident, upper, upper_diag, below1, above1, level_masks), "ident": ident,
                 "masks_n": 2 + len(level_masks) + 3 + 5 + 2 * len(level_masks)}
        phase_normalise(nc, ctx, x, wb, xT, const, sqrt_beta)
        phase_attention(nc, ctx, wqkv, wo, rms, xT, part, const, sqrt_beta)
        phase_feed_forward(nc, ctx, x, wf, xT, part, out)


def kernel(L0_attn_x, L0_attn_Wq, L0_attn_Wk, L0_attn_Wv, L0_attn_Wb, L0_attn_Wo, L0_attn_conv_q,
           L0_attn_conv_k, L0_attn_conv_v, L0_attn_rms_w, L0_ffn_w_gate, L0_ffn_w_up, L0_ffn_w_down):
    import numpy as np
    import concourse.bacc as bacc
    from concourse.bass_utils import run_bass_kernel_spmd as run

    def a(v):
        return np.asarray(v)

    xs = a(L0_attn_x).reshape(B * S // P, P, DM)
    tiles = []
    for w, cw in ((L0_attn_Wk, L0_attn_conv_k), (L0_attn_Wv, L0_attn_conv_v), (L0_attn_Wq, L0_attn_conv_q)):
        wt = a(w).reshape(NG, 2, 2, P, KT, P).transpose(0, 1, 5, 2, 4, 3).reshape(NG, 2, P, 2, KT * P)
        ct = a(cw).reshape(NG, 2, 2, P, KW).transpose(0, 1, 3, 2, 4)
        tiles.append(np.concatenate([wt, ct], axis=-1))
    wqkv = np.ascontiguousarray(np.stack(tiles, axis=1).reshape(NG, PAIRS, P, 2, KT * P + KW))
    wb = np.ascontiguousarray(a(L0_attn_Wb).reshape(NH, KT, P).transpose(2, 1, 0).reshape(P, KT * NH))
    wo = np.ascontiguousarray(a(L0_attn_Wo).reshape(DM, NG, HG, P).transpose(1, 3, 2, 0))
    rms = np.ascontiguousarray(a(L0_attn_rms_w).reshape(P, 1))
    nj = DH // P
    gu = [a(w).reshape(nj, P, KT, P).transpose(3, 0, 2, 1).reshape(P, nj, DM)
          for w in (L0_ffn_w_gate, L0_ffn_w_up)]
    down = a(L0_ffn_w_down).reshape(DM, nj, P).transpose(2, 1, 0)
    wf = np.ascontiguousarray(np.concatenate([*gu, down], axis=-1))

    nc = bacc.Bacc("TRN2", target_bir_lowering=False, num_devices=1)
    arrays, aps = {}, []
    for name, v in (("x", xs), ("wqkv", wqkv), ("wb", wb), ("wo", wo), ("rms", rms), ("wf", wf)):
        arrays[name] = v
        aps.append(nc.dram_tensor(name, v.shape, mybir.dt.from_np(v.dtype), kind="ExternalInput").ap())
    out = nc.dram_tensor("out", (B * S // P, P, DM), F32, kind="ExternalOutput").ap()
    build(nc, *aps, out)
    r = run(nc, [arrays], core_ids=[0])
    return r.results[0]["out"].reshape(B, S, DM)
```
